# Optimizing a Trainium2 kernel written in Bass

```python
import numpy as np
import jax
import jax.numpy as jnp

def _softmax(x, axis=-1):
    return jax.nn.softmax(x, axis=axis)
def _gelu(x):
    return jax.nn.gelu(x, approximate=True)
def _silu(x):
    return jax.nn.silu(x)
def _sigmoid(x):
    return jax.nn.sigmoid(x)
def _layernorm(x, axis=-1, eps=1e-5):
    m = jnp.mean(x, axis=axis, keepdims=True)
    v = jnp.var(x, axis=axis, keepdims=True)
    return (x - m) / jnp.sqrt(v + eps)
def _scatter_add(tgt, idx, src, axis=0):
    return tgt.at[idx].add(src)
def _segment_sum(src, seg, n):
    return jax.ops.segment_sum(src, seg, n)

kernel_name = 'mk_metaformer_d1_conv_nchw1024_d4a4d3'

def setup_inputs(seed: int = 0):
    np.random.seed(seed)
    _w = jnp.asarray
    def _rec_inputs():
        import jax
        import jax.numpy as jnp
        _gk = jax.random.key(seed)
        x = -0.0002928 + 1 * jax.random.normal(jax.random.fold_in(_gk, 1), (1, 1024, 64, 64), jnp.float32)
        return x
    x = _rec_inputs()
    def _L0_conv_setup():
        import jax, jax.numpy as jnp
        import numpy as np
        EPS = 1e-05

        def _layernorm2d(x, w, b):
            mean = jnp.mean(x, axis=(-2, -1), keepdims=True)
            var = jnp.mean(jnp.square(x - mean), axis=(-2, -1), keepdims=True)
            return (x - mean) / jnp.sqrt(var + EPS) * w + b
        key = jax.random.key(seed)
        ks = jax.random.split(key, 6)
        b, seq, d = (1, 1024, 64)
        x = jax.random.normal(ks[0], (b, seq, d, d), dtype=jnp.float32)
        log_A = jax.random.normal(ks[1], (d,), dtype=jnp.float32) * 0.02
        dt_w = jax.random.normal(ks[2], (1, d), dtype=jnp.float32) / np.sqrt(d)
        dt_b = jax.random.normal(ks[3], (1,), dtype=jnp.float32) * 0.01
        ln_w = jnp.ones((d, d), dtype=jnp.float32)
        ln_b = jnp.zeros((d, d), dtype=jnp.float32)
        return {'x': x, 'log_A': log_A, 'dt_w': dt_w, 'dt_b': dt_b, 'ln_w': ln_w, 'ln_b': ln_b}
    _L0_conv_all = _L0_conv_setup()
    _L0_conv_in = {k: v for k, v in _L0_conv_all.items() if k in ('log_A', 'dt_w', 'dt_b', 'ln_w', 'ln_b', )}
    del _L0_conv_all

    def _L0_ffn_setup():
        import jax, jax.numpy as jnp
        import numpy as np
        from jax import lax
        B, L = (4, 512)
        D_MODEL, D_STATE, D_CONV, EXPAND = (1024, 16, 4, 2)
        D_INNER = EXPAND * D_MODEL
        DT_RANK = (D_MODEL + 15) // 16

        def _selective_scan(u, delta, A, Bm, Cm, Dv):

            def step(h, inp):
                u_t, dt_t, B_t, C_t = inp
                dA = jnp.exp(dt_t[:, :, None] * A)
                h = dA * h + (dt_t * u_t)[:, :, None] * B_t[:, None, :]
                y = jnp.einsum('bdn,bn->bd', h, C_t)
                return (h, y)
            b, l, d = u.shape
            h0 = jnp.zeros((b, d, A.shape[1]), u.dtype)
            xs = (u.transpose(1, 0, 2), delta.transpose(1, 0, 2), Bm.transpose(1, 0, 2), Cm.transpose(1, 0, 2))
            _, ys = lax.scan(step, h0, xs)
            return ys.transpose(1, 0, 2) + u * Dv

        def _direction(x_bdl, conv_w, conv_b, xproj_w, dtproj_w, dtproj_b, A_log, Dv):
            xc = lax.conv_general_dilated(x_bdl, conv_w, (1,), [(D_CONV - 1, 0)], dimension_numbers=('NCH', 'OIH', 'NCH'), feature_group_count=D_INNER)
            xc = (xc + conv_b[None, :, None]).transpose(0, 2, 1)
            x_dbl = xc @ xproj_w.T
            dt = x_dbl[..., :DT_RANK] @ dtproj_w.T + dtproj_b
            Bm = x_dbl[..., DT_RANK:DT_RANK + D_STATE]
            Cm = x_dbl[..., DT_RANK + D_STATE:]
            xc = jnp.clip(xc, -10.0, 10.0)
            dt = jnp.clip(dt, 1e-05, 1.0)
            delta = jax.nn.softplus(dt + dtproj_b)
            A = -jnp.exp(A_log)
            return _selective_scan(xc, delta, A, Bm, Cm, Dv)
        key = jax.random.key(seed)
        ks = jax.random.split(key, 16)

        def rn(k, shape, scale=1.0):
            return jax.random.normal(k, shape, jnp.float32) * scale
        A_log = jnp.log(jnp.broadcast_to(jnp.arange(1, D_STATE + 1, dtype=jnp.float32), (D_INNER, D_STATE)))
        return {'hidden_states': rn(ks[0], (B, L, D_MODEL)), 'in_proj_w': rn(ks[1], (2 * D_INNER, D_MODEL), D_MODEL ** (-0.5)), 'conv1d_w': rn(ks[2], (D_INNER, 1, D_CONV), D_CONV ** (-0.5)), 'conv1d_bias': rn(ks[3], (D_INNER,), 0.02), 'x_proj_w': rn(ks[4], (DT_RANK + 2 * D_STATE, D_INNER), D_INNER ** (-0.5)), 'dt_proj_w': rn(ks[5], (D_INNER, DT_RANK), DT_RANK ** (-0.5)), 'dt_proj_bias': rn(ks[6], (D_INNER,), 0.02) - 4.0, 'A_log': A_log, 'D': jnp.ones((D_INNER,), jnp.float32), 'conv1d_b_w': rn(ks[7], (D_INNER, 1, D_CONV), D_CONV ** (-0.5)), 'conv1d_b_bias': rn(ks[8], (D_INNER,), 0.02), 'x_proj_b_w': rn(ks[9], (DT_RANK + 2 * D_STATE, D_INNER), D_INNER ** (-0.5)), 'dt_proj_b_w': rn(ks[10], (D_INNER, DT_RANK), DT_RANK ** (-0.5)), 'dt_proj_b_bias': rn(ks[11], (D_INNER,), 0.02) - 4.0, 'A_b_log': A_log, 'D_b': jnp.ones((D_INNER,), jnp.float32), 'out_proj_w': rn(ks[12], (D_MODEL, D_INNER), D_INNER ** (-0.5))}
    _L0_ffn_all = _L0_ffn_setup()
    _L0_ffn_in = {k: v for k, v in _L0_ffn_all.items() if k in ('in_proj_w', 'conv1d_w', 'conv1d_bias', 'x_proj_w', 'dt_proj_w', 'dt_proj_bias', 'A_log', 'D', 'conv1d_b_w', 'conv1d_b_bias', 'x_proj_b_w', 'dt_proj_b_w', 'dt_proj_b_bias', 'A_b_log', 'D_b', 'out_proj_w', )}
    del _L0_ffn_all

    return {
        "x": x,
        "L0_conv_log_A": _L0_conv_in["log_A"],
        "L0_conv_dt_w": _L0_conv_in["dt_w"],
        "L0_conv_dt_b": _L0_conv_in["dt_b"],
        "L0_conv_ln_w": _L0_conv_in["ln_w"],
        "L0_conv_ln_b": _L0_conv_in["ln_b"],
        "L0_ffn_in_proj_w": _L0_ffn_in["in_proj_w"],
        "L0_ffn_conv1d_w": _L0_ffn_in["conv1d_w"],
        "L0_ffn_conv1d_bias": _L0_ffn_in["conv1d_bias"],
        "L0_ffn_x_proj_w": _L0_ffn_in["x_proj_w"],
        "L0_ffn_dt_proj_w": _L0_ffn_in["dt_proj_w"],
        "L0_ffn_dt_proj_bias": _L0_ffn_in["dt_proj_bias"],
        "L0_ffn_A_log": _L0_ffn_in["A_log"],
        "L0_ffn_D": _L0_ffn_in["D"],
        "L0_ffn_conv1d_b_w": _L0_ffn_in["conv1d_b_w"],
        "L0_ffn_conv1d_b_bias": _L0_ffn_in["conv1d_b_bias"],
        "L0_ffn_x_proj_b_w": _L0_ffn_in["x_proj_b_w"],
        "L0_ffn_dt_proj_b_w": _L0_ffn_in["dt_proj_b_w"],
        "L0_ffn_dt_proj_b_bias": _L0_ffn_in["dt_proj_b_bias"],
        "L0_ffn_A_b_log": _L0_ffn_in["A_b_log"],
        "L0_ffn_D_b": _L0_ffn_in["D_b"],
        "L0_ffn_out_proj_w": _L0_ffn_in["out_proj_w"],
    }

def reference(x, L0_conv_log_A, L0_conv_dt_w, L0_conv_dt_b, L0_conv_ln_w, L0_conv_ln_b, L0_ffn_in_proj_w, L0_ffn_conv1d_w, L0_ffn_conv1d_bias, L0_ffn_x_proj_w, L0_ffn_dt_proj_w, L0_ffn_dt_proj_bias, L0_ffn_A_log, L0_ffn_D, L0_ffn_conv1d_b_w, L0_ffn_conv1d_b_bias, L0_ffn_x_proj_b_w, L0_ffn_dt_proj_b_w, L0_ffn_dt_proj_b_bias, L0_ffn_A_b_log, L0_ffn_D_b, L0_ffn_out_proj_w):
    import jax
    import jax.numpy as jnp
    def _L0_conv_ref(x, log_A, dt_w, dt_b, ln_w, ln_b):
        import jax, jax.numpy as jnp
        import numpy as np
        EPS = 1e-05

        def _layernorm2d(x, w, b):
            mean = jnp.mean(x, axis=(-2, -1), keepdims=True)
            var = jnp.mean(jnp.square(x - mean), axis=(-2, -1), keepdims=True)
            return (x - mean) / jnp.sqrt(var + EPS) * w + b
        x_norm = _layernorm2d(x, ln_w, ln_b)
        b, seq, d, _ = x_norm.shape
        A_cont = -jnp.exp(log_A)
        dt = jax.nn.softplus(jnp.einsum('bsdc,c->bsd', x_norm, dt_w[0]) + dt_b[0])
        log_a = dt * A_cont
        cums = jnp.cumsum(log_a, axis=1)
        log_M = cums[:, :, None, :] - cums[:, None, :, :]
        idx = jnp.arange(seq)
        mask = idx[:, None] >= idx[None, :]
        log_M = jnp.where(mask[None, :, :, None], log_M, -jnp.inf)
        M = jnp.exp(log_M)
        out = jnp.einsum('btjr,bjrc->btrc', M, x_norm)
        return out

    def _L0_ffn_ref(hidden_states, in_proj_w, conv1d_w, conv1d_bias, x_proj_w, dt_proj_w, dt_proj_bias, A_log, D, conv1d_b_w, conv1d_b_bias, x_proj_b_w, dt_proj_b_w, dt_proj_b_bias, A_b_log, D_b, out_proj_w):
        import jax, jax.numpy as jnp
        import numpy as np
        from jax import lax
        B, L = (4, 512)
        D_MODEL, D_STATE, D_CONV, EXPAND = (1024, 16, 4, 2)
        D_INNER = EXPAND * D_MODEL
        DT_RANK = (D_MODEL + 15) // 16

        def _selective_scan(u, delta, A, Bm, Cm, Dv):

            def step(h, inp):
                u_t, dt_t, B_t, C_t = inp
                dA = jnp.exp(dt_t[:, :, None] * A)
                h = dA * h + (dt_t * u_t)[:, :, None] * B_t[:, None, :]
                y = jnp.einsum('bdn,bn->bd', h, C_t)
                return (h, y)
            b, l, d = u.shape
            h0 = jnp.zeros((b, d, A.shape[1]), u.dtype)
            xs = (u.transpose(1, 0, 2), delta.transpose(1, 0, 2), Bm.transpose(1, 0, 2), Cm.transpose(1, 0, 2))
            _, ys = lax.scan(step, h0, xs)
            return ys.transpose(1, 0, 2) + u * Dv

        def _direction(x_bdl, conv_w, conv_b, xproj_w, dtproj_w, dtproj_b, A_log, Dv):
            xc = lax.conv_general_dilated(x_bdl, conv_w, (1,), [(D_CONV - 1, 0)], dimension_numbers=('NCH', 'OIH', 'NCH'), feature_group_count=D_INNER)
            xc = (xc + conv_b[None, :, None]).transpose(0, 2, 1)
            x_dbl = xc @ xproj_w.T
            dt = x_dbl[..., :DT_RANK] @ dtproj_w.T + dtproj_b
            Bm = x_dbl[..., DT_RANK:DT_RANK + D_STATE]
            Cm = x_dbl[..., DT_RANK + D_STATE:]
            xc = jnp.clip(xc, -10.0, 10.0)
            dt = jnp.clip(dt, 1e-05, 1.0)
            delta = jax.nn.softplus(dt + dtproj_b)
            A = -jnp.exp(A_log)
            return _selective_scan(xc, delta, A, Bm, Cm, Dv)
        xz = (hidden_states @ in_proj_w.T).transpose(0, 2, 1)
        x, z = jnp.split(xz, 2, axis=1)
        y_fwd = _direction(x, conv1d_w, conv1d_bias, x_proj_w, dt_proj_w, dt_proj_bias, A_log, D)
        y_bwd = _direction(x[:, :, ::-1], conv1d_b_w, conv1d_b_bias, x_proj_b_w, dt_proj_b_w, dt_proj_b_bias, A_b_log, D_b)[:, ::-1, :]
        y = (y_fwd + y_bwd) * jax.nn.silu(z.transpose(0, 2, 1))
        out = y @ out_proj_w.T
        return jnp.nan_to_num(out, nan=0.0, posinf=1.0, neginf=-1.0)

    def _gn(v, G=32, eps=1e-5):
        B_, C_, H_, W_ = v.shape
        g = v.reshape(B_, G, C_ // G, H_, W_)
        m = jnp.mean(g, axis=(2, 3, 4), keepdims=True)
        s = jnp.var(g, axis=(2, 3, 4), keepdims=True)
        return ((g - m) / jnp.sqrt(s + eps)).reshape(v.shape)

    def _ln_c(v, eps=1e-6):
        m = jnp.mean(v, axis=1, keepdims=True)
        s = jnp.var(v, axis=1, keepdims=True)
        return (v - m) / jnp.sqrt(s + eps)

    def _ln_t(v, eps=1e-5):
        m = jnp.mean(v, axis=-1, keepdims=True)
        s = jnp.var(v, axis=-1, keepdims=True)
        return (v - m) / jnp.sqrt(s + eps)

    def _to_tokens(v):
        B_, C_, H_, W_ = v.shape
        return v.reshape(B_, C_, H_ * W_).transpose(0, 2, 1)
    def _from_tokens(t, like):
        B_, C_, H_, W_ = like.shape
        return t.transpose(0, 2, 1).reshape(B_, C_, H_, W_)

    x = x + _L0_conv_ref(_ln_c(x), L0_conv_log_A, L0_conv_dt_w, L0_conv_dt_b, L0_conv_ln_w, L0_conv_ln_b)
    t = _to_tokens(x)
    t = t + _L0_ffn_ref(_ln_t(t), L0_ffn_in_proj_w, L0_ffn_conv1d_w, L0_ffn_conv1d_bias, L0_ffn_x_proj_w, L0_ffn_dt_proj_w, L0_ffn_dt_proj_bias, L0_ffn_A_log, L0_ffn_D, L0_ffn_conv1d_b_w, L0_ffn_conv1d_b_bias, L0_ffn_x_proj_b_w, L0_ffn_dt_proj_b_w, L0_ffn_dt_proj_b_bias, L0_ffn_A_b_log, L0_ffn_D_b, L0_ffn_out_proj_w)
    x = _from_tokens(t, x)
    return x


_drawn_inputs = setup_inputs


def setup_inputs(seed=0):
    import zlib

    import numpy as np

    out = dict(_drawn_inputs(seed))
    spreads = {'L0_conv_ln_w': (1.0, 0.2),
     'L0_conv_ln_b': (0.0, 0.1),
     'L0_ffn_D': (1.0, 0.2),
     'L0_ffn_D_b': (1.0, 0.2)}
    factors = {'L0_conv_log_A': 8.0,
     'L0_ffn_conv1d_bias': 8.0,
     'L0_ffn_dt_proj_w': 64.0,
     'L0_ffn_dt_proj_bias': 64.0,
     'L0_ffn_conv1d_b_bias': 8.0,
     'L0_ffn_dt_proj_b_w': 64.0,
     'L0_ffn_dt_proj_b_bias': 64.0,
     'L0_ffn_x_proj_w': 64.0,
     'L0_ffn_x_proj_b_w': 64.0}
    for name, (base, spread) in spreads.items():
        noise = np.random.default_rng([zlib.crc32(name.encode()), seed]).standard_normal(out[name].shape)
        drawn = base * np.exp(spread * noise) if base else spread * noise
        out[name] = jnp.asarray(drawn.astype(out[name].dtype))
    for name, factor in factors.items():
        out[name] = (out[name] * factor).astype(out[name].dtype)
    return out
```

```python
from contextlib import ExitStack

import concourse.bass as bass
from concourse import mybir

F32 = mybir.dt.float32
ALU = mybir.AluOpType
ACT = mybir.ActivationFunctionType

P = 128
C = 1024
HW = 4096
ROW = 64
NT = HW // P
KT = C // P
DI = 2048
DB = DI // P
NS = 16
R = 64
XO = R + 2 * NS
T = 512
NCH = HW // T
TB = T // P
TAPS = 4
HALO = TAPS - 1
G = 4
NG = NS // G
NOUT = 8
EPS_C, EPS_HW, EPS_T = 1e-6, 1e-5, 1e-5
FMAX = 3.4028234663852886e38
LOAD = 16


def ds(start, n):
    return bass.ds(start, n)


def hold(eng, sem, value, passed):
    eng.wait_ge(sem, value)
    eng.sem_inc(passed, 1)


class Scope:

    def __init__(self, nc, stage):
        self.nc, self.stage, self.stack = nc, stage, ExitStack()

    def __enter__(self):
        self.stack.__enter__()
        return self

    def __exit__(self, *a):
        return self.stack.__exit__(*a)

    def sb(self, name, shape):
        return self.stack.enter_context(self.nc.sbuf_tensor(f"{self.stage}_{name}", shape, F32))

    def ps(self, name, shape):
        return self.stack.enter_context(self.nc.psum_tensor(f"{self.stage}_{name}", shape, F32))

    def sem(self, name):
        return self.stack.enter_context(self.nc.semaphore(f"{self.stage}_{name}"))

    def block(self):
        return self.stack.enter_context(self.nc.Block())


def stage_channel_norm(nc, xn, ident, mean_w, mean_ps, x_d):
    with Scope(nc, "n1") as sc:
        xin = sc.sb("xin", [P, 2, KT, P])
        zero = sc.sb("zero", [P, 512])
        stats = sc.sb("stats", [P, 2, 2, 6])
        mv = sc.sb("mv", [P, 2, 2])
        std = sc.sb("std", [P, 2])
        rstd = sc.sb("rstd", [P, 2])
        xt = sc.ps("xt", [P, 2, C])
        const_ready, x_loaded = sc.sem("const_ready"), [sc.sem("x_loaded0"), sc.sem("x_loaded1")]
        transposed, var_ready, std_ready = sc.sem("transposed"), sc.sem("var_ready"), sc.sem("std_ready")
        passed = sc.sem("passed")
        chain, normalised, summed = sc.sem("chain"), sc.sem("normalised"), sc.sem("summed")
        x_v = x_d.rearrange("(k p) t -> p k t", p=P)
        block = sc.block()

        @block.gpsimd
        def _(pool):
            nc.gpsimd.memset(ident[:], 0.0).then_inc(const_ready, 1)
            pool.wait_ge(const_ready, 1)
            nc.gpsimd.affine_select(out=ident[:], in_=ident[:], compare_op=ALU.not_equal, fill=1.0, base=0,
                                    pattern=[[-1, P]], channel_multiplier=1).then_inc(const_ready, 1)
            nc.gpsimd.memset(mean_w[:], 1.0 / HW).then_inc(const_ready, 1)
            nc.gpsimd.memset(zero[:], 0.0).then_inc(const_ready, 1)

        @block.sync
        def _(sp):
            for s in range(2):
                sp.dma_start(xin[:, s], x_v[:, :, s * P:(s + 1) * P]).then_inc(x_loaded[s], LOAD)
            with sp.Fori(0, NT // 2 - 1) as j:
                for s in range(2):
                    sp.wait_ge(transposed, j * 2 + s + 1)
                    sp.dma_start(xin[:, s], x_v[:, :, ds(j * (2 * P) + (2 + s) * P, P)]).then_inc(x_loaded[s], LOAD)

        @block.tensor
        def _(pe):
            pe.wait_ge(const_ready, 4)
            for h in range(2):
                nc.tensor.matmul(mean_ps[:, h * 512:(h + 1) * 512], zero[:, 0:P], zero[:], start=True, stop=False)
            with pe.Fori(0, NT // 2) as j:
                for s in range(2):
                    pe.wait_ge(x_loaded[s], (j + 1) * LOAD)
                    pe.wait_ge(normalised, j * 2 + s + 1)
                    for k in range(KT):
                        last = nc.tensor.matmul(xt[:, s, k * P:(k + 1) * P], xin[:, s, k], ident[:], is_transpose=True,
                                                start=(k % 4 == 0), stop=(k % 4 == 3))
                    last.then_inc(transposed, 1)
                for s in range(2):
                    pe.wait_ge(normalised, j * 2 + s + 3)
                    for h in range(2):
                        last = nc.tensor.matmul(mean_ps[:, h * 512:(h + 1) * 512], mean_w[:],
                                                xn[:, ds(j * (2 * C) + s * C + h * 512, 512)], start=False, stop=False)
                    last.then_inc(summed, 1)
            for h in range(2):
                nc.tensor.matmul(mean_ps[:, h * 512:(h + 1) * 512], zero[:, 0:P], zero[:], start=False, stop=True)

        @block.vector
        def _(dve):
            dve.sem_inc(normalised, 2)
            with dve.Fori(0, NT // 2) as j:
                for s in range(2):
                    dve.wait_ge(transposed, j * 2 + s + 1)
                    for h in range(2):
                        last = nc.vector.bn_stats(stats[:, s, h], xt[:, s, h * 512:(h + 1) * 512])
                    last.then_inc(chain, 1)
                for s in range(2):
                    hold(dve, chain, j * 6 + 1 + s, passed)
                    nc.vector.bn_aggr(mv[:, s], stats[:, s].rearrange("p a b -> p (a b)")).then_inc(chain, 1)
                    dve.wait_ge(chain, j * 6 + 3 + s)
                    nc.vector.tensor_scalar(mv[:, s, 1:2], mv[:, s, 1:2], EPS_C, None, ALU.add).then_inc(var_ready, 1)
                for s in range(2):
                    dve.wait_ge(std_ready, j * 2 + s + 1)
                    nc.vector.reciprocal(rstd[:, s:s + 1], std[:, s:s + 1]).then_inc(chain, 1)
                for s in range(2):
                    dve.wait_ge(chain, j * 6 + 5 + s)
                    nc.vector.tensor_scalar(xn[:, ds(j * (2 * C) + s * C, C)], xt[:, s], mv[:, s, 0:1],
                                            rstd[:, s:s + 1], ALU.subtract, ALU.mult).then_inc(normalised, 1)

        @block.scalar
        def _(act):
            with act.Fori(0, NT // 2) as j:
                for s in range(2):
                    act.wait_ge(var_ready, j * 2 + s + 1)
                    nc.scalar.activation(std[:, s:s + 1], mv[:, s, 1:2], ACT.Sqrt).then_inc(std_ready, 1)


def stage_pixel_variance(nc, xn, mean_w, mean_ps, rstd2):
    with Scope(nc, "n2") as sc:
        sq = sc.sb("sq", [P, 2, C])
        zero = sc.sb("zero", [P, 512])
        var_ps = sc.ps("var_ps", [P, C])
        zero_ready, centred, squared = sc.sem("zero_ready"), sc.sem("centred"), sc.sem("squared")
        summed, var_done, chain = sc.sem("summed"), sc.sem("var_done"), sc.sem("chain")
        block = sc.block()

        @block.gpsimd
        def _(pool):
            nc.gpsimd.memset(zero[:], 0.0).then_inc(zero_ready, 1)

        @block.vector
        def _(dve):
            with dve.Fori(0, NT) as t:
                nc.vector.tensor_tensor(xn[:, ds(t * C, C)], xn[:, ds(t * C, C)], mean_ps[:],
                                        ALU.subtract).then_inc(centred, 1)
            dve.wait_ge(var_done, 1)
            nc.vector.tensor_scalar(rstd2[:], var_ps[:], EPS_HW, None, ALU.add).then_inc(chain, 1)
            dve.wait_ge(chain, 2)
            nc.vector.reciprocal(rstd2[:], rstd2[:]).then_inc(chain, 1)

        @block.scalar
        def _(act):
            with act.Fori(0, NT // 2) as j:
                for s in range(2):
                    act.wait_ge(zero_ready, 1)
                    act.wait_ge(summed, j * 2 + s + 1)
                    act.wait_ge(centred, j * 2 + s + 1)
                    nc.scalar.activation(sq[:, s], xn[:, ds(j * (2 * C) + s * C, C)], ACT.Square).then_inc(squared, 1)
            act.wait_ge(chain, 1)
            nc.scalar.activation(rstd2[:], rstd2[:], ACT.Sqrt).then_inc(chain, 1)

        @block.tensor
        def _(pe):
            pe.sem_inc(summed, 2)
            pe.wait_ge(zero_ready, 1)
            for h in range(2):
                nc.tensor.matmul(var_ps[:, h * 512:(h + 1) * 512], zero[:, 0:P], zero[:], start=True, stop=False)
            with pe.Fori(0, NT // 2) as j:
                for s in range(2):
                    pe.wait_ge(squared, j * 2 + s + 1)
                    for h in range(2):
                        last = nc.tensor.matmul(var_ps[:, h * 512:(h + 1) * 512], mean_w[:],
                                                sq[:, s, h * 512:(h + 1) * 512], start=False, stop=False)
                    last.then_inc(summed, 1)
            for h in range(2):
                last = nc.tensor.matmul(var_ps[:, h * 512:(h + 1) * 512], zero[:, 0:P], zero[:], start=False, stop=True)
            last.then_inc(var_done, 1)


def stage_channel_scan(nc, xn, ident, rstd2, mv, x_d, lnw_d, lnb_d, dtw_d, dtb_d, loga_d):
    with Scope(nc, "n3") as sc:
        lnw, lnb, aneg = sc.sb("lnw", [P, NT]), sc.sb("lnb", [P, NT]), sc.sb("aneg", [P, NT])
        dtw, dtb, row_w = sc.sb("dtw", [P, 1]), sc.sb("dtb", [P, 1]), sc.sb("row_w", [P, P])
        xin = sc.sb("xin", [P, 2, KT, P])
        mag = sc.sb("mag", [P, C])
        sp_ = sc.sb("softplus", [P, 2, C])
        decay = sc.sb("decay", [P, C])
        scanned = sc.sb("scanned", [P, C])
        stats, mv_t = sc.sb("stats", [P, 2, 6]), sc.sb("mv_t", [P, 2])
        dt_ps = sc.ps("dt_ps", [P, 2, C])
        xt = sc.ps("xt", [P, 2, C])
        par_loaded, x_loaded = sc.sem("par_loaded"), [sc.sem("x_loaded0"), sc.sem("x_loaded1")]
        scaled, normed, dt_done = sc.sem("scaled"), sc.sem("normed"), sc.sem("dt_done")
        ab_done, log_done, relu_done = sc.sem("ab_done"), sc.sem("log_done"), sc.sem("relu_done")
        sp_done, decay_done, scan_done = sc.sem("sp_done"), sc.sem("decay_done"), sc.sem("scan_done")
        transposed, added, chain = sc.sem("transposed"), sc.sem("added"), sc.sem("chain")
        achain, setup, passed = sc.sem("achain"), sc.sem("setup"), sc.sem("passed")
        x_v = x_d.rearrange("(k p) t -> p k t", p=P)
        block = sc.block()

        @block.sync
        def _(sp):
            for dst, src in ((lnw, lnw_d), (lnb, lnb_d), (aneg, loga_d), (dtw, dtw_d), (dtb, dtb_d)):
                sp.dma_start(dst[:], src).then_inc(par_loaded, LOAD)
            for s in range(2):
                sp.dma_start(xin[:, s], x_v[:, :, s * P:(s + 1) * P]).then_inc(x_loaded[s], LOAD)
            with sp.Fori(0, NT // 2 - 1) as j:
                for s in range(2):
                    sp.wait_ge(transposed, j * 2 + s + 1)
                    sp.dma_start(xin[:, s], x_v[:, :, ds(j * (2 * P) + (2 + s) * P, P)]).then_inc(x_loaded[s], LOAD)

        @block.gpsimd
        def _(pool):
            with pool.Fori(0, NT) as t:
                nc.gpsimd.tensor_tensor(xn[:, ds(t * C, C)], xn[:, ds(t * C, C)], rstd2[:],
                                        ALU.mult).then_inc(scaled, 1)

        @block.vector
        def _(dve):
            nc.vector.memset(row_w[:], 0.0).then_inc(setup, 1)
            dve.wait_ge(setup, 1)
            for r in range(2):
                nc.vector.memset(row_w[r * ROW:(r + 1) * ROW, r * ROW:(r + 1) * ROW], 1.0).then_inc(setup, 1)
            dve.wait_ge(par_loaded, 5 * LOAD)
            dve.wait_ge(setup, 3)
            nc.vector.tensor_scalar(row_w[:], row_w[:], dtw[:], None, ALU.mult).then_inc(setup, 1)
            dve.sem_inc(added, 2)

            def affine(j, s):
                dve.wait_ge(scaled, j * 2 + s + 1)
                nc.vector.tensor_scalar(xn[:, ds(j * (2 * C) + s * C, C)], xn[:, ds(j * (2 * C) + s * C, C)],
                                        lnw[:, ds(j * 2 + s, 1)], lnb[:, ds(j * 2 + s, 1)],
                                        ALU.mult, ALU.add).then_inc(normed, 1)

            with dve.Fori(0, NT // 2) as j:
                for s in range(2):
                    affine(j, s)
                for s in range(2):
                    dve.wait_ge(dt_done, j * 2 + s + 1)
                    dve.wait_ge(decay_done, j * 2 + s + 1)
                    nc.vector.tensor_scalar(sp_[:, s], dt_ps[:, s], dtb[:], 0.0, ALU.add,
                                            ALU.max).then_inc(relu_done, 1)
                    dve.wait_ge(log_done, j * 2 + s + 1)
                    dve.wait_ge(relu_done, j * 2 + s + 1)
                    nc.vector.tensor_tensor(sp_[:, s], sp_[:, s], mag[:], ALU.add).then_inc(sp_done, 1)
                for s in range(2):
                    dve.wait_ge(decay_done, j * 2 + s + 3)
                    dve.wait_ge(added, j * 2 + s + 2)
                    nc.vector.tensor_tensor_scan(scanned[:], decay[:], xn[:, ds(j * (2 * C) + s * C, C)], 0.0,
                                                 ALU.mult, ALU.add).then_inc(scan_done, 1)
                    dve.wait_ge(scan_done, j * 2 + s + 2)
                    dve.wait_ge(transposed, j * 2 + s + 1)
                    nc.vector.tensor_tensor(xn[:, ds(j * (2 * C) + s * C, C)], scanned[:], xt[:, s],
                                            ALU.add).then_inc(added, 1)
                    hold(dve, added, j * 2 + s + 3, passed)
                    for h in range(2):
                        last = nc.vector.bn_stats(stats[:, h], xn[:, ds(j * (2 * C) + s * C + h * 512, 512)])
                    last.then_inc(chain, 1)
                    hold(dve, chain, j * 6 + s * 3 + 1, passed)
                    nc.vector.bn_aggr(mv_t[:], stats[:].rearrange("p a b -> p (a b)")).then_inc(chain, 1)
                    dve.wait_ge(chain, j * 6 + s * 3 + 2)
                    nc.vector.tensor_copy(mv[:, ds(j * 4 + s * 2, 2)], mv_t[:]).then_inc(chain, 1)

        @block.scalar
        def _(act):
            act.wait_ge(par_loaded, 5 * LOAD)
            nc.scalar.activation(aneg[:], aneg[:], ACT.Exp).then_inc(achain, 1)
            act.wait_ge(achain, 1)
            nc.scalar.mul(aneg[:], aneg[:], -1.0).then_inc(achain, 1)
            act.wait_ge(achain, 2)
            act.sem_inc(decay_done, 2)
            act.sem_inc(scan_done, 1)
            with act.Fori(0, NT // 2) as j:
                for s in range(2):
                    act.wait_ge(relu_done, j * 2 + s + 1)
                    act.wait_ge(sp_done, j * 2 + s + 2)
                    nc.scalar.activation(mag[:], dt_ps[:, s], ACT.Abs, bias=dtb[:]).then_inc(ab_done, 1)
                    act.wait_ge(ab_done, j * 4 + s * 2 + 1)
                    nc.scalar.activation(mag[:], mag[:], ACT.Exp, scale=-1.0).then_inc(ab_done, 1)
                    act.wait_ge(ab_done, j * 4 + s * 2 + 2)
                    nc.scalar.activation(mag[:], mag[:], ACT.Ln, bias=1.0).then_inc(log_done, 1)
                for s in range(2):
                    act.wait_ge(par_loaded, 5 * LOAD)
                    act.wait_ge(sp_done, j * 2 + s + 3)
                    act.wait_ge(scan_done, j * 2 + s + 1)
                    nc.scalar.activation(decay[:], sp_[:, s], ACT.Exp,
                                         scale=aneg[:, ds(j * 2 + s, 1)]).then_inc(decay_done, 1)

        @block.tensor
        def _(pe):
            pe.sem_inc(sp_done, 2)
            pe.wait_ge(setup, 4)
            with pe.Fori(0, NT // 2) as j:
                for s in range(2):
                    pe.wait_ge(normed, j * 2 + s + 1)
                    pe.wait_ge(sp_done, j * 2 + s + 1)
                    for h in range(2):
                        last = nc.tensor.matmul(dt_ps[:, s, h * 512:(h + 1) * 512], row_w[:],
                                                xn[:, ds(j * (2 * C) + s * C + h * 512, 512)], start=True, stop=True)
                    last.then_inc(dt_done, 1)
                for s in range(2):
                    pe.wait_ge(x_loaded[s], (j + 1) * LOAD)
                    pe.wait_ge(added, j * 2 + s + 1)
                    for k in range(KT):
                        last = nc.tensor.matmul(xt[:, s, k * P:(k + 1) * P], xin[:, s, k], ident[:], is_transpose=True,
                                                start=(k % 4 == 0), stop=(k % 4 == 3))
                    last.then_inc(transposed, 1)


def stage_token_norm(nc, xn, ident, mv, hnT_d, x1T_d, x_pad_d, state_ds):
    with Scope(nc, "n4") as sc:
        rstd, nmr = sc.sb("rstd", [P, NT]), sc.sb("nmr", [P, NT])
        hn, xs = sc.sb("hn", [P, 2, C]), sc.sb("xs", [P, 2, C])
        hn_out, x_out = sc.sb("hn_out", [P, 2, C]), sc.sb("x_out", [P, 2, C])
        zero = sc.sb("zero", [P, DB * NS])
        hn_ps, x_ps = sc.ps("hn_ps", [P, 2, C]), sc.ps("x_ps", [P, 2, C])
        zero_ready, zero_stored = sc.sem("zero_ready"), sc.sem("zero_stored")
        chain, stats_ready = sc.sem("chain"), sc.sem("stats_ready")
        normed, hn_t, x_t, x_moved = sc.sem("normed"), sc.sem("hn_t"), sc.sem("x_t"), sc.sem("x_moved")
        hn_copied, x_copied = sc.sem("hn_copied"), sc.sem("x_copied")
        hn_stored = [sc.sem("hn_stored0"), sc.sem("hn_stored1")]
        x_stored = [sc.sem("x_stored0"), sc.sem("x_stored1")]
        mv3 = mv[:].rearrange("p (t c) -> p t c", c=2)
        hn_v = hnT_d.rearrange("(k p) t -> p k t", p=P)
        x1_v = x1T_d.rearrange("(k p) t -> p k t", p=P)
        block = sc.block()

        @block.gpsimd
        def _(pool):
            nc.gpsimd.memset(zero[:], 0.0).then_inc(zero_ready, 1)
            with pool.Fori(0, NT // 2) as j:
                for s in range(2):
                    pool.wait_ge(x_t, j * 2 + s + 1)
                    nc.gpsimd.tensor_copy(xs[:, s], xn[:, ds(j * (2 * C) + s * C, C)]).then_inc(x_moved, 1)

        @block.vector
        def _(dve):
            dve.sem_inc(x_copied, 2)
            nc.vector.tensor_scalar(rstd[:], mv3[:, :, 1], EPS_T, None, ALU.add).then_inc(chain, 1)
            dve.wait_ge(chain, 2)
            nc.vector.reciprocal(rstd[:], rstd[:]).then_inc(chain, 1)
            dve.wait_ge(chain, 3)
            nc.vector.scalar_tensor_tensor(nmr[:], mv3[:, :, 0], -1.0, rstd[:], ALU.mult,
                                           ALU.mult).then_inc(stats_ready, 1)
            with dve.Fori(0, NT // 2) as j:
                for s in range(2):
                    dve.wait_ge(x_t, j * 2 + s + 3)
                    dve.wait_ge(x_stored[s], (j + 1) * LOAD)
                    nc.vector.tensor_copy(x_out[:, s], x_ps[:, s]).then_inc(x_copied, 1)

        @block.scalar
        def _(act):
            act.sem_inc(hn_copied, 2)
            act.wait_ge(chain, 1)
            nc.scalar.activation(rstd[:], rstd[:], ACT.Sqrt).then_inc(chain, 1)
            with act.Fori(0, NT // 2) as j:
                for s in range(2):
                    act.wait_ge(stats_ready, 1)
                    act.wait_ge(hn_t, j * 2 + s + 1)
                    nc.scalar.activation(hn[:, s], xn[:, ds(j * (2 * C) + s * C, C)], ACT.Identity,
                                         bias=nmr[:, ds(j * 2 + s, 1)],
                                         scale=rstd[:, ds(j * 2 + s, 1)]).then_inc(normed, 1)
                for s in range(2):
                    act.wait_ge(hn_t, j * 2 + s + 3)
                    act.wait_ge(hn_stored[s], (j + 1) * LOAD)
                    nc.scalar.activation(hn_out[:, s], hn_ps[:, s], ACT.Copy).then_inc(hn_copied, 1)

        @block.tensor
        def _(pe):
            pe.sem_inc(hn_t, 2)
            pe.sem_inc(x_t, 2)
            with pe.Fori(0, NT // 2) as j:
                for s in range(2):
                    pe.wait_ge(x_moved, j * 2 + s + 1)
                    pe.wait_ge(x_copied, j * 2 + s + 1)
                    for k in range(KT):
                        last = nc.tensor.matmul(x_ps[:, s, k * P:(k + 1) * P], xs[:, s, k * P:(k + 1) * P], ident[:],
                                                is_transpose=True, start=(k % 4 == 0), stop=(k % 4 == 3))
                    last.then_inc(x_t, 1)
                    pe.wait_ge(normed, j * 2 + s + 1)
                    pe.wait_ge(hn_copied, j * 2 + s + 1)
                    for k in range(KT):
                        last = nc.tensor.matmul(hn_ps[:, s, k * P:(k + 1) * P], hn[:, s, k * P:(k + 1) * P], ident[:],
                                                is_transpose=True, start=(k % 4 == 0), stop=(k % 4 == 3))
                    last.then_inc(hn_t, 1)

        @block.sync
        def _(sp):
            for s in range(2):
                sp.sem_inc(hn_stored[s], LOAD)
                sp.sem_inc(x_stored[s], LOAD)
            sp.wait_ge(zero_ready, 1)
            for side in (0, HALO + HW):
                sp.dma_start(x_pad_d[:, side:side + HALO].rearrange("(b p) t -> p b t", p=P),
                             zero[:, 0:DB * HALO].rearrange("p (b t) -> p b t", t=HALO)).then_inc(zero_stored, LOAD)
            for state_d in state_ds:
                sp.dma_start(state_d[0:DB].rearrange("u p n -> p u n"),
                             zero[:].rearrange("p (u n) -> p u n", n=NS)).then_inc(zero_stored, LOAD)
            with sp.Fori(0, NT // 2) as j:
                for s in range(2):
                    sp.wait_ge(x_copied, j * 2 + s + 3)
                    sp.dma_start(x1_v[:, :, ds(j * (2 * P) + s * P, P)],
                                 x_out[:, s].rearrange("p (k t) -> p k t", t=P)).then_inc(x_stored[s], LOAD)
                    sp.wait_ge(hn_copied, j * 2 + s + 3)
                    sp.dma_start(hn_v[:, :, ds(j * (2 * P) + s * P, P)],
                                 hn_out[:, s].rearrange("p (k t) -> p k t", t=P)).then_inc(hn_stored[s], LOAD)
            sp.wait_ge(zero_stored, 4 * LOAD)
            for s in range(2):
                sp.wait_ge(x_stored[s], (NT // 2 + 1) * LOAD)
                sp.wait_ge(hn_stored[s], (NT // 2 + 1) * LOAD)


def stage_scan(nc, rev, ident, hnT_d, winx_d, winz_d, wx_d, wdt_d, convp_d, parb_d,
               x_pad_d, xc_d, z_d, bc_d, state_d, yT_d):
    name = "bwd" if rev else "fwd"
    first = rev
    with Scope(nc, name) as sc:
        hn = sc.sb("hn", [P, KT, T]) if first else None
        winx = sc.sb("winx", [P, 2, KT, P]) if first else None
        winz = sc.sb("winz", [P, 2, KT, P]) if first else None
        wx = sc.sb("wx", [P, 2, XO])
        convp = sc.sb("convp", [P, 2, TAPS + 1])
        x = sc.sb("x", [P, 2, T + HALO])
        xc_out = sc.sb("xc_out", [P, 2, T])
        z_out = sc.sb("z_out", [P, 2, T])
        zero = sc.sb("zero", [P, T])
        proj = sc.sb("proj", [XO, T])
        bcast_b, bcast_c = sc.sb("bcast_b", [P, NS, T]), sc.sb("bcast_c", [P, NS, T])
        par = sc.sb("par", [P, 2, 2 + NS])
        wdt = sc.sb("wdt", [R, 2, P])
        xc = sc.sb("xc", [P, 2, T])
        state_in, state_out = sc.sb("state_in", [P, 2, NS]), sc.sb("state_out", [P, 2, NS])
        aneg = sc.sb("aneg", [P, 2, NS])
        v = sc.sb("v", [P, T])
        mag = sc.sb("mag", [P, T])
        delta, u, du, ud = (sc.sb(n, [P, 2, T]) for n in ("delta", "u", "du", "ud"))
        w = sc.sb("w", [P, 2, G, T])
        hc = sc.sb("hc", [P, NOUT, T])
        y_out = sc.sb("y_out", [P, 2, TB, P])
        da = sc.ps("da", [P, 2, T])
        h = sc.ps("h", [P, 3, T])
        yT = sc.ps("yT", [P, TB, P])
        proj_ps = sc.ps("proj_ps", [P, T])
        misc = sc.ps("misc", [P, T])

        names = ("setup", "hn_loaded", "x_mm", "z_mm", "x_copied", "z_copied", "conv_step", "conv_done", "proj_mm",
                 "proj_closed", "proj_copied", "tap0_done", "bc_stored", "dt_mm", "dt_read", "v_done", "abs_exp", "ln_done", "aneg_step",
                 "pre_step", "du_done", "ud_done", "exp_done", "w_done", "scan_done", "hc_done", "h_saved",
                 "h_saved_dve", "hc_used", "yT_done", "yT_copied", "stored", "passed")
        S = {n: sc.sem(n) for n in names}
        b_loaded, c_loaded = [sc.sem(f"b_loaded{g}") for g in range(NG)], [sc.sem(f"c_loaded{g}") for g in range(NG)]
        a_in, b_in = [sc.sem(f"a_in{s}") for s in range(2)], [sc.sem(f"b_in{s}") for s in range(2)]
        NA = 5 if first else 3
        NB = 4

        def t0(k):
            return (NCH - 1) * T - k * T if rev else k * T

        def col(k):
            return t0(k) + HALO

        def flip(ap):
            return ap[:, ::-1] if rev else ap

        last_col = 0 if rev else T - 1
        x_at = 0 if rev else HALO
        tap_at = [HALO - k if rev else k for k in range(TAPS)]

        def chunks(eng, pair, boundary, prologue):
            prologue()
            with eng.Fori(0, DB // 2) as j:
                pair(eng, j, j, a=True, b=False)
            with eng.Fori(0, NCH - 1) as k:
                boundary(k, True)
                with eng.Fori(0, DB // 2 - 1) as j:
                    pair(eng, k * (DB // 2) + j, j, a=True, b=True, k=k)
                pair(eng, k * (DB // 2) + DB // 2 - 1, DB // 2 - 1, a=True, b=True, k=k, end=True)
            boundary(NCH - 1, False)
            with eng.Fori(0, DB // 2 - 1) as j:
                pair(eng, (NCH - 1) * (DB // 2) + j, j, a=False, b=True, k=NCH - 1)
            pair(eng, NCH * (DB // 2) - 1, DB // 2 - 1, a=False, b=True, k=NCH - 1, end=True)

        def a_pair(m, b):
            return m + DB // 2 if b else m

        stores = {(True, False): (3 if first else 1), (True, True): (5 if first else 3), (False, True): 2}
        base = {(True, False): 0, (True, True): DB * stores[True, False],
                (False, True): DB * stores[True, False] + DB * (NCH - 1) * stores[True, True]}
        all_stores = base[False, True] + DB * stores[False, True]

        block = sc.block()

        @block.sync
        def _(sp):
            def load_a(s, db, k):
                if first:
                    sp.dma_start(winx[:, s], winx_d[ds(db, 1)].rearrange("o p k d -> (o p) k d")).then_inc(a_in[s], LOAD)
                    sp.dma_start(winz[:, s], winz_d[ds(db, 1)].rearrange("o p k d -> (o p) k d")).then_inc(a_in[s], LOAD)
                    halo = x[:, s, T:T + HALO]
                    sp.dma_start(halo, x_pad_d[ds(db * P, P), ds(col(k) + T, HALO)]).then_inc(a_in[s], LOAD)
                else:
                    sp.dma_start(x[:, s], x_pad_d[ds(db * P, P), ds(t0(k), T + HALO)]).then_inc(a_in[s], LOAD)
                sp.dma_start(wx[:, s], wx_d[ds(db, 1)].rearrange("o p k -> (o p) k")).then_inc(a_in[s], LOAD)
                sp.dma_start(convp[:, s], convp_d[ds(db, 1)].rearrange("o p k -> (o p) k")).then_inc(a_in[s], LOAD)

            def load_b(s, u_, db):
                sp.dma_start(par[:, s], parb_d[ds(db, 1)].rearrange("o p k -> (o p) k")).then_inc(b_in[s], LOAD)
                sp.dma_start(wdt[:, s], wdt_d[ds(db, 1)].rearrange("o p k -> (o p) k")).then_inc(b_in[s], LOAD)
                sp.dma_start(xc[:, s], xc_d[ds(u_, 1)].rearrange("o p k -> (o p) k")).then_inc(b_in[s], LOAD)
                sp.dma_start(state_in[:, s], state_d[ds(u_, 1)].rearrange("o p k -> (o p) k")).then_inc(b_in[s], LOAD)

            def pair(eng, m, j, a, b, k=None, end=False):
                n = stores[a, b]
                ma = a_pair(m, b)
                ka = 0 if not b else k + 1
                start = base[a, b] + (m * (2 * n) if b and a or not b else (m - (NCH - 1) * (DB // 2)) * (2 * n))
                for s in range(2):
                    db = j * 2 + s
                    if b:
                        hold(sp, S["yT_copied"], m * 2 + s + 1, S["passed"])
                        sp.dma_start(yT_d[ds(m * 2 + s, 1)].rearrange("o p t d -> (o p) t d"),
                                     y_out[:, 1 - s]).then_inc(S["stored"], LOAD)
                    if a:
                        u_a = ma * 2 + s
                        if first:
                            hold(sp, S["x_copied"], ma * 2 + s + 2, S["passed"])
                            sp.dma_start(x_pad_d[ds(db * P, P), ds(col(ka), T)],
                                         x[:, s, x_at:x_at + T]).then_inc(S["stored"], LOAD)
                        hold(sp, S["conv_done"], ma * 2 + s + 1, S["passed"])
                        sp.dma_start(xc_d[ds(u_a, 1)].rearrange("o p k -> (o p) k"),
                                     xc_out[:, s]).then_inc(S["stored"], LOAD)
                        if first:
                            hold(sp, S["z_copied"], ma * 2 + s + 2, S["passed"])
                            sp.dma_start(z_d[ds(db * P, P), ds(t0(ka), T)],
                                         z_out[:, s]).then_inc(S["stored"], LOAD)
                    if b:
                        hold(sp, S["h_saved"], m * 26 + s * 13 + 14, S["passed"])
                        hold(sp, S["h_saved_dve"], m * 6 + s * 3 + 6, S["passed"])
                        sp.dma_start(state_d[ds(m * 2 + s + DB, 1)].rearrange("o p k -> (o p) k"),
                                     state_out[:, s]).then_inc(S["stored"], LOAD)
                    hold(sp, S["stored"], start * LOAD + (s + 1) * n * LOAD, S["passed"])
                    if a:
                        hold(sp, S["proj_mm"], ma * 2 + s + 1, S["passed"])
                        if first:
                            hold(sp, S["z_mm"], ma * 2 + s + 1, S["passed"])
                    if b:
                        hold(sp, S["exp_done"], m * 32 + (s + 1) * 16, S["passed"])
                        hold(sp, S["ud_done"], m * 2 + s + 1, S["passed"])
                    if not end:
                        if a and b:
                            load_a(s, db + 2, ka)
                        if b:
                            load_b(s, m * 2 + s + 2, db + 2)

            def boundary(k, more):
                if more:
                    for s in range(2):
                        load_a(s, s, k + 1)
                for s in range(2):
                    load_b(s, k * DB + s, s)
                if more and first:
                    hold(sp, S["z_mm"], k * DB + DB, S["passed"])
                    sp.dma_start(hn[:], hnT_d.rearrange("(k p) t -> p k t", p=P)[:, :, ds(t0(k + 1), T)]
                                 ).then_inc(S["hn_loaded"], LOAD)
                hold(sp, S["proj_copied"], k + 1, S["passed"])
                sp.dma_start(bc_d[ds(k, 1)].rearrange("o n t -> (o n) t"), proj[R:XO, :]).then_inc(S["bc_stored"], LOAD)
                hold(sp, S["bc_stored"], k * LOAD + LOAD, S["passed"])
                hold(sp, S["w_done"], k * (DB * NG) + 1, S["passed"])
                for g in range(NG):
                    src = bc_d[ds(k, 1)][:, g * G:(g + 1) * G].rearrange("o n t -> (o n) t")
                    sp.dma_start(bcast_b[:, g * G:(g + 1) * G], src.partition_broadcast(P)).then_inc(b_loaded[g], LOAD)
                hold(sp, S["hc_done"], k * (DB * NS) + 3, S["passed"])
                for g in range(NG):
                    src = bc_d[ds(k, 1)][:, NS + g * G:NS + (g + 1) * G].rearrange("o n t -> (o n) t")
                    sp.dma_start(bcast_c[:, g * G:(g + 1) * G], src.partition_broadcast(P)).then_inc(c_loaded[g], LOAD)

            def prologue():
                if first:
                    sp.dma_start(hn[:], hnT_d.rearrange("(k p) t -> p k t", p=P)[:, :, t0(0):t0(0) + T]
                                 ).then_inc(S["hn_loaded"], LOAD)
                for s in range(2):
                    load_a(s, s, 0)
                with sp.Fori(0, DB // 2 - 1) as j:
                    pair(sp, j, j, a=True, b=False)
                    for s in range(2):
                        load_a(s, j * 2 + s + 2, 0)
                pair(sp, DB // 2 - 1, DB // 2 - 1, a=True, b=False)

            prologue()
            with sp.Fori(0, NCH - 1) as k:
                boundary(k, True)
                with sp.Fori(0, DB // 2 - 1) as j:
                    pair(sp, k * (DB // 2) + j, j, a=True, b=True, k=k)
                pair(sp, k * (DB // 2) + DB // 2 - 1, DB // 2 - 1, a=True, b=True, k=k, end=True)
            boundary(NCH - 1, False)
            with sp.Fori(0, DB // 2 - 1) as j:
                pair(sp, (NCH - 1) * (DB // 2) + j, j, a=False, b=True, k=NCH - 1)
            pair(sp, NCH * (DB // 2) - 1, DB // 2 - 1, a=False, b=True, k=NCH - 1, end=True)
            hold(sp, S["yT_copied"], NCH * DB + 1, S["passed"])
            sp.dma_start(yT_d[NCH * DB], y_out[:, 1]).then_inc(S["stored"], LOAD)
            hold(sp, S["stored"], all_stores * LOAD + LOAD, S["passed"])

        @block.tensor
        def _(pe):
            def dt_matmul(s, loads, free, need):
                pe.wait_ge(b_in[s], loads)
                pe.wait_ge(S[free], need)
                nc.tensor.matmul(misc[:], wdt[:, s], proj[0:R, :], start=True, stop=True).then_inc(S["dt_mm"], 1)

            def pair(eng, m, j, a, b, k=None, end=False):
                ma = a_pair(m, b)
                for s in range(2):
                    nxt = b and not (end and s == 1)
                    m_next = (m + s) * (NB * LOAD) + NB * LOAD

                    def x_part(i0, i1):
                        if i0 == 0:
                            pe.wait_ge(a_in[s], (ma + 1) * (NA * LOAD))
                            if s == 0:
                                pe.wait_ge(S["hn_loaded"], ((k + 2) if b else 1) * LOAD)
                            pe.wait_ge(S["z_copied"], ma * 2 + s + 1)
                            if b:
                                pe.wait_ge(S["dt_read"], m * 2 + s + 1)
                        for i in range(i0, i1):
                            last = nc.tensor.matmul(misc[:], winx[:, s, i], hn[:, i], start=(i == 0), stop=(i == KT - 1))
                        if i1 == KT:
                            last.then_inc(S["x_mm"], 1)

                    def z_part(i0, i1):
                        if i0 == 0:
                            if nxt:
                                pe.wait_ge(S["dt_read"], m * 2 + s + 2)
                            else:
                                pe.wait_ge(S["x_copied"], ma * 2 + s + 2)
                        for i in range(i0, i1):
                            last = nc.tensor.matmul(misc[:], winz[:, s, i], hn[:, i], start=(i == 0), stop=(i == KT - 1))
                        if i1 == KT:
                            last.then_inc(S["z_mm"], 1)

                    def projection():
                        if not first:
                            pe.wait_ge(a_in[s], (ma + 1) * (NA * LOAD))
                        pe.wait_ge(S["conv_done"], ma * 2 + s + 1)
                        nc.tensor.matmul(proj_ps[0:XO, :], wx[:, s], xc_out[:, s], start=False,
                                         stop=False).then_inc(S["proj_mm"], 1)

                    if not b:
                        if first:
                            x_part(0, KT)
                            z_part(0, KT)
                        projection()
                        continue
                    for n in range(NS):
                        if first and a and 1 <= n <= 4:
                            x_part(2 * (n - 1), 2 * n)
                        if n == 7 and nxt:
                            if first and a:
                                dt_matmul(1 - s, m_next, "x_copied", ma * 2 + s + 2)
                            else:
                                dt_matmul(1 - s, m_next, "dt_read", m * 2 + s + (1 if first else 2))
                        if first and a and 10 <= n <= 13:
                            z_part(2 * (n - 10), 2 * (n - 9))
                        if a and n == 14:
                            projection()
                        pe.wait_ge(S["hc_done"], m * 32 + s * 16 + n + 4)
                        if n == 0:
                            pe.wait_ge(S["yT_copied"], m * 2 + s + 1)
                        for tb in range(TB):
                            last = nc.tensor.matmul(yT[:, tb], hc[:, (s * 16 + n) % NOUT, tb * P:(tb + 1) * P], ident[:],
                                                    is_transpose=True, start=(n == 0 and tb == 0), stop=False)
                        last.then_inc(S["hc_used"], 1)
                    pe.wait_ge(S["ud_done"], m * 2 + s + 1)
                    for tb in range(TB):
                        last = nc.tensor.matmul(yT[:, tb], ud[:, s, tb * P:(tb + 1) * P], ident[:], is_transpose=True,
                                                start=False, stop=(tb == TB - 1))
                    last.then_inc(S["yT_done"], 1)

            def boundary(k, more):
                nc.tensor.matmul(proj_ps[0:XO, :], zero[:, 0:XO], zero[:], start=False, stop=True).then_inc(S["proj_closed"], 1)
                pe.wait_ge(S["proj_copied"], k + 1)
                if first:
                    pe.wait_ge(S["z_copied"], k * DB + DB + 1)
                else:
                    pe.wait_ge(S["dt_read"], k * DB + 1)
                pe.wait_ge(b_in[0], k * (DB // 2 * NB * LOAD) + NB * LOAD)
                nc.tensor.matmul(misc[:], wdt[:, 0], proj[0:R, :], start=True, stop=True).then_inc(S["dt_mm"], 1)
                if more:
                    nc.tensor.matmul(proj_ps[0:XO, :], zero[:, 0:XO], zero[:], start=True, stop=False)

            def prologue():
                pe.sem_inc(S["yT_done"], 1)
                pe.sem_inc(S["hc_used"], NOUT)
                pe.wait_ge(S["setup"], 2)
                nc.tensor.matmul(proj_ps[0:XO, :], zero[:, 0:XO], zero[:], start=True, stop=False)

            chunks(pe, pair, boundary, prologue)

        @block.scalar
        def _(act):
            def softplus_tail(s, b_next_p1):
                act.wait_ge(S["v_done"], b_next_p1)
                nc.scalar.activation(mag[:], v[:], ACT.Abs).then_inc(S["abs_exp"], 1)
                act.wait_ge(S["abs_exp"], b_next_p1 * 2 - 1)
                nc.scalar.activation(mag[:], mag[:], ACT.Exp, scale=-1.0).then_inc(S["abs_exp"], 1)
                act.wait_ge(S["abs_exp"], b_next_p1 * 2)
                nc.scalar.activation(mag[:], mag[:], ACT.Ln, bias=1.0).then_inc(S["ln_done"], 1)
                nc.scalar.activation(aneg[:, s], par[:, s, 2:2 + NS], ACT.Exp).then_inc(S["aneg_step"], 1)
                act.wait_ge(S["aneg_step"], b_next_p1 * 2 - 1)
                nc.scalar.mul(aneg[:, s], aneg[:, s], -1.0).then_inc(S["aneg_step"], 1)

            def x_copy(s, ma):
                act.wait_ge(a_in[s], (ma + 1) * (NA * LOAD))
                if first:
                    act.wait_ge(S["x_mm"], ma * 2 + s + 1)
                    nc.scalar.activation(x[:, s, x_at:x_at + T], misc[:], ACT.Copy).then_inc(S["x_copied"], 1)
                    act.wait_ge(S["x_copied"], ma * 2 + s + 2)
                nc.scalar.activation(xc_out[:, s], x[:, s, tap_at[0]:tap_at[0] + T], ACT.Identity,
                                     bias=convp[:, s, TAPS:TAPS + 1], scale=convp[:, s, 0:1]).then_inc(S["tap0_done"], 1)

            def z_copy(s, ma):
                act.wait_ge(S["z_mm"], ma * 2 + s + 1)
                nc.scalar.activation(z_out[:, s], misc[:], ACT.Copy).then_inc(S["z_copied"], 1)

            def yT_copy(s, b):
                act.wait_ge(S["yT_done"], b + 1)
                nc.scalar.activation(y_out[:, s], yT[:], ACT.Copy).then_inc(S["yT_copied"], 1)

            def pair(eng, m, j, a, b, k=None, end=False):
                ma = a_pair(m, b)
                for s in range(2):
                    if not b:
                        x_copy(s, ma)
                        if first:
                            z_copy(s, ma)
                        continue
                    for n in range(NS):
                        act.wait_ge(S["scan_done"], m * 32 + s * 16 + n + 4)
                        if n == 0:
                            act.wait_ge(S["du_done"], m * 2 + s + 1)
                            act.wait_ge(S["aneg_step"], m * 4 + s * 2 + 2)
                            act.wait_ge(b_in[s], (m + 1) * (NB * LOAD))
                        nc.scalar.activation(da[:, n % 2], delta[:, s], ACT.Exp,
                                             scale=aneg[:, s, n:n + 1]).then_inc(S["exp_done"], 1)
                        if n >= 3:
                            act.wait_ge(S["hc_done"], m * 32 + s * 16 + n + 1)
                            nc.scalar.activation(state_out[:, s, n - 3:n - 2],
                                                 h[:, (s * 16 + n - 3) % 3, last_col:last_col + 1],
                                                 ACT.Copy).then_inc(S["h_saved"], 1)
                        if n == 2:
                            yT_copy(1 - s, m * 2 + s)
                        if n == 3:
                            nc.scalar.activation(ud[:, s], u[:, s], ACT.Copy,
                                                 scale=par[:, s, 1:2]).then_inc(S["ud_done"], 1)
                        if a and n == 7:
                            x_copy(s, ma)
                        if n == 11 and not (end and s == 1):
                            act.wait_ge(b_in[1 - s], (m + s) * (NB * LOAD) + NB * LOAD)
                            softplus_tail(1 - s, m * 2 + s + 2)
                    if a and first:
                        z_copy(s, ma)

            def boundary(k, more):
                act.wait_ge(S["proj_closed"], k + 1)
                nc.scalar.activation(proj[:], proj_ps[0:XO, :], ACT.Copy).then_inc(S["proj_copied"], 1)
                act.wait_ge(b_in[0], k * (DB // 2 * NB * LOAD) + NB * LOAD)
                softplus_tail(0, k * DB + 1)

            def prologue():
                act.sem_inc(S["x_copied"], 1)
                act.sem_inc(S["z_copied"], 1)
                act.sem_inc(S["h_saved"], 1)
                act.wait_ge(S["setup"], 2)

            chunks(act, pair, boundary, prologue)
            act.wait_ge(S["stored"], all_stores * LOAD)
            yT_copy(1, NCH * DB)

        @block.gpsimd
        def _(pool):
            def pair(eng, m, j, a, b, k=None, end=False):
                if not b:
                    return
                for s in range(2):
                    pool.wait_ge(S["du_done"], m * 2 + s + 1)
                    for g in range(NG):
                        pool.wait_ge(b_loaded[g], k * LOAD + LOAD)
                        pool.wait_ge(S["scan_done"], m * 32 + s * 16 + g * G + 1)
                        nc.gpsimd.tensor_tensor(w[:, g % 2], du[:, s].unsqueeze(1).to_broadcast([P, G, T]),
                                                bcast_b[:, g * G:(g + 1) * G], ALU.mult).then_inc(S["w_done"], 1)

            nc.gpsimd.memset(zero[:], 0.0).then_inc(S["setup"], 1)
            pool.sem_inc(S["w_done"], 1)
            with pool.Fori(0, NCH - 1) as k:
                with pool.Fori(0, DB // 2) as j:
                    pair(pool, k * (DB // 2) + j, j, a=True, b=True, k=k)
            with pool.Fori(0, DB // 2) as j:
                pair(pool, (NCH - 1) * (DB // 2) + j, j, a=False, b=True, k=NCH - 1)

        @block.vector
        def _(dve):
            def dt_step(s, b_p1):
                dve.wait_ge(S["dt_mm"], b_p1)
                nc.vector.tensor_scalar(v[:], misc[:], par[:, s, 0:1], 1e-5, ALU.add, ALU.max).then_inc(S["dt_read"], 1)

            def v_step(s, dt_base):
                dve.wait_ge(S["dt_read"], dt_base)
                nc.vector.tensor_scalar(v[:], v[:], 1.0, par[:, s, 0:1], ALU.min, ALU.add).then_inc(S["v_done"], 1)

            def delta_step(s, b_p1):
                dve.wait_ge(S["ln_done"], b_p1)
                nc.vector.scalar_tensor_tensor(delta[:, s], v[:], 0.0, mag[:], ALU.max,
                                               ALU.add).then_inc(S["pre_step"], 1)
                nc.vector.tensor_scalar(u[:, s], xc[:, s], 10.0, -10.0, ALU.min, ALU.max).then_inc(S["pre_step"], 1)

            def du_step(s, b_p1):
                dve.wait_ge(S["pre_step"], b_p1 * 2)
                nc.vector.tensor_tensor(du[:, s], delta[:, s], u[:, s], ALU.mult).then_inc(S["du_done"], 1)

            def conv_tap(s, ma, i):
                if i == 1:
                    dve.wait_ge(S["tap0_done"], ma * 2 + s + 1)
                else:
                    dve.wait_ge(S["conv_step"], ma * 4 + s * 2 + i - 1)
                nc.vector.scalar_tensor_tensor(xc_out[:, s], x[:, s, tap_at[i]:tap_at[i] + T], convp[:, s, i:i + 1],
                                               xc_out[:, s], ALU.mult, ALU.add
                                               ).then_inc(S["conv_done" if i == TAPS - 1 else "conv_step"], 1)

            def saved_by(q, m):
                unit, n = divmod(q, NS)
                if n < NS - 3:
                    dve.wait_ge(S["h_saved"], m * 26 + (unit * 13 + n + 2))
                else:
                    dve.wait_ge(S["h_saved_dve"], m * 6 + (unit * 3 + n - 12 + 3))

            def pair(eng, m, j, a, b, k=None, end=False):
                ma = a_pair(m, b)
                for s in range(2):
                    if not b:
                        for i in range(1, TAPS):
                            conv_tap(s, ma, i)
                        continue
                    nxt = not (end and s == 1)

                    def scan(n):
                        p = s * NS + n
                        dve.wait_ge(S["exp_done"], m * 32 + p + 1)
                        if n % G == 0:
                            dve.wait_ge(S["w_done"], m * 8 + s * 4 + n // G + 2)
                        if n == 0:
                            dve.wait_ge(b_in[s], (m + 1) * (NB * LOAD))
                        q = p - 3 if p >= 3 else {0: -2, 1: -1, 2: -3}[p]
                        dve.wait_ge(S["hc_done"], m * 32 + q + 4)
                        saved_by(q, m)
                        nc.vector.tensor_tensor_scan(flip(h[:, p % 3]), flip(da[:, n % 2]), flip(w[:, n // G % 2, n % G]),
                                                     state_in[:, s, n:n + 1], ALU.mult,
                                                     ALU.add).then_inc(S["scan_done"], 1)

                    def weigh(n):
                        p = s * NS + n
                        if n % G == 0:
                            dve.wait_ge(c_loaded[n // G], k * LOAD + LOAD)
                        dve.wait_ge(S["scan_done"], m * 32 + p + 6)
                        dve.wait_ge(S["hc_used"], m * 32 + p + 1)
                        nc.vector.tensor_tensor(hc[:, p % NOUT], h[:, p % 3], bcast_c[:, n],
                                                ALU.mult).then_inc(S["hc_done"], 1)

                    for n in range(NS):
                        scan(n)
                        if n:
                            weigh(n - 1)
                        if a and 9 <= n <= 11:
                            conv_tap(s, ma, n - 8)
                        if n == 10 and nxt:
                            dve.wait_ge(b_in[1 - s], (m + s) * (NB * LOAD) + NB * LOAD)
                            dt_step(1 - s, m * 2 + s + 2)
                        if n == 11 and nxt:
                            v_step(1 - s, m * 2 + s + (3 if not first else 2))
                        if n == 13 and nxt:
                            dve.wait_ge(S["ud_done"], m * 2 + s + 1)
                            delta_step(1 - s, m * 2 + s + 2)
                        if n == 14 and nxt:
                            du_step(1 - s, m * 2 + s + 2)
                    weigh(NS - 1)
                    for n in range(NS - 3, NS):
                        nc.vector.tensor_copy(state_out[:, s, n:n + 1],
                                              h[:, (s * NS + n) % 3, last_col:last_col + 1]
                                              ).then_inc(S["h_saved_dve"], 1)

            def boundary(k, more):
                dve.wait_ge(b_in[0], k * (DB // 2 * NB * LOAD) + NB * LOAD)
                dt_step(0, k * DB + 1)
                v_step(0, k * DB + (2 if not first else 1))
                dve.wait_ge(S["ln_done"], k * DB + 1)
                delta_step(0, k * DB + 1)
                du_step(0, k * DB + 1)

            def prologue():
                if not first:
                    dve.sem_inc(S["dt_read"], 1)
                dve.sem_inc(S["scan_done"], 5)
                dve.sem_inc(S["hc_done"], 3)
                dve.sem_inc(S["h_saved_dve"], 3)
                nc.vector.memset(yT[:], 0.0).then_inc(S["setup"], 1)

            chunks(dve, pair, boundary, prologue)


def stage_out(nc, ident, yf_d, yb_d, z_d, wout_d, x1T_d, out_d):
    with Scope(nc, "out") as sc:
        wout = sc.sb("wout", [P, KT, DB, P])
        yg = sc.sb("yg", [P, 2, DB, T])
        yf, yb = sc.sb("yf", [P, 2, T]), sc.sb("yb", [P, 2, T])
        z, sz = sc.sb("z", [P, 2, T]), sc.sb("sz", [P, 2, T])
        x1 = sc.sb("x1", [P, 2, T])
        o, test = sc.sb("o", [P, 2, T]), sc.sb("test", [P, 2, T])
        zero, one, minus = sc.sb("zero", [P, T]), sc.sb("one", [P, T]), sc.sb("minus", [P, T])
        yt_ps, o_ps = sc.ps("yt_ps", [P, 2, T]), sc.ps("o_ps", [P, 2, T])
        w_loaded, const_ready = sc.sem("w_loaded"), sc.sem("const_ready")
        y_loaded, x_loaded = [sc.sem(f"y_loaded{s}") for s in range(2)], [sc.sem(f"x_loaded{s}") for s in range(2)]
        o_stored = [sc.sem(f"o_stored{s}") for s in range(2)]
        summed, silu_done, yt_done, gated = sc.sem("summed"), sc.sem("silu_done"), sc.sem("yt_done"), sc.sem("gated")
        o_mm, o_read, o_step, o_done = sc.sem("o_mm"), sc.sem("o_read"), sc.sem("o_step"), sc.sem("o_done")
        passed = sc.sem("passed")
        STEPS = 6
        block = sc.block()

        def chunks(eng, prepare, project):
            for q in range(KT):
                prepare(0, 0, q)
            with eng.Fori(0, NCH // 2 - 1) as i:
                for g in range(2):
                    for q in range(KT):
                        project(i * 2 + g, g, q)
                        prepare(i * 2 + g + 1, 1 - g, q)
            for q in range(KT):
                project(NCH - 2, 0, q)
                prepare(NCH - 1, 1, q)
            for q in range(KT):
                project(NCH - 1, 1, q)

        @block.sync
        def _(sp):
            sp.sem_inc(o_stored[0], LOAD)
            sp.sem_inc(o_stored[1], LOAD)

            def prepare(c, g, q):
                for s in range(2):
                    db = 2 * q + s
                    sp.wait_ge(gated, c * DB + db + 1)
                    sp.dma_start(yf[:, s], yf_d[ds(c * DB + db + 1, 1)].rearrange("o p t d -> (o p) (t d)")
                                 ).then_inc(y_loaded[s], LOAD)
                    sp.dma_start(yb[:, s], yb_d[ds((NCH - 1) * DB + db + 1 - c * DB, 1)]
                                 .rearrange("o p t d -> (o p) (t d)")).then_inc(y_loaded[s], LOAD)
                    sp.dma_start(z[:, s], z_d[db * P:(db + 1) * P, ds(c * T, T)]).then_inc(y_loaded[s], LOAD)
                if q == 0 and isinstance(c, int) and c == 0:
                    for r in range(KT):
                        sp.dma_start(wout[:, r], wout_d[r]).then_inc(w_loaded, LOAD)

            def project(c, g, q):
                s = q % 2
                sp.wait_ge(o_done, c * KT + q + 1)
                sp.dma_start(x1[:, s], x1T_d[q * P:(q + 1) * P, ds(c * T, T)]).then_inc(x_loaded[s], LOAD)
                sp.wait_ge(o_done, c * KT + q + 3)
                sp.dma_start(out_d[q * P:(q + 1) * P, ds(c * T, T)], o[:, s]).then_inc(o_stored[s], LOAD)

            chunks(sp, prepare, project)
            for s in range(2):
                sp.wait_ge(o_stored[s], (NCH * KT // 2 + 1) * LOAD)

        @block.gpsimd
        def _(pool):
            nc.gpsimd.memset(zero[:], 0.0).then_inc(const_ready, 1)
            nc.gpsimd.memset(one[:], 1.0).then_inc(const_ready, 1)
            nc.gpsimd.memset(minus[:], -1.0).then_inc(const_ready, 1)

            def prepare(c, g, q):
                for s in range(2):
                    pool.wait_ge(y_loaded[s], c * (KT * 3 * LOAD) + (q + 1) * 3 * LOAD)
                    nc.gpsimd.tensor_tensor(yf[:, s], yf[:, s], yb[:, s], ALU.add).then_inc(summed, 1)

            chunks(pool, prepare, lambda c, g, q: None)

        @block.scalar
        def _(act):
            def prepare(c, g, q):
                for s in range(2):
                    act.wait_ge(y_loaded[s], c * (KT * 3 * LOAD) + (q + 1) * 3 * LOAD)
                    nc.scalar.activation(sz[:, s], z[:, s], ACT.Silu).then_inc(silu_done, 1)

            chunks(act, prepare, lambda c, g, q: None)

        @block.tensor
        def _(pe):
            def prepare(c, g, q):
                for s in range(2):
                    u = 2 * q + s
                    pe.wait_ge(summed, c * DB + u + 1)
                    pe.wait_ge(gated, c * DB + u + 1)
                    for tb in range(TB):
                        last = nc.tensor.matmul(yt_ps[:, s, tb * P:(tb + 1) * P], yf[:, s, tb * P:(tb + 1) * P],
                                                ident[:], is_transpose=True, start=(tb == 0), stop=(tb == TB - 1))
                    last.then_inc(yt_done, 1)

            def project(c, g, q):
                if q == 0:
                    pe.wait_ge(w_loaded, KT * LOAD)
                    pe.wait_ge(gated, c * DB + DB + 2)
                pe.wait_ge(o_read, c * KT + q + 1)
                for b in range(DB):
                    last = nc.tensor.matmul(o_ps[:, q % 2], wout[:, q, b], yg[:, g, b], start=(b == 0),
                                            stop=(b == DB - 1))
                last.then_inc(o_mm, 1)

            chunks(pe, prepare, project)

        @block.vector
        def _(dve):
            dve.sem_inc(gated, 2)
            dve.sem_inc(o_read, 2)
            dve.sem_inc(o_done, 2)
            u32 = mybir.dt.uint32

            def prepare(c, g, q):
                for s in range(2):
                    u = 2 * q + s
                    dve.wait_ge(yt_done, c * DB + u + 1)
                    dve.wait_ge(silu_done, c * DB + u + 1)
                    nc.vector.tensor_tensor(yg[:, g, u], yt_ps[:, s], sz[:, s], ALU.mult).then_inc(gated, 1)

            def project(c, g, q):
                s = q % 2

                def after(step):
                    hold(dve, o_step, c * (KT * STEPS) + (q * STEPS + step), passed)

                dve.wait_ge(const_ready, 3)
                dve.wait_ge(o_mm, c * KT + q + 1)
                dve.wait_ge(o_stored[s], c * (KT // 2 * LOAD) + (q // 2 + 1) * LOAD)
                nc.vector.tensor_copy(o[:, s], o_ps[:, s]).then_inc(o_read, 1)
                dve.wait_ge(o_read, c * KT + q + 3)
                nc.vector.tensor_tensor(test[:, s], o[:, s], o[:, s], ALU.not_equal).then_inc(o_step, 1)
                after(1)
                nc.vector.copy_predicated(o[:, s], test[:, s].bitcast(u32), zero[:]).then_inc(o_step, 1)
                for step, (op, bound, value) in ((2, (ALU.is_gt, FMAX, one)), (4, (ALU.is_lt, -FMAX, minus))):
                    dve.wait_ge(o_step, c * (KT * STEPS) + (q * STEPS + step))
                    nc.vector.tensor_scalar(test[:, s], o[:, s], bound, None, op).then_inc(o_step, 1)
                    after(step + 1)
                    nc.vector.copy_predicated(o[:, s], test[:, s].bitcast(u32), value[:]).then_inc(o_step, 1)
                dve.wait_ge(o_step, c * (KT * STEPS) + (q * STEPS + STEPS))
                dve.wait_ge(x_loaded[s], c * (KT // 2 * LOAD) + (q // 2 + 1) * LOAD)
                nc.vector.tensor_tensor(o[:, s], o[:, s], x1[:, s], ALU.add).then_inc(o_done, 1)

            chunks(dve, prepare, project)


def metaformer(nc, x, dt_w, dt_b, log_a, ln_w, ln_b, winx, winz, wout, wx, wdt, convp, parb, out):
    def scratch(name, shape):
        return nc.dram_tensor(name, shape, F32).ap()

    hnT, x1T = scratch("hnT", (C, HW)), scratch("x1T", (C, HW))
    x_pad, z = scratch("x_pad", (DI, HALO + HW + HALO)), scratch("z", (DI, HW))
    xc = scratch("xc", (NCH * DB, P, T))
    bc = scratch("bc", (NCH, 2 * NS, T))
    states = [scratch(f"state{d}", ((NCH + 1) * DB, P, NS)) for d in range(2)]
    yT = [scratch(f"yT{d}", (NCH * DB + 1, P, TB, P)) for d in range(2)]
    with Scope(nc, "all") as top:
        ident = top.sb("ident", [P, P])
        with Scope(nc, "norm") as sc:
            xn = sc.sb("xn", [P, NT * C])
            mv = sc.sb("mv", [P, NT * 2])
            mean_w = sc.sb("mean_w", [P, P])
            rstd2 = sc.sb("rstd2", [P, C])
            with Scope(nc, "mean") as ms:
                mean_ps = ms.ps("mean_ps", [P, C])
                stage_channel_norm(nc, xn, ident, mean_w, mean_ps, x)
                stage_pixel_variance(nc, xn, mean_w, mean_ps, rstd2)
            stage_channel_scan(nc, xn, ident, rstd2, mv, x, ln_w, ln_b, dt_w, dt_b, log_a)
            stage_token_norm(nc, xn, ident, mv, hnT, x1T, x_pad, states)
        for rev in (True, False):
            d = int(rev)
            stage_scan(nc, rev, ident, hnT, winx, winz, wx[d], wdt[d], convp[d], parb[d], x_pad, xc, z, bc,
                       states[d], yT[d])
        stage_out(nc, ident, yT[0], yT[1], z, wout, x1T, out)


def kernel(**inputs):
    import numpy as np
    import concourse.bacc as bacc
    from concourse.bass_utils import run_bass_kernel_spmd

    g = {n: np.asarray(a) for n, a in inputs.items()}

    def tiles(a, n):
        return a.reshape(n, P, a.shape[1] // P, P).transpose(0, 3, 2, 1)

    def per_block(*cols):
        return np.concatenate([c.reshape(DB, P, -1) for c in cols], axis=2)

    win = g["L0_ffn_in_proj_w"]
    arrays = {
        "x": g["x"].reshape(C, HW),
        "dt_w": np.concatenate([g["L0_conv_dt_w"].reshape(ROW, 1)] * 2),
        "dt_b": np.broadcast_to(g["L0_conv_dt_b"].reshape(1, 1), (P, 1)),
        "log_a": np.repeat(g["L0_conv_log_A"].reshape(NT, 2).T, ROW, axis=0),
        "ln_w": g["L0_conv_ln_w"].reshape(NT, P).T,
        "ln_b": g["L0_conv_ln_b"].reshape(NT, P).T,
        "winx": tiles(win[:DI], DB),
        "winz": tiles(win[DI:], DB),
        "wout": tiles(g["L0_ffn_out_proj_w"], KT),
    }
    for d, b in enumerate(("", "b_")):
        arrays[f"wx{d}"] = g[f"L0_ffn_x_proj_{b}w"].T.reshape(DB, P, XO)
        arrays[f"wdt{d}"] = g[f"L0_ffn_dt_proj_{b}w"].reshape(DB, P, R).transpose(0, 2, 1)
        arrays[f"convp{d}"] = per_block(g[f"L0_ffn_conv1d_{b}w"], g[f"L0_ffn_conv1d_{b}bias"])
        arrays[f"parb{d}"] = per_block(g[f"L0_ffn_dt_proj_{b}bias"], g["L0_ffn_D_b" if d else "L0_ffn_D"],
                                       g["L0_ffn_A_b_log" if d else "L0_ffn_A_log"])
    arrays = {n: np.ascontiguousarray(a) for n, a in arrays.items()}

    nc = bacc.Bacc("TRN2", target_bir_lowering=False, num_devices=1)
    ap = {n: nc.dram_tensor(n, a.shape, F32, kind="ExternalInput").ap() for n, a in arrays.items()}
    out = nc.dram_tensor("out", (C, HW), F32, kind="ExternalOutput").ap()
    both = {n: [ap[f"{n}0"], ap[f"{n}1"]] for n in ("wx", "wdt", "convp", "parb")}
    metaformer(nc, ap["x"], ap["dt_w"], ap["dt_b"], ap["log_a"], ap["ln_w"], ap["ln_b"], ap["winx"], ap["winz"],
               ap["wout"], both["wx"], both["wdt"], both["convp"], both["parb"], out)
    r = run_bass_kernel_spmd(nc, [arrays], core_ids=[0])
    return r.results[0]["out"].reshape(1, C, 64, 64)
```

```python
from contextlib import ExitStack

import concourse.bass as bass
from concourse import mybir

F32 = mybir.dt.float32
ALU = mybir.AluOpType
ACT = mybir.ActivationFunctionType

P = 128
C = 1024
HW = 4096
ROW = 64
NT = HW // P
KT = C // P
DI = 2048
DB = DI // P
NS = 16
R = 64
XO = R + 2 * NS
T = 512
NCH = HW // T
TB = T // P
TAPS = 4
HALO = TAPS - 1
G = 4
NG = NS // G
NOUT = 8
EPS_C, EPS_HW, EPS_T = 1e-6, 1e-5, 1e-5
FMAX = 3.4028234663852886e38
LOAD = 16


def ds(start, n):
    return bass.ds(start, n)


def hold(eng, sem, value, passed):
    eng.wait_ge(sem, value)
    eng.sem_inc(passed, 1)


class Scope:

    def __init__(self, nc, stage):
        self.nc, self.stage, self.stack = nc, stage, ExitStack()

    def __enter__(self):
        self.stack.__enter__()
        return self

    def __exit__(self, *a):
        return self.stack.__exit__(*a)

    def sb(self, name, shape):
        return self.stack.enter_context(self.nc.sbuf_tensor(f"{self.stage}_{name}", shape, F32))

    def ps(self, name, shape):
        return self.stack.enter_context(self.nc.psum_tensor(f"{self.stage}_{name}", shape, F32))

    def sem(self, name):
        return self.stack.enter_context(self.nc.semaphore(f"{self.stage}_{name}"))

    def block(self):
        return self.stack.enter_context(self.nc.Block())


def stage_channel_norm(nc, xn, ident, mean_w, mean_ps, x_d):
    with Scope(nc, "n1") as sc:
        xin = sc.sb("xin", [P, 2, KT, P])
        zero = sc.sb("zero", [P, 512])
        stats = sc.sb("stats", [P, 2, 2, 6])
        mv = sc.sb("mv", [P, 2, 2])
        std = sc.sb("std", [P, 2])
        rstd = sc.sb("rstd", [P, 2])
        xt = sc.ps("xt", [P, 2, C])
        const_ready, x_loaded = sc.sem("const_ready"), [sc.sem("x_loaded0"), sc.sem("x_loaded1")]
        transposed, var_ready, std_ready = sc.sem("transposed"), sc.sem("var_ready"), sc.sem("std_ready")
        passed, inverted = sc.sem("passed"), sc.sem("inverted")
        chain, normalised = sc.sem("chain"), sc.sem("normalised")
        x_v = x_d.rearrange("(k p) t -> p k t", p=P)
        block = sc.block()

        @block.gpsimd
        def _(pool):
            nc.gpsimd.memset(ident[:], 0.0).then_inc(const_ready, 1)
            pool.wait_ge(const_ready, 1)
            nc.gpsimd.affine_select(out=ident[:], in_=ident[:], compare_op=ALU.not_equal, fill=1.0, base=0,
                                    pattern=[[-1, P]], channel_multiplier=1).then_inc(const_ready, 1)
            nc.gpsimd.memset(mean_w[:], 1.0 / HW).then_inc(const_ready, 1)
            nc.gpsimd.memset(zero[:], 0.0).then_inc(const_ready, 1)

        @block.sync
        def _(sp):
            for s in range(2):
                sp.dma_start(xin[:, s], x_v[:, :, s * P:(s + 1) * P]).then_inc(x_loaded[s], LOAD)
            with sp.Fori(0, NT // 2 - 1) as j:
                for s in range(2):
                    sp.wait_ge(transposed, j * 2 + s + 1)
                    sp.dma_start(xin[:, s], x_v[:, :, ds(j * (2 * P) + (2 + s) * P, P)]).then_inc(x_loaded[s], LOAD)

        @block.tensor
        def _(pe):
            pe.wait_ge(const_ready, 4)
            for h in range(2):
                nc.tensor.matmul(mean_ps[:, h * 512:(h + 1) * 512], zero[:, 0:P], zero[:], start=True, stop=False)
            def transpose(j, s):
                pe.wait_ge(x_loaded[s], (j + 1) * LOAD)
                pe.wait_ge(normalised, j * 2 + s + 1)
                for k in range(KT):
                    last = nc.tensor.matmul(xt[:, s, k * P:(k + 1) * P], xin[:, s, k], ident[:], is_transpose=True,
                                            start=(k % 4 == 0), stop=(k % 4 == 3))
                last.then_inc(transposed, 1)

            def add_to_mean(j, s):
                pe.wait_ge(normalised, j * 2 + s + 3)
                for h in range(2):
                    nc.tensor.matmul(mean_ps[:, h * 512:(h + 1) * 512], mean_w[:],
                                     xn[:, ds(j * (2 * C) + s * C + h * 512, 512)], start=False, stop=False)

            for s in range(2):
                transpose(0, s)
            with pe.Fori(0, NT // 2 - 1) as j:
                for s in range(2):
                    transpose(j + 1, s)
                    add_to_mean(j, s)
            for s in range(2):
                add_to_mean(NT // 2 - 1, s)
            for h in range(2):
                nc.tensor.matmul(mean_ps[:, h * 512:(h + 1) * 512], zero[:, 0:P], zero[:], start=False, stop=True)

        @block.vector
        def _(dve):
            def statistics(j, s):
                dve.wait_ge(transposed, j * 2 + s + 1)
                for h in range(2):
                    last = nc.vector.bn_stats(stats[:, s, h], xt[:, s, h * 512:(h + 1) * 512])
                last.then_inc(chain, 1)
                hold(dve, chain, j * 4 + s * 2 + 1, passed)
                nc.vector.bn_aggr(mv[:, s], stats[:, s].rearrange("p a b -> p (a b)")).then_inc(chain, 1)
                dve.wait_ge(chain, j * 4 + s * 2 + 2)
                nc.vector.tensor_scalar(mv[:, s, 1:2], mv[:, s, 1:2], EPS_C, None, ALU.add).then_inc(var_ready, 1)

            def inverse(j, s):
                dve.wait_ge(std_ready, j * 2 + s + 1)
                nc.vector.reciprocal(rstd[:, s:s + 1], std[:, s:s + 1]).then_inc(inverted, 1)

            def normalise(j, s):
                dve.wait_ge(inverted, j * 2 + s + 1)
                nc.vector.tensor_scalar(xn[:, ds(j * (2 * C) + s * C, C)], xt[:, s], mv[:, s, 0:1],
                                        rstd[:, s:s + 1], ALU.subtract, ALU.mult).then_inc(normalised, 1)

            dve.sem_inc(normalised, 2)
            statistics(0, 0)
            with dve.Fori(0, NT // 2 - 1) as j:
                statistics(j, 1)
                inverse(j, 0)
                normalise(j, 0)
                statistics(j + 1, 0)
                inverse(j, 1)
                normalise(j, 1)
            statistics(NT // 2 - 1, 1)
            for s in range(2):
                inverse(NT // 2 - 1, s)
                normalise(NT // 2 - 1, s)

        @block.scalar
        def _(act):
            with act.Fori(0, NT // 2) as j:
                for s in range(2):
                    act.wait_ge(var_ready, j * 2 + s + 1)
                    nc.scalar.activation(std[:, s:s + 1], mv[:, s, 1:2], ACT.Sqrt).then_inc(std_ready, 1)


def stage_pixel_variance(nc, xn, mean_w, mean_ps, rstd2):
    with Scope(nc, "n2") as sc:
        sq = sc.sb("sq", [P, 2, C])
        zero = sc.sb("zero", [P, 512])
        var_ps = sc.ps("var_ps", [P, C])
        zero_ready, centred, squared = sc.sem("zero_ready"), sc.sem("centred"), sc.sem("squared")
        summed, var_done, chain = sc.sem("summed"), sc.sem("var_done"), sc.sem("chain")
        block = sc.block()

        @block.gpsimd
        def _(pool):
            nc.gpsimd.memset(zero[:], 0.0).then_inc(zero_ready, 1)

        @block.vector
        def _(dve):
            with dve.Fori(0, NT) as t:
                nc.vector.tensor_tensor(xn[:, ds(t * C, C)], xn[:, ds(t * C, C)], mean_ps[:],
                                        ALU.subtract).then_inc(centred, 1)
            dve.wait_ge(var_done, 1)
            nc.vector.tensor_scalar(rstd2[:], var_ps[:], EPS_HW, None, ALU.add).then_inc(chain, 1)
            dve.wait_ge(chain, 2)
            nc.vector.reciprocal(rstd2[:], rstd2[:]).then_inc(chain, 1)

        @block.scalar
        def _(act):
            with act.Fori(0, NT // 2) as j:
                for s in range(2):
                    act.wait_ge(zero_ready, 1)
                    act.wait_ge(summed, j * 2 + s + 1)
                    act.wait_ge(centred, j * 2 + s + 1)
                    nc.scalar.activation(sq[:, s], xn[:, ds(j * (2 * C) + s * C, C)], ACT.Square).then_inc(squared, 1)
            act.wait_ge(chain, 1)
            nc.scalar.activation(rstd2[:], rstd2[:], ACT.Sqrt).then_inc(chain, 1)

        @block.tensor
        def _(pe):
            pe.sem_inc(summed, 2)
            pe.wait_ge(zero_ready, 1)
            for h in range(2):
                nc.tensor.matmul(var_ps[:, h * 512:(h + 1) * 512], zero[:, 0:P], zero[:], start=True, stop=False)
            with pe.Fori(0, NT // 2) as j:
                for s in range(2):
                    pe.wait_ge(squared, j * 2 + s + 1)
                    for h in range(2):
                        last = nc.tensor.matmul(var_ps[:, h * 512:(h + 1) * 512], mean_w[:],
                                                sq[:, s, h * 512:(h + 1) * 512], start=False, stop=False)
                    last.then_inc(summed, 1)
            for h in range(2):
                last = nc.tensor.matmul(var_ps[:, h * 512:(h + 1) * 512], zero[:, 0:P], zero[:], start=False, stop=True)
            last.then_inc(var_done, 1)


def stage_channel_scan(nc, xn, ident, rstd2, mv, x_d, lnw_d, lnb_d, dtw_d, dtb_d, loga_d):
    with Scope(nc, "n3") as sc:
        lnw, lnb, aneg = sc.sb("lnw", [P, NT]), sc.sb("lnb", [P, NT]), sc.sb("aneg", [P, NT])
        dtw, dtb, row_w = sc.sb("dtw", [P, 1]), sc.sb("dtb", [P, 1]), sc.sb("row_w", [P, P])
        xin = sc.sb("xin", [P, 2, KT, P])
        mag = sc.sb("mag", [P, 2, C])
        sp_ = sc.sb("softplus", [P, 2, C])
        decay = sc.sb("decay", [P, 2, C])
        scanned = sc.sb("scanned", [P, 2, C])
        stats, mv_t = sc.sb("stats", [P, 2, 2, 6]), sc.sb("mv_t", [P, 2, 2])
        dt_ps = sc.ps("dt_ps", [P, 2, C])
        xt = sc.ps("xt", [P, 2, C])
        par_loaded, x_loaded = sc.sem("par_loaded"), [sc.sem("x_loaded0"), sc.sem("x_loaded1")]
        scaled, normed, dt_done = sc.sem("scaled"), sc.sem("normed"), sc.sem("dt_done")
        ab_done, log_done, relu_done = sc.sem("ab_done"), sc.sem("log_done"), sc.sem("relu_done")
        sp_done, decay_done, scan_done = sc.sem("sp_done"), sc.sem("decay_done"), sc.sem("scan_done")
        transposed, added, chain = sc.sem("transposed"), sc.sem("added"), sc.sem("chain")
        achain, setup, passed = sc.sem("achain"), sc.sem("setup"), sc.sem("passed")
        x_v = x_d.rearrange("(k p) t -> p k t", p=P)
        block = sc.block()

        @block.sync
        def _(sp):
            for dst, src in ((lnw, lnw_d), (lnb, lnb_d), (aneg, loga_d), (dtw, dtw_d), (dtb, dtb_d)):
                sp.dma_start(dst[:], src).then_inc(par_loaded, LOAD)
            for s in range(2):
                sp.dma_start(xin[:, s], x_v[:, :, s * P:(s + 1) * P]).then_inc(x_loaded[s], LOAD)
            with sp.Fori(0, NT // 2 - 1) as j:
                for s in range(2):
                    sp.wait_ge(transposed, j * 2 + s + 1)
                    sp.dma_start(xin[:, s], x_v[:, :, ds(j * (2 * P) + (2 + s) * P, P)]).then_inc(x_loaded[s], LOAD)

        @block.gpsimd
        def _(pool):
            with pool.Fori(0, NT) as t:
                nc.gpsimd.tensor_tensor(xn[:, ds(t * C, C)], xn[:, ds(t * C, C)], rstd2[:],
                                        ALU.mult).then_inc(scaled, 1)

        @block.vector
        def _(dve):
            nc.vector.memset(row_w[:], 0.0).then_inc(setup, 1)
            dve.wait_ge(setup, 1)
            for r in range(2):
                nc.vector.memset(row_w[r * ROW:(r + 1) * ROW, r * ROW:(r + 1) * ROW], 1.0).then_inc(setup, 1)
            dve.wait_ge(par_loaded, 5 * LOAD)
            dve.wait_ge(setup, 3)
            nc.vector.tensor_scalar(row_w[:], row_w[:], dtw[:], None, ALU.mult).then_inc(setup, 1)
            dve.sem_inc(added, 2)

            def affine(j):
                for s in range(2):
                    dve.wait_ge(scaled, j * 2 + s + 1)
                    nc.vector.tensor_scalar(xn[:, ds(j * (2 * C) + s * C, C)], xn[:, ds(j * (2 * C) + s * C, C)],
                                            lnw[:, ds(j * 2 + s, 1)], lnb[:, ds(j * 2 + s, 1)],
                                            ALU.mult, ALU.add).then_inc(normed, 1)

            def relu(j):
                for s in range(2):
                    dve.wait_ge(dt_done, j * 2 + s + 1)
                    dve.wait_ge(decay_done, j * 2 + s + 1)
                    nc.vector.tensor_scalar(sp_[:, s], dt_ps[:, s], dtb[:], 0.0, ALU.add,
                                            ALU.max).then_inc(relu_done, 1)

            def add_log(j):
                for s in range(2):
                    dve.wait_ge(log_done, j * 2 + s + 1)
                    dve.wait_ge(relu_done, j * 2 + s + 1)
                    nc.vector.tensor_tensor(sp_[:, s], sp_[:, s], mag[:, s], ALU.add).then_inc(sp_done, 1)

            def scan(j):
                for s in range(2):
                    dve.wait_ge(decay_done, j * 2 + s + 3)
                    dve.wait_ge(added, j * 2 + s + 1)
                    nc.vector.tensor_tensor_scan(scanned[:, s], decay[:, s], xn[:, ds(j * (2 * C) + s * C, C)], 0.0,
                                                 ALU.mult, ALU.add).then_inc(scan_done, 1)
                for s in range(2):
                    dve.wait_ge(scan_done, j * 2 + s + 3)
                    dve.wait_ge(transposed, j * 2 + s + 1)
                    nc.vector.tensor_tensor(xn[:, ds(j * (2 * C) + s * C, C)], scanned[:, s], xt[:, s],
                                            ALU.add).then_inc(added, 1)
                for s in range(2):
                    hold(dve, added, j * 2 + s + 3, passed)
                    for h in range(2):
                        last = nc.vector.bn_stats(stats[:, s, h], xn[:, ds(j * (2 * C) + s * C + h * 512, 512)])
                    last.then_inc(chain, 1)
                for s in range(2):
                    hold(dve, chain, j * 6 + s + 1, passed)
                    nc.vector.bn_aggr(mv_t[:, s], stats[:, s].rearrange("p a b -> p (a b)")).then_inc(chain, 1)
                for s in range(2):
                    dve.wait_ge(chain, j * 6 + s + 3)
                    nc.vector.tensor_copy(mv[:, ds(j * 4 + s * 2, 2)], mv_t[:, s]).then_inc(chain, 1)

            def step(j, before=True, after=True):
                if after:
                    affine(j + 1)
                relu(j)
                if before:
                    scan(j - 1)
                add_log(j)

            affine(0)
            step(0, before=False)
            with dve.Fori(0, NT // 2 - 2) as i:
                step(i + 1)
            step(NT // 2 - 1, after=False)
            scan(NT // 2 - 1)

        @block.scalar
        def _(act):
            act.wait_ge(par_loaded, 5 * LOAD)
            nc.scalar.activation(aneg[:], aneg[:], ACT.Exp).then_inc(achain, 1)
            act.wait_ge(achain, 1)
            nc.scalar.mul(aneg[:], aneg[:], -1.0).then_inc(achain, 1)
            act.wait_ge(achain, 2)
            act.sem_inc(decay_done, 2)
            act.sem_inc(scan_done, 2)
            with act.Fori(0, NT // 2) as j:
                for s in range(2):
                    act.wait_ge(relu_done, j * 2 + s + 1)
                    nc.scalar.activation(mag[:, s], dt_ps[:, s], ACT.Abs, bias=dtb[:]).then_inc(ab_done, 1)
                for s in range(2):
                    act.wait_ge(ab_done, j * 4 + s + 1)
                    nc.scalar.activation(mag[:, s], mag[:, s], ACT.Exp, scale=-1.0).then_inc(ab_done, 1)
                for s in range(2):
                    act.wait_ge(ab_done, j * 4 + s + 3)
                    nc.scalar.activation(mag[:, s], mag[:, s], ACT.Ln, bias=1.0).then_inc(log_done, 1)
                for s in range(2):
                    act.wait_ge(par_loaded, 5 * LOAD)
                    act.wait_ge(sp_done, j * 2 + s + 1)
                    act.wait_ge(scan_done, j * 2 + s + 1)
                    nc.scalar.activation(decay[:, s], sp_[:, s], ACT.Exp,
                                         scale=aneg[:, ds(j * 2 + s, 1)]).then_inc(decay_done, 1)

        @block.tensor
        def _(pe):
            def dt_rows(j, ahead):
                for s in range(2):
                    pe.wait_ge(normed, j * 2 + s + 1)
                    if ahead:
                        pe.wait_ge(ab_done, j * 4 - 4 + s + 1)
                    for h in range(2):
                        last = nc.tensor.matmul(dt_ps[:, s, h * 512:(h + 1) * 512], row_w[:],
                                                xn[:, ds(j * (2 * C) + s * C + h * 512, 512)], start=True, stop=True)
                    last.then_inc(dt_done, 1)

            def transpose(j):
                for s in range(2):
                    pe.wait_ge(x_loaded[s], (j + 1) * LOAD)
                    pe.wait_ge(added, j * 2 + s + 1)
                    for k in range(KT):
                        last = nc.tensor.matmul(xt[:, s, k * P:(k + 1) * P], xin[:, s, k], ident[:], is_transpose=True,
                                                start=(k % 4 == 0), stop=(k % 4 == 3))
                    last.then_inc(transposed, 1)

            pe.wait_ge(setup, 4)
            dt_rows(0, False)
            with pe.Fori(0, NT // 2 - 1) as j:
                dt_rows(j + 1, True)
                transpose(j)
            transpose(NT // 2 - 1)


def stage_token_norm(nc, xn, ident, mv, hnT_d, x1T_d, x_pad_d, state_ds):
    with Scope(nc, "n4") as sc:
        rstd, nmr = sc.sb("rstd", [P, NT]), sc.sb("nmr", [P, NT])
        hn, xs = sc.sb("hn", [P, 2, C]), sc.sb("xs", [P, 2, C])
        hn_out, x_out = sc.sb("hn_out", [P, 2, C]), sc.sb("x_out", [P, 2, C])
        zero = sc.sb("zero", [P, DB * NS])
        hn_ps, x_ps = sc.ps("hn_ps", [P, 2, C]), sc.ps("x_ps", [P, 2, C])
        zero_ready, zero_stored = sc.sem("zero_ready"), sc.sem("zero_stored")
        chain, stats_ready = sc.sem("chain"), sc.sem("stats_ready")
        normed, hn_t, x_t, x_moved = sc.sem("normed"), sc.sem("hn_t"), sc.sem("x_t"), sc.sem("x_moved")
        hn_copied, x_copied = sc.sem("hn_copied"), sc.sem("x_copied")
        hn_stored = [sc.sem("hn_stored0"), sc.sem("hn_stored1")]
        x_stored = [sc.sem("x_stored0"), sc.sem("x_stored1")]
        mv3 = mv[:].rearrange("p (t c) -> p t c", c=2)
        hn_v = hnT_d.rearrange("(k p) t -> p k t", p=P)
        x1_v = x1T_d.rearrange("(k p) t -> p k t", p=P)
        block = sc.block()

        @block.gpsimd
        def _(pool):
            nc.gpsimd.memset(zero[:], 0.0).then_inc(zero_ready, 1)
            with pool.Fori(0, NT // 2) as j:
                for s in range(2):
                    pool.wait_ge(x_t, j * 2 + s + 1)
                    nc.gpsimd.tensor_copy(xs[:, s], xn[:, ds(j * (2 * C) + s * C, C)]).then_inc(x_moved, 1)

        @block.vector
        def _(dve):
            dve.sem_inc(x_copied, 2)
            nc.vector.tensor_scalar(rstd[:], mv3[:, :, 1], EPS_T, None, ALU.add).then_inc(chain, 1)
            dve.wait_ge(chain, 2)
            nc.vector.reciprocal(rstd[:], rstd[:]).then_inc(chain, 1)
            dve.wait_ge(chain, 3)
            nc.vector.scalar_tensor_tensor(nmr[:], mv3[:, :, 0], -1.0, rstd[:], ALU.mult,
                                           ALU.mult).then_inc(stats_ready, 1)
            with dve.Fori(0, NT // 2) as j:
                for s in range(2):
                    dve.wait_ge(x_t, j * 2 + s + 3)
                    dve.wait_ge(x_stored[s], (j + 1) * LOAD)
                    nc.vector.tensor_copy(x_out[:, s], x_ps[:, s]).then_inc(x_copied, 1)

        @block.scalar
        def _(act):
            act.sem_inc(hn_copied, 2)
            act.wait_ge(chain, 1)
            nc.scalar.activation(rstd[:], rstd[:], ACT.Sqrt).then_inc(chain, 1)
            with act.Fori(0, NT // 2) as j:
                for s in range(2):
                    act.wait_ge(stats_ready, 1)
                    act.wait_ge(hn_t, j * 2 + s + 1)
                    nc.scalar.activation(hn[:, s], xn[:, ds(j * (2 * C) + s * C, C)], ACT.Identity,
                                         bias=nmr[:, ds(j * 2 + s, 1)],
                                         scale=rstd[:, ds(j * 2 + s, 1)]).then_inc(normed, 1)
                for s in range(2):
                    act.wait_ge(hn_t, j * 2 + s + 3)
                    act.wait_ge(hn_stored[s], (j + 1) * LOAD)
                    nc.scalar.activation(hn_out[:, s], hn_ps[:, s], ACT.Copy).then_inc(hn_copied, 1)

        @block.tensor
        def _(pe):
            pe.sem_inc(hn_t, 2)
            pe.sem_inc(x_t, 2)
            with pe.Fori(0, NT // 2) as j:
                for s in range(2):
                    pe.wait_ge(x_moved, j * 2 + s + 1)
                    pe.wait_ge(x_copied, j * 2 + s + 1)
                    for k in range(KT):
                        last = nc.tensor.matmul(x_ps[:, s, k * P:(k + 1) * P], xs[:, s, k * P:(k + 1) * P], ident[:],
                                                is_transpose=True, start=(k % 4 == 0), stop=(k % 4 == 3))
                    last.then_inc(x_t, 1)
                    pe.wait_ge(normed, j * 2 + s + 1)
                    pe.wait_ge(hn_copied, j * 2 + s + 1)
                    for k in range(KT):
                        last = nc.tensor.matmul(hn_ps[:, s, k * P:(k + 1) * P], hn[:, s, k * P:(k + 1) * P], ident[:],
                                                is_transpose=True, start=(k % 4 == 0), stop=(k % 4 == 3))
                    last.then_inc(hn_t, 1)

        @block.sync
        def _(sp):
            for s in range(2):
                sp.sem_inc(hn_stored[s], LOAD)
                sp.sem_inc(x_stored[s], LOAD)
            sp.wait_ge(zero_ready, 1)
            for side in (0, HALO + HW):
                sp.dma_start(x_pad_d[:, side:side + HALO].rearrange("(b p) t -> p b t", p=P),
                             zero[:, 0:DB * HALO].rearrange("p (b t) -> p b t", t=HALO)).then_inc(zero_stored, LOAD)
            for state_d in state_ds:
                sp.dma_start(state_d[0:DB].rearrange("u p n -> p u n"),
                             zero[:].rearrange("p (u n) -> p u n", n=NS)).then_inc(zero_stored, LOAD)
            with sp.Fori(0, NT // 2) as j:
                for s in range(2):
                    sp.wait_ge(x_copied, j * 2 + s + 3)
                    sp.dma_start(x1_v[:, :, ds(j * (2 * P) + s * P, P)],
                                 x_out[:, s].rearrange("p (k t) -> p k t", t=P)).then_inc(x_stored[s], LOAD)
                    sp.wait_ge(hn_copied, j * 2 + s + 3)
                    sp.dma_start(hn_v[:, :, ds(j * (2 * P) + s * P, P)],
                                 hn_out[:, s].rearrange("p (k t) -> p k t", t=P)).then_inc(hn_stored[s], LOAD)
            sp.wait_ge(zero_stored, 4 * LOAD)
            for s in range(2):
                sp.wait_ge(x_stored[s], (NT // 2 + 1) * LOAD)
                sp.wait_ge(hn_stored[s], (NT // 2 + 1) * LOAD)


def stage_scan(nc, rev, ident, hnT_d, winx_d, winz_d, wx_d, wdt_d, convp_d, par_d, skip_d,
               x_pad_d, xc_d, z_d, bc_d, state_d, yT_d):
    name = "bwd" if rev else "fwd"
    first = rev
    with Scope(nc, name) as sc:
        hn = sc.sb("hn", [P, KT, T]) if first else None
        winx = sc.sb("winx", [P, 2, KT, P]) if first else None
        winz = sc.sb("winz", [P, 2, KT, P]) if first else None
        wx = sc.sb("wx", [P, 2, XO])
        convp = sc.sb("convp", [P, 2, TAPS + 1])
        x = sc.sb("x", [P, 2, T + HALO])
        xc_out = sc.sb("xc_out", [P, 2, T])
        z_out = sc.sb("z_out", [P, 2, T])
        zero = sc.sb("zero", [P, T])
        proj = sc.sb("proj", [XO, T])
        bcast_b, bcast_c = sc.sb("bcast_b", [P, NS, T]), sc.sb("bcast_c", [P, NS, T])
        par, skip = sc.sb("par", [P, 2, 1 + NS]), sc.sb("skip", [P, 2, 1])
        wdt = sc.sb("wdt", [R, 2, P])
        xc = sc.sb("xc", [P, 2, T])
        state_in, state_out = sc.sb("state_in", [P, 2, NS]), sc.sb("state_out", [P, 2, NS])
        aneg = sc.sb("aneg", [P, 2, NS])
        v = sc.sb("v", [P, T])
        mag = sc.sb("mag", [P, T])
        delta, u, du, ud = (sc.sb(n, [P, 2, T]) for n in ("delta", "u", "du", "ud"))
        w = sc.sb("w", [P, 2, G, T])
        hc = sc.sb("hc", [P, NOUT, T])
        y_out = sc.sb("y_out", [P, 2, TB, P])
        da = sc.ps("da", [P, 2, T])
        h = sc.ps("h", [P, 3, T])
        yT = sc.ps("yT", [P, TB, P])
        proj_ps = sc.ps("proj_ps", [P, T])
        misc = sc.ps("misc", [P, T])

        names = ("setup", "hn_loaded", "x_mm", "z_mm", "x_copied", "z_copied", "conv_step", "conv_done", "proj_mm",
                 "proj_closed", "proj_copied", "tap0_done", "bc_stored", "dt_mm", "dt_read", "v_done", "abs_exp", "ln_done", "aneg_step",
                 "pre_step", "du_done", "ud_done", "exp_done", "w_done", "scan_done", "hc_done", "h_saved",
                 "h_saved_dve", "hc_used", "yT_copied", "stored", "passed")
        S = {n: sc.sem(n) for n in names}
        b_loaded, c_loaded = [sc.sem(f"b_loaded{g}") for g in range(NG)], [sc.sem(f"c_loaded{g}") for g in range(NG)]
        a_in, p_in, b_in = ([sc.sem(f"{n}{s}") for s in range(2)] for n in ("a_in", "p_in", "b_in"))
        NA = 5 if first else 3
        NPL, NB = 3, 2

        def t0(k):
            return (NCH - 1) * T - k * T if rev else k * T

        def col(k):
            return t0(k) + HALO

        def flip(ap):
            return ap[:, ::-1] if rev else ap

        last_col = 0 if rev else T - 1
        x_at = 0 if rev else HALO
        tap_at = [HALO - k if rev else k for k in range(TAPS)]

        def chunks(eng, pair, boundary, prologue):
            prologue()
            with eng.Fori(0, DB // 2) as j:
                pair(eng, j, j, a=True, b=False)
            with eng.Fori(0, NCH - 1) as k:
                boundary(k, True)
                with eng.Fori(0, DB // 2 - 1) as j:
                    pair(eng, k * (DB // 2) + j, j, a=True, b=True, k=k)
                pair(eng, k * (DB // 2) + DB // 2 - 1, DB // 2 - 1, a=True, b=True, k=k, end=True)
            boundary(NCH - 1, False)
            with eng.Fori(0, DB // 2 - 1) as j:
                pair(eng, (NCH - 1) * (DB // 2) + j, j, a=False, b=True, k=NCH - 1)
            pair(eng, NCH * (DB // 2) - 1, DB // 2 - 1, a=False, b=True, k=NCH - 1, end=True)

        def a_pair(m, b):
            return m + DB // 2 if b else m

        stores = {(True, False): (3 if first else 1), (True, True): (5 if first else 3), (False, True): 2}
        base = {(True, False): 0, (True, True): DB * stores[True, False],
                (False, True): DB * stores[True, False] + DB * (NCH - 1) * stores[True, True]}
        all_stores = base[False, True] + DB * stores[False, True]

        block = sc.block()

        @block.sync
        def _(sp):
            def load_a(s, db, k):
                if first:
                    sp.dma_start(winx[:, s], winx_d[ds(db, 1)].rearrange("o p k d -> (o p) k d")).then_inc(a_in[s], LOAD)
                    sp.dma_start(winz[:, s], winz_d[ds(db, 1)].rearrange("o p k d -> (o p) k d")).then_inc(a_in[s], LOAD)
                    halo = x[:, s, T:T + HALO]
                    sp.dma_start(halo, x_pad_d[ds(db * P, P), ds(col(k) + T, HALO)]).then_inc(a_in[s], LOAD)
                else:
                    sp.dma_start(x[:, s], x_pad_d[ds(db * P, P), ds(t0(k), T + HALO)]).then_inc(a_in[s], LOAD)
                sp.dma_start(wx[:, s], wx_d[ds(db, 1)].rearrange("o p k -> (o p) k")).then_inc(a_in[s], LOAD)
                sp.dma_start(convp[:, s], convp_d[ds(db, 1)].rearrange("o p k -> (o p) k")).then_inc(a_in[s], LOAD)

            def load_p(s, u_, db):
                sp.dma_start(wdt[:, s], wdt_d[ds(db, 1)].rearrange("o p k -> (o p) k")).then_inc(p_in[s], LOAD)
                sp.dma_start(par[:, s], par_d[ds(db, 1)].rearrange("o p k -> (o p) k")).then_inc(p_in[s], LOAD)
                sp.dma_start(xc[:, s], xc_d[ds(u_, 1)].rearrange("o p k -> (o p) k")).then_inc(p_in[s], LOAD)

            def load_b(s, u_, db):
                sp.dma_start(skip[:, s], skip_d[ds(db, 1)].rearrange("o p k -> (o p) k")).then_inc(b_in[s], LOAD)
                sp.dma_start(state_in[:, s], state_d[ds(u_, 1)].rearrange("o p k -> (o p) k")).then_inc(b_in[s], LOAD)

            def pair(eng, m, j, a, b, k=None, end=False):
                n = stores[a, b]
                ma = a_pair(m, b)
                ka = 0 if not b else k + 1
                start = base[a, b] + (m * (2 * n) if b and a or not b else (m - (NCH - 1) * (DB // 2)) * (2 * n))
                for s in range(2):
                    db = j * 2 + s
                    if b and not end:
                        hold(sp, S["du_done"], m * 2 + s + 1, S["passed"])
                        load_p(s, m * 2 + s + 2, db + 2)
                    if b:
                        hold(sp, S["yT_copied"], m * 2 + s + 1, S["passed"])
                        sp.dma_start(yT_d[ds(m * 2 + s, 1)].rearrange("o p t d -> (o p) t d"),
                                     y_out[:, 1 - s]).then_inc(S["stored"], LOAD)
                    if a:
                        u_a = ma * 2 + s
                        if first:
                            hold(sp, S["x_copied"], ma * 2 + s + 2, S["passed"])
                            sp.dma_start(x_pad_d[ds(db * P, P), ds(col(ka), T)],
                                         x[:, s, x_at:x_at + T]).then_inc(S["stored"], LOAD)
                        hold(sp, S["conv_done"], ma * 2 + s + 1, S["passed"])
                        sp.dma_start(xc_d[ds(u_a, 1)].rearrange("o p k -> (o p) k"),
                                     xc_out[:, s]).then_inc(S["stored"], LOAD)
                        if first:
                            hold(sp, S["z_copied"], ma * 2 + s + 2, S["passed"])
                            sp.dma_start(z_d[ds(db * P, P), ds(t0(ka), T)],
                                         z_out[:, s]).then_inc(S["stored"], LOAD)
                    if b:
                        hold(sp, S["h_saved"], m * 26 + s * 13 + 14, S["passed"])
                        hold(sp, S["h_saved_dve"], m * 6 + s * 3 + 6, S["passed"])
                        sp.dma_start(state_d[ds(m * 2 + s + DB, 1)].rearrange("o p k -> (o p) k"),
                                     state_out[:, s]).then_inc(S["stored"], LOAD)
                    hold(sp, S["stored"], start * LOAD + (s + 1) * n * LOAD, S["passed"])
                    if a:
                        hold(sp, S["proj_mm"], ma * 2 + s + 1, S["passed"])
                        if first:
                            hold(sp, S["z_mm"], ma * 2 + s + 1, S["passed"])
                    if b:
                        hold(sp, S["exp_done"], m * 32 + (s + 1) * 16, S["passed"])
                        hold(sp, S["ud_done"], m * 2 + s + 1, S["passed"])
                    if not end:
                        if a and b:
                            load_a(s, db + 2, ka)
                        if b:
                            load_b(s, m * 2 + s + 2, db + 2)

            def boundary(k, more):
                for s in range(2):
                    load_p(s, k * DB + s, s)
                for s in range(2):
                    load_b(s, k * DB + s, s)
                hold(sp, S["proj_copied"], k + 1, S["passed"])
                sp.dma_start(bc_d[ds(k, 1)].rearrange("o n t -> (o n) t"), proj[R:XO, :]).then_inc(S["bc_stored"], LOAD)
                hold(sp, S["bc_stored"], k * LOAD + LOAD, S["passed"])
                hold(sp, S["w_done"], k * (DB * NG) + 1, S["passed"])
                for g in range(NG):
                    src = bc_d[ds(k, 1)][:, g * G:(g + 1) * G].rearrange("o n t -> (o n) t")
                    sp.dma_start(bcast_b[:, g * G:(g + 1) * G], src.partition_broadcast(P)).then_inc(b_loaded[g], LOAD)
                if more and first:
                    hold(sp, S["z_mm"], k * DB + DB, S["passed"])
                    sp.dma_start(hn[:], hnT_d.rearrange("(k p) t -> p k t", p=P)[:, :, ds(t0(k + 1), T)]
                                 ).then_inc(S["hn_loaded"], LOAD)
                if more:
                    load_a(0, 0, k + 1)
                hold(sp, S["hc_done"], k * (DB * NS) + 3, S["passed"])
                for g in range(NG):
                    src = bc_d[ds(k, 1)][:, NS + g * G:NS + (g + 1) * G].rearrange("o n t -> (o n) t")
                    sp.dma_start(bcast_c[:, g * G:(g + 1) * G], src.partition_broadcast(P)).then_inc(c_loaded[g], LOAD)
                if more:
                    load_a(1, 1, k + 1)

            def prologue():
                if first:
                    sp.dma_start(hn[:], hnT_d.rearrange("(k p) t -> p k t", p=P)[:, :, t0(0):t0(0) + T]
                                 ).then_inc(S["hn_loaded"], LOAD)
                for s in range(2):
                    load_a(s, s, 0)
                with sp.Fori(0, DB // 2 - 1) as j:
                    pair(sp, j, j, a=True, b=False)
                    for s in range(2):
                        load_a(s, j * 2 + s + 2, 0)
                pair(sp, DB // 2 - 1, DB // 2 - 1, a=True, b=False)

            prologue()
            with sp.Fori(0, NCH - 1) as k:
                boundary(k, True)
                with sp.Fori(0, DB // 2 - 1) as j:
                    pair(sp, k * (DB // 2) + j, j, a=True, b=True, k=k)
                pair(sp, k * (DB // 2) + DB // 2 - 1, DB // 2 - 1, a=True, b=True, k=k, end=True)
            boundary(NCH - 1, False)
            with sp.Fori(0, DB // 2 - 1) as j:
                pair(sp, (NCH - 1) * (DB // 2) + j, j, a=False, b=True, k=NCH - 1)
            pair(sp, NCH * (DB // 2) - 1, DB // 2 - 1, a=False, b=True, k=NCH - 1, end=True)
            hold(sp, S["yT_copied"], NCH * DB + 1, S["passed"])
            sp.dma_start(yT_d[NCH * DB], y_out[:, 1]).then_inc(S["stored"], LOAD)
            hold(sp, S["stored"], all_stores * LOAD + LOAD, S["passed"])

        @block.tensor
        def _(pe):
            def dt_matmul(s, loads, reads):
                pe.wait_ge(p_in[s], loads)
                pe.wait_ge(S["dt_read"], reads)
                nc.tensor.matmul(misc[:], wdt[:, s], proj[0:R, :], start=True, stop=True).then_inc(S["dt_mm"], 1)

            def pair(eng, m, j, a, b, k=None, end=False):
                ma = a_pair(m, b)
                for s in range(2):
                    nxt = b and not (end and s == 1)
                    m_next = (m + s) * (NPL * LOAD) + NPL * LOAD

                    def x_part(i0, i1):
                        if i0 == 0:
                            pe.wait_ge(a_in[s], (ma + 1) * (NA * LOAD))
                            if s == 0:
                                pe.wait_ge(S["hn_loaded"], ((k + 2) if b else 1) * LOAD)
                            if b:
                                pe.wait_ge(S["dt_read"], m * 2 + s + (2 if nxt else 1))
                            else:
                                pe.wait_ge(S["z_copied"], ma * 2 + s + 1)
                        for i in range(i0, i1):
                            last = nc.tensor.matmul(misc[:], winx[:, s, i], hn[:, i], start=(i == 0), stop=(i == KT - 1))
                        if i1 == KT:
                            last.then_inc(S["x_mm"], 1)

                    def z_part(i0, i1):
                        if i0 == 0:
                            pe.wait_ge(S["x_copied"], ma * 2 + s + 2)
                        for i in range(i0, i1):
                            last = nc.tensor.matmul(misc[:], winz[:, s, i], hn[:, i], start=(i == 0), stop=(i == KT - 1))
                        if i1 == KT:
                            last.then_inc(S["z_mm"], 1)

                    def projection():
                        if not first:
                            pe.wait_ge(a_in[s], (ma + 1) * (NA * LOAD))
                        pe.wait_ge(S["conv_done"], ma * 2 + s + 1)
                        nc.tensor.matmul(proj_ps[0:XO, :], wx[:, s], xc_out[:, s], start=False,
                                         stop=False).then_inc(S["proj_mm"], 1)

                    if not b:
                        if first:
                            x_part(0, KT)
                            z_part(0, KT)
                        projection()
                        continue
                    if nxt:
                        if first and a:
                            pe.wait_ge(S["z_copied"], ma * 2 + s + 1)
                        dt_matmul(1 - s, m_next, m * 2 + s + (1 if first else 2))
                    for n in range(NS):
                        if first and a and 1 <= n <= 4:
                            x_part(2 * (n - 1), 2 * n)
                        if first and a and 7 <= n <= 10:
                            z_part(2 * (n - 7), 2 * (n - 6))
                        if a and n == 13:
                            projection()
                        if n == NS - 1:
                            pe.wait_ge(S["ud_done"], m * 2 + s + 1)
                            for tb in range(TB):
                                nc.tensor.matmul(yT[:, tb], ud[:, s, tb * P:(tb + 1) * P], ident[:],
                                                 is_transpose=True, start=False, stop=False)
                        pe.wait_ge(S["hc_done"], m * 32 + s * 16 + n + 4)
                        if n == 0:
                            pe.wait_ge(S["yT_copied"], m * 2 + s + 1)
                        for tb in range(TB):
                            last = nc.tensor.matmul(yT[:, tb], hc[:, (s * 16 + n) % NOUT, tb * P:(tb + 1) * P], ident[:],
                                                    is_transpose=True, start=(n == 0 and tb == 0),
                                                    stop=(n == NS - 1 and tb == TB - 1))
                        last.then_inc(S["hc_used"], 1)

            def boundary(k, more):
                nc.tensor.matmul(proj_ps[0:XO, :], zero[:, 0:XO], zero[:], start=False, stop=True).then_inc(S["proj_closed"], 1)
                pe.wait_ge(S["proj_copied"], k + 1)
                if first:
                    pe.wait_ge(S["z_copied"], k * DB + DB + 1)
                else:
                    pe.wait_ge(S["dt_read"], k * DB + 1)
                pe.wait_ge(p_in[0], k * (DB // 2 * NPL * LOAD) + NPL * LOAD)
                nc.tensor.matmul(misc[:], wdt[:, 0], proj[0:R, :], start=True, stop=True).then_inc(S["dt_mm"], 1)
                if more:
                    nc.tensor.matmul(proj_ps[0:XO, :], zero[:, 0:XO], zero[:], start=True, stop=False)

            def prologue():
                pe.sem_inc(S["hc_used"], NOUT)
                pe.wait_ge(S["setup"], 2)
                nc.tensor.matmul(proj_ps[0:XO, :], zero[:, 0:XO], zero[:], start=True, stop=False)

            chunks(pe, pair, boundary, prologue)

        @block.scalar
        def _(act):
            def softplus_tail(s, b_p1, step):
                if step == 0:
                    act.wait_ge(S["v_done"], b_p1)
                    nc.scalar.activation(mag[:], v[:], ACT.Abs).then_inc(S["abs_exp"], 1)
                    nc.scalar.activation(aneg[:, s], par[:, s, 1:1 + NS], ACT.Exp).then_inc(S["aneg_step"], 1)
                elif step == 1:
                    act.wait_ge(S["abs_exp"], b_p1 * 2 - 1)
                    nc.scalar.activation(mag[:], mag[:], ACT.Exp, scale=-1.0).then_inc(S["abs_exp"], 1)
                    act.wait_ge(S["aneg_step"], b_p1 * 2 - 1)
                    nc.scalar.mul(aneg[:, s], aneg[:, s], -1.0).then_inc(S["aneg_step"], 1)
                elif step == 2:
                    act.wait_ge(S["abs_exp"], b_p1 * 2)
                    nc.scalar.activation(mag[:], mag[:], ACT.Ln, bias=1.0).then_inc(S["ln_done"], 1)

            def x_copy(s, ma):
                act.wait_ge(a_in[s], (ma + 1) * (NA * LOAD))
                if first:
                    act.wait_ge(S["x_mm"], ma * 2 + s + 1)
                    nc.scalar.activation(x[:, s, x_at:x_at + T], misc[:], ACT.Copy).then_inc(S["x_copied"], 1)
                    act.wait_ge(S["x_copied"], ma * 2 + s + 2)
                nc.scalar.activation(xc_out[:, s], x[:, s, tap_at[0]:tap_at[0] + T], ACT.Identity,
                                     bias=convp[:, s, TAPS:TAPS + 1], scale=convp[:, s, 0:1]).then_inc(S["tap0_done"], 1)

            def z_copy(s, ma):
                act.wait_ge(S["z_mm"], ma * 2 + s + 1)
                nc.scalar.activation(z_out[:, s], misc[:], ACT.Copy).then_inc(S["z_copied"], 1)

            def yT_copy(s, b):
                act.wait_ge(S["hc_used"], b * NS + NOUT)
                nc.scalar.activation(y_out[:, s], yT[:], ACT.Copy).then_inc(S["yT_copied"], 1)

            def pair(eng, m, j, a, b, k=None, end=False):
                ma = a_pair(m, b)
                for s in range(2):
                    if not b:
                        x_copy(s, ma)
                        if first:
                            z_copy(s, ma)
                        continue
                    for n in range(NS):
                        act.wait_ge(S["scan_done"], m * 32 + s * 16 + n + 4)
                        if n == 0:
                            act.wait_ge(S["du_done"], m * 2 + s + 1)
                            act.wait_ge(S["aneg_step"], m * 4 + s * 2 + 2)
                            act.wait_ge(b_in[s], (m + 1) * (NB * LOAD))
                        nc.scalar.activation(da[:, n % 2], delta[:, s], ACT.Exp,
                                             scale=aneg[:, s, n:n + 1]).then_inc(S["exp_done"], 1)
                        if n >= 3:
                            act.wait_ge(S["hc_done"], m * 32 + s * 16 + n + 1)
                            nc.scalar.activation(state_out[:, s, n - 3:n - 2],
                                                 h[:, (s * 16 + n - 3) % 3, last_col:last_col + 1],
                                                 ACT.Copy).then_inc(S["h_saved"], 1)
                        if n == 2:
                            yT_copy(1 - s, m * 2 + s)
                        if n == 4:
                            nc.scalar.activation(ud[:, s], u[:, s], ACT.Copy,
                                                 scale=skip[:, s]).then_inc(S["ud_done"], 1)
                        if a and n == (9 if first else 8):
                            x_copy(s, ma)
                        if n == 5 and not (end and s == 1):
                            act.wait_ge(p_in[1 - s], (m + s) * (NPL * LOAD) + NPL * LOAD)
                        if 5 <= n <= 7 and not (end and s == 1):
                            softplus_tail(1 - s, m * 2 + s + 2, n - 5)
                    if a and first:
                        z_copy(s, ma)

            def boundary(k, more):
                act.wait_ge(S["proj_closed"], k + 1)
                nc.scalar.activation(proj[:], proj_ps[0:XO, :], ACT.Copy).then_inc(S["proj_copied"], 1)
                act.wait_ge(p_in[0], k * (DB // 2 * NPL * LOAD) + NPL * LOAD)
                for step in range(3):
                    softplus_tail(0, k * DB + 1, step)

            def prologue():
                act.sem_inc(S["x_copied"], 1)
                act.sem_inc(S["z_copied"], 1)
                act.sem_inc(S["h_saved"], 1)
                act.wait_ge(S["setup"], 2)

            chunks(act, pair, boundary, prologue)
            act.wait_ge(S["stored"], all_stores * LOAD)
            yT_copy(1, NCH * DB)

        @block.gpsimd
        def _(pool):
            def pair(eng, m, j, a, b, k=None, end=False):
                if not b:
                    return
                for s in range(2):
                    pool.wait_ge(S["du_done"], m * 2 + s + 1)
                    for g in range(NG):
                        pool.wait_ge(b_loaded[g], k * LOAD + LOAD)
                        pool.wait_ge(S["scan_done"], m * 32 + s * 16 + g * G + 1)
                        nc.gpsimd.tensor_tensor(w[:, g % 2], du[:, s].unsqueeze(1).to_broadcast([P, G, T]),
                                                bcast_b[:, g * G:(g + 1) * G], ALU.mult).then_inc(S["w_done"], 1)

            nc.gpsimd.memset(zero[:], 0.0).then_inc(S["setup"], 1)
            pool.sem_inc(S["w_done"], 1)
            with pool.Fori(0, NCH - 1) as k:
                with pool.Fori(0, DB // 2) as j:
                    pair(pool, k * (DB // 2) + j, j, a=True, b=True, k=k)
            with pool.Fori(0, DB // 2) as j:
                pair(pool, (NCH - 1) * (DB // 2) + j, j, a=False, b=True, k=NCH - 1)

        @block.vector
        def _(dve):
            def dt_step(s, b_p1):
                dve.wait_ge(S["dt_mm"], b_p1)
                nc.vector.tensor_scalar(v[:], misc[:], par[:, s, 0:1], 1e-5, ALU.add, ALU.max).then_inc(S["dt_read"], 1)

            def v_step(s, dt_base):
                dve.wait_ge(S["dt_read"], dt_base)
                nc.vector.tensor_scalar(v[:], v[:], 1.0, par[:, s, 0:1], ALU.min, ALU.add).then_inc(S["v_done"], 1)

            def delta_step(s, b_p1):
                dve.wait_ge(S["ln_done"], b_p1)
                nc.vector.scalar_tensor_tensor(delta[:, s], v[:], 0.0, mag[:], ALU.max,
                                               ALU.add).then_inc(S["pre_step"], 1)
                nc.vector.tensor_scalar(u[:, s], xc[:, s], 10.0, -10.0, ALU.min, ALU.max).then_inc(S["pre_step"], 1)

            def du_step(s, b_p1):
                dve.wait_ge(S["pre_step"], b_p1 * 2)
                nc.vector.tensor_tensor(du[:, s], delta[:, s], u[:, s], ALU.mult).then_inc(S["du_done"], 1)

            def conv_tap(s, ma, i):
                if i == 1:
                    dve.wait_ge(S["tap0_done"], ma * 2 + s + 1)
                else:
                    dve.wait_ge(S["conv_step"], ma * 4 + s * 2 + i - 1)
                nc.vector.scalar_tensor_tensor(xc_out[:, s], x[:, s, tap_at[i]:tap_at[i] + T], convp[:, s, i:i + 1],
                                               xc_out[:, s], ALU.mult, ALU.add
                                               ).then_inc(S["conv_done" if i == TAPS - 1 else "conv_step"], 1)

            def saved_by(q, m):
                unit, n = divmod(q, NS)
                if n < NS - 3:
                    dve.wait_ge(S["h_saved"], m * 26 + (unit * 13 + n + 2))
                else:
                    dve.wait_ge(S["h_saved_dve"], m * 6 + (unit * 3 + n - 12 + 3))

            def pair(eng, m, j, a, b, k=None, end=False):
                ma = a_pair(m, b)
                for s in range(2):
                    if not b:
                        for i in range(1, TAPS):
                            conv_tap(s, ma, i)
                        continue
                    nxt = not (end and s == 1)

                    def scan(n):
                        p = s * NS + n
                        dve.wait_ge(S["exp_done"], m * 32 + p + 1)
                        if n % G == 0:
                            dve.wait_ge(S["w_done"], m * 8 + s * 4 + n // G + 2)
                        if n == 0:
                            dve.wait_ge(b_in[s], (m + 1) * (NB * LOAD))
                        q = p - 3 if p >= 3 else {0: -2, 1: -1, 2: -3}[p]
                        dve.wait_ge(S["hc_done"], m * 32 + q + 4)
                        saved_by(q, m)
                        nc.vector.tensor_tensor_scan(flip(h[:, p % 3]), flip(da[:, n % 2]), flip(w[:, n // G % 2, n % G]),
                                                     state_in[:, s, n:n + 1], ALU.mult,
                                                     ALU.add).then_inc(S["scan_done"], 1)

                    def weigh(n):
                        p = s * NS + n
                        if n % G == 0:
                            dve.wait_ge(c_loaded[n // G], k * LOAD + LOAD)
                        dve.wait_ge(S["scan_done"], m * 32 + p + 6)
                        dve.wait_ge(S["hc_used"], m * 32 + p + 1)
                        nc.vector.tensor_tensor(hc[:, p % NOUT], h[:, p % 3], bcast_c[:, n],
                                                ALU.mult).then_inc(S["hc_done"], 1)

                    for n in range(NS):
                        scan(n)
                        if n:
                            weigh(n - 1)
                        if a and 11 <= n <= 13:
                            conv_tap(s, ma, n - 10)
                        if n == 2 and nxt:
                            dve.wait_ge(p_in[1 - s], (m + s) * (NPL * LOAD) + NPL * LOAD)
                            dt_step(1 - s, m * 2 + s + 2)
                        if n == 3 and nxt:
                            v_step(1 - s, m * 2 + s + (3 if not first else 2))
                        if n == 8 and nxt:
                            dve.wait_ge(S["ud_done"], m * 2 + s + 1)
                            delta_step(1 - s, m * 2 + s + 2)
                        if n == 9 and nxt:
                            du_step(1 - s, m * 2 + s + 2)
                    weigh(NS - 1)
                    for n in range(NS - 3, NS):
                        nc.vector.tensor_copy(state_out[:, s, n:n + 1],
                                              h[:, (s * NS + n) % 3, last_col:last_col + 1]
                                              ).then_inc(S["h_saved_dve"], 1)

            def boundary(k, more):
                dve.wait_ge(p_in[0], k * (DB // 2 * NPL * LOAD) + NPL * LOAD)
                dt_step(0, k * DB + 1)
                v_step(0, k * DB + (2 if not first else 1))
                dve.wait_ge(S["ln_done"], k * DB + 1)
                delta_step(0, k * DB + 1)
                du_step(0, k * DB + 1)

            def prologue():
                if not first:
                    dve.sem_inc(S["dt_read"], 1)
                dve.sem_inc(S["scan_done"], 5)
                dve.sem_inc(S["hc_done"], 3)
                dve.sem_inc(S["h_saved_dve"], 3)
                nc.vector.memset(yT[:], 0.0).then_inc(S["setup"], 1)

            chunks(dve, pair, boundary, prologue)


def stage_out(nc, ident, yf_d, yb_d, z_d, wout_d, x1T_d, out_d):
    with Scope(nc, "out") as sc:
        wout = sc.sb("wout", [P, KT, DB, P])
        yg = sc.sb("yg", [P, 2, DB, T])
        yf, yb = sc.sb("yf", [P, 2, T]), sc.sb("yb", [P, 2, T])
        z, sz = sc.sb("z", [P, 2, T]), sc.sb("sz", [P, 2, T])
        x1 = sc.sb("x1", [P, 2, T])
        o, test = sc.sb("o", [P, 2, T]), sc.sb("test", [P, 2, T])
        zero, one, minus = sc.sb("zero", [P, T]), sc.sb("one", [P, T]), sc.sb("minus", [P, T])
        yt_ps, o_ps = sc.ps("yt_ps", [P, 2, T]), sc.ps("o_ps", [P, 2, T])
        w_loaded, const_ready = sc.sem("w_loaded"), sc.sem("const_ready")
        y_loaded, x_loaded = [sc.sem(f"y_loaded{s}") for s in range(2)], [sc.sem(f"x_loaded{s}") for s in range(2)]
        o_stored = [sc.sem(f"o_stored{s}") for s in range(2)]
        summed, silu_done, yt_done, gated = sc.sem("summed"), sc.sem("silu_done"), sc.sem("yt_done"), sc.sem("gated")
        o_mm, o_read, o_step, o_done = sc.sem("o_mm"), sc.sem("o_read"), sc.sem("o_step"), sc.sem("o_done")
        passed = sc.sem("passed")
        STEPS = 6
        block = sc.block()

        def chunks(eng, prepare, project, loads_first=False):
            def step(c, g, q):
                if loads_first:
                    prepare(c + 1, 1 - g, q)
                project(c, g, q)
                if not loads_first:
                    prepare(c + 1, 1 - g, q)

            for q in range(KT):
                prepare(0, 0, q)
            with eng.Fori(0, NCH // 2 - 1) as i:
                for g in range(2):
                    for q in range(KT):
                        step(i * 2 + g, g, q)
            for q in range(KT):
                step(NCH - 2, 0, q)
            for q in range(KT):
                project(NCH - 1, 1, q)

        @block.sync
        def _(sp):
            sp.sem_inc(o_stored[0], LOAD)
            sp.sem_inc(o_stored[1], LOAD)

            def prepare(c, g, q):
                for s in range(2):
                    db = 2 * q + s
                    sp.wait_ge(gated, c * DB + db + 1)
                    sp.dma_start(yf[:, s], yf_d[ds(c * DB + db + 1, 1)].rearrange("o p t d -> (o p) (t d)")
                                 ).then_inc(y_loaded[s], LOAD)
                    sp.dma_start(yb[:, s], yb_d[ds((NCH - 1) * DB + db + 1 - c * DB, 1)]
                                 .rearrange("o p t d -> (o p) (t d)")).then_inc(y_loaded[s], LOAD)
                    sp.dma_start(z[:, s], z_d[db * P:(db + 1) * P, ds(c * T, T)]).then_inc(y_loaded[s], LOAD)
                if q == 0 and isinstance(c, int) and c == 0:
                    for r in range(KT):
                        sp.dma_start(wout[:, r], wout_d[r]).then_inc(w_loaded, LOAD)

            def project(c, g, q):
                s = q % 2
                sp.wait_ge(o_done, c * KT + q + 1)
                sp.dma_start(x1[:, s], x1T_d[q * P:(q + 1) * P, ds(c * T, T)]).then_inc(x_loaded[s], LOAD)
                sp.wait_ge(o_done, c * KT + q + 3)
                sp.dma_start(out_d[q * P:(q + 1) * P, ds(c * T, T)], o[:, s]).then_inc(o_stored[s], LOAD)

            chunks(sp, prepare, project, loads_first=True)
            for s in range(2):
                sp.wait_ge(o_stored[s], (NCH * KT // 2 + 1) * LOAD)

        @block.gpsimd
        def _(pool):
            nc.gpsimd.memset(zero[:], 0.0).then_inc(const_ready, 1)
            nc.gpsimd.memset(one[:], 1.0).then_inc(const_ready, 1)
            nc.gpsimd.memset(minus[:], -1.0).then_inc(const_ready, 1)

            def prepare(c, g, q):
                for s in range(2):
                    pool.wait_ge(y_loaded[s], c * (KT * 3 * LOAD) + (q + 1) * 3 * LOAD)
                    nc.gpsimd.tensor_tensor(yf[:, s], yf[:, s], yb[:, s], ALU.add).then_inc(summed, 1)

            chunks(pool, prepare, lambda c, g, q: None)

        @block.scalar
        def _(act):
            def prepare(c, g, q):
                for s in range(2):
                    act.wait_ge(y_loaded[s], c * (KT * 3 * LOAD) + (q + 1) * 3 * LOAD)
                    nc.scalar.activation(sz[:, s], z[:, s], ACT.Silu).then_inc(silu_done, 1)

            chunks(act, prepare, lambda c, g, q: None)

        @block.tensor
        def _(pe):
            def prepare(c, g, q):
                for s in range(2):
                    u = 2 * q + s
                    pe.wait_ge(summed, c * DB + u + 1)
                    pe.wait_ge(gated, c * DB + u + 1)
                    for tb in range(TB):
                        last = nc.tensor.matmul(yt_ps[:, s, tb * P:(tb + 1) * P], yf[:, s, tb * P:(tb + 1) * P],
                                                ident[:], is_transpose=True, start=(tb == 0), stop=(tb == TB - 1))
                    last.then_inc(yt_done, 1)

            def project(c, g, q):
                if q == 0:
                    pe.wait_ge(w_loaded, KT * LOAD)
                    pe.wait_ge(gated, c * DB + DB + 2)
                pe.wait_ge(o_read, c * KT + q + 1)
                for b in range(DB):
                    last = nc.tensor.matmul(o_ps[:, q % 2], wout[:, q, b], yg[:, g, b], start=(b == 0),
                                            stop=(b == DB - 1))
                last.then_inc(o_mm, 1)

            chunks(pe, prepare, project)

        @block.vector
        def _(dve):
            dve.sem_inc(gated, 2)
            dve.sem_inc(o_read, 2)
            dve.sem_inc(o_done, 2)
            u32 = mybir.dt.uint32

            def prepare(c, g, q):
                for s in range(2):
                    u = 2 * q + s
                    dve.wait_ge(yt_done, c * DB + u + 1)
                    dve.wait_ge(silu_done, c * DB + u + 1)
                    nc.vector.tensor_tensor(yg[:, g, u], yt_ps[:, s], sz[:, s], ALU.mult).then_inc(gated, 1)

            def project(c, g, q):
                s = q % 2

                def after(step):
                    hold(dve, o_step, c * (KT * STEPS) + (q * STEPS + step), passed)

                dve.wait_ge(const_ready, 3)
                dve.wait_ge(o_mm, c * KT + q + 1)
                dve.wait_ge(o_stored[s], c * (KT // 2 * LOAD) + (q // 2 + 1) * LOAD)
                nc.vector.tensor_copy(o[:, s], o_ps[:, s]).then_inc(o_read, 1)
                dve.wait_ge(o_read, c * KT + q + 3)
                nc.vector.tensor_tensor(test[:, s], o[:, s], o[:, s], ALU.not_equal).then_inc(o_step, 1)
                after(1)
                nc.vector.copy_predicated(o[:, s], test[:, s].bitcast(u32), zero[:]).then_inc(o_step, 1)
                for step, (op, bound, value) in ((2, (ALU.is_gt, FMAX, one)), (4, (ALU.is_lt, -FMAX, minus))):
                    dve.wait_ge(o_step, c * (KT * STEPS) + (q * STEPS + step))
                    nc.vector.tensor_scalar(test[:, s], o[:, s], bound, None, op).then_inc(o_step, 1)
                    after(step + 1)
                    nc.vector.copy_predicated(o[:, s], test[:, s].bitcast(u32), value[:]).then_inc(o_step, 1)
                dve.wait_ge(o_step, c * (KT * STEPS) + (q * STEPS + STEPS))
                dve.wait_ge(x_loaded[s], c * (KT // 2 * LOAD) + (q // 2 + 1) * LOAD)
                nc.vector.tensor_tensor(o[:, s], o[:, s], x1[:, s], ALU.add).then_inc(o_done, 1)

            chunks(dve, prepare, project)


def metaformer(nc, x, dt_w, dt_b, log_a, ln_w, ln_b, winx, winz, wout, wx, wdt, convp, par, skip, out):
    def scratch(name, shape):
        return nc.dram_tensor(name, shape, F32).ap()

    hnT, x1T = scratch("hnT", (C, HW)), scratch("x1T", (C, HW))
    x_pad, z = scratch("x_pad", (DI, HALO + HW + HALO)), scratch("z", (DI, HW))
    xc = scratch("xc", (NCH * DB, P, T))
    bc = scratch("bc", (NCH, 2 * NS, T))
    states = [scratch(f"state{d}", ((NCH + 1) * DB, P, NS)) for d in range(2)]
    yT = [scratch(f"yT{d}", (NCH * DB + 1, P, TB, P)) for d in range(2)]
    with Scope(nc, "all") as top:
        ident = top.sb("ident", [P, P])
        with Scope(nc, "norm") as sc:
            xn = sc.sb("xn", [P, NT * C])
            mv = sc.sb("mv", [P, NT * 2])
            mean_w = sc.sb("mean_w", [P, P])
            rstd2 = sc.sb("rstd2", [P, C])
            with Scope(nc, "mean") as ms:
                mean_ps = ms.ps("mean_ps", [P, C])
                stage_channel_norm(nc, xn, ident, mean_w, mean_ps, x)
                stage_pixel_variance(nc, xn, mean_w, mean_ps, rstd2)
            stage_channel_scan(nc, xn, ident, rstd2, mv, x, ln_w, ln_b, dt_w, dt_b, log_a)
            stage_token_norm(nc, xn, ident, mv, hnT, x1T, x_pad, states)
        for rev in (True, False):
            d = int(rev)
            stage_scan(nc, rev, ident, hnT, winx, winz, wx[d], wdt[d], convp[d], par[d], skip[d], x_pad, xc, z, bc,
                       states[d], yT[d])
        stage_out(nc, ident, yT[0], yT[1], z, wout, x1T, out)


def kernel(**inputs):
    import numpy as np
    import concourse.bacc as bacc
    from concourse.bass_utils import run_bass_kernel_spmd

    g = {n: np.asarray(a) for n, a in inputs.items()}

    def tiles(a, n):
        return a.reshape(n, P, a.shape[1] // P, P).transpose(0, 3, 2, 1)

    def per_block(*cols):
        return np.concatenate([c.reshape(DB, P, -1) for c in cols], axis=2)

    win = g["L0_ffn_in_proj_w"]
    arrays = {
        "x": g["x"].reshape(C, HW),
        "dt_w": np.concatenate([g["L0_conv_dt_w"].reshape(ROW, 1)] * 2),
        "dt_b": np.broadcast_to(g["L0_conv_dt_b"].reshape(1, 1), (P, 1)),
        "log_a": np.repeat(g["L0_conv_log_A"].reshape(NT, 2).T, ROW, axis=0),
        "ln_w": g["L0_conv_ln_w"].reshape(NT, P).T,
        "ln_b": g["L0_conv_ln_b"].reshape(NT, P).T,
        "winx": tiles(win[:DI], DB),
        "winz": tiles(win[DI:], DB),
        "wout": tiles(g["L0_ffn_out_proj_w"], KT),
    }
    for d, b in enumerate(("", "b_")):
        arrays[f"wx{d}"] = g[f"L0_ffn_x_proj_{b}w"].T.reshape(DB, P, XO)
        arrays[f"wdt{d}"] = g[f"L0_ffn_dt_proj_{b}w"].reshape(DB, P, R).transpose(0, 2, 1)
        arrays[f"convp{d}"] = per_block(g[f"L0_ffn_conv1d_{b}w"], g[f"L0_ffn_conv1d_{b}bias"])
        arrays[f"par{d}"] = per_block(g[f"L0_ffn_dt_proj_{b}bias"], g["L0_ffn_A_b_log" if d else "L0_ffn_A_log"])
        arrays[f"skip{d}"] = per_block(g["L0_ffn_D_b" if d else "L0_ffn_D"])
    arrays = {n: np.ascontiguousarray(a) for n, a in arrays.items()}

    nc = bacc.Bacc("TRN2", target_bir_lowering=False, num_devices=1)
    ap = {n: nc.dram_tensor(n, a.shape, F32, kind="ExternalInput").ap() for n, a in arrays.items()}
    out = nc.dram_tensor("out", (C, HW), F32, kind="ExternalOutput").ap()
    both = {n: [ap[f"{n}0"], ap[f"{n}1"]] for n in ("wx", "wdt", "convp", "par", "skip")}
    metaformer(nc, ap["x"], ap["dt_w"], ap["dt_b"], ap["log_a"], ap["ln_w"], ap["ln_b"], ap["winx"], ap["winz"],
               ap["wout"], both["wx"], both["wdt"], both["convp"], both["par"], both["skip"], out)
    r = run_bass_kernel_spmd(nc, [arrays], core_ids=[0])
    return r.results[0]["out"].reshape(1, C, 64, 64)
```

```python
from contextlib import ExitStack

import concourse.bass as bass
from concourse import mybir

F32 = mybir.dt.float32
ALU = mybir.AluOpType
ACT = mybir.ActivationFunctionType

P = 128
C = 1024
HW = 4096
ROW = 64
NT = HW // P
KT = C // P
DI = 2048
DB = DI // P
NS = 16
R = 64
XO = R + 2 * NS
T = 512
NCH = HW // T
TB = T // P
TAPS = 4
HALO = TAPS - 1
G = 4
NG = NS // G
NOUT = 8
NW = 4
EPS_C, EPS_HW, EPS_T = 1e-6, 1e-5, 1e-5
FMAX = 3.4028234663852886e38
LOAD = 16


def ds(start, n):
    return bass.ds(start, n)


def hold(eng, sem, value, passed):
    eng.wait_ge(sem, value)
    eng.sem_inc(passed, 1)


class Scope:

    def __init__(self, nc, stage):
        self.nc, self.stage, self.stack = nc, stage, ExitStack()

    def __enter__(self):
        self.stack.__enter__()
        return self

    def __exit__(self, *a):
        return self.stack.__exit__(*a)

    def sb(self, name, shape):
        return self.stack.enter_context(self.nc.sbuf_tensor(f"{self.stage}_{name}", shape, F32))

    def ps(self, name, shape):
        return self.stack.enter_context(self.nc.psum_tensor(f"{self.stage}_{name}", shape, F32))

    def sem(self, name):
        return self.stack.enter_context(self.nc.semaphore(f"{self.stage}_{name}"))

    def block(self):
        return self.stack.enter_context(self.nc.Block())


def stage_channel_norm(nc, passed, xn, ident, mean_w, mean_ps, x_d):
    NX = 3
    FULL, LEFT = NT // NX, NT % NX
    with Scope(nc, "n1") as sc:
        xin = sc.sb("xin", [P, NX, KT, P])
        zero = sc.sb("zero", [P, 512])
        stats = sc.sb("stats", [P, NX, 2, 6])
        mv = sc.sb("mv", [P, NX, 2])
        std = sc.sb("std", [P, NX])
        rstd = sc.sb("rstd", [P, NX])
        xt = sc.ps("xt", [P, NX, C])
        const_ready, x_loaded = sc.sem("const_ready"), [sc.sem(f"x_loaded{i}") for i in range(NX)]
        transposed, var_ready, std_ready = sc.sem("transposed"), sc.sem("var_ready"), sc.sem("std_ready")
        inverted = sc.sem("inverted")
        chain, normalised = sc.sem("chain"), sc.sem("normalised")
        x_v = x_d.rearrange("(k p) t -> p k t", p=P)
        block = sc.block()

        @block.gpsimd
        def _(pool):
            nc.gpsimd.memset(ident[:], 0.0).then_inc(const_ready, 1)
            pool.wait_ge(const_ready, 1)
            nc.gpsimd.affine_select(out=ident[:], in_=ident[:], compare_op=ALU.not_equal, fill=1.0, base=0,
                                    pattern=[[-1, P]], channel_multiplier=1).then_inc(const_ready, 1)
            nc.gpsimd.memset(mean_w[:], 1.0 / HW).then_inc(const_ready, 1)
            nc.gpsimd.memset(zero[:], 0.0).then_inc(const_ready, 1)

        @block.sync
        def _(sp):
            for i in range(NX):
                sp.dma_start(xin[:, i], x_v[:, :, i * P:(i + 1) * P]).then_inc(x_loaded[i], LOAD)

            def reload(j, i):
                sp.wait_ge(transposed, j * NX + i + 1)
                sp.dma_start(xin[:, i], x_v[:, :, ds(j * (NX * P) + (NX + i) * P, P)]).then_inc(x_loaded[i], LOAD)

            with sp.Fori(0, FULL - 1) as j:
                for i in range(NX):
                    reload(j, i)
            for i in range(LEFT):
                reload(FULL - 1, i)

        @block.tensor
        def _(pe):
            pe.wait_ge(const_ready, 4)
            for h in range(2):
                nc.tensor.matmul(mean_ps[:, h * 512:(h + 1) * 512], zero[:, 0:P], zero[:], start=True, stop=False)
            def transpose(j, i):
                pe.wait_ge(x_loaded[i], (j + 1) * LOAD)
                pe.wait_ge(normalised, j * NX + i + 1)
                for k in range(KT):
                    last = nc.tensor.matmul(xt[:, i, k * P:(k + 1) * P], xin[:, i, k], ident[:], is_transpose=True,
                                            start=(k % 4 == 0), stop=(k % 4 == 3))
                last.then_inc(transposed, 1)

            def add_to_mean(j, i):
                pe.wait_ge(normalised, j * NX + i + NX + 1)
                for h in range(2):
                    nc.tensor.matmul(mean_ps[:, h * 512:(h + 1) * 512], mean_w[:],
                                     xn[:, ds(j * (NX * C) + i * C + h * 512, 512)], start=False, stop=False)

            transpose(0, 0)
            transpose(0, 1)
            with pe.Fori(0, FULL) as j:
                for i in range(NX):
                    transpose(j + (i + 2) // NX, (i + 2) % NX)
                    add_to_mean(j, i)
            for i in range(LEFT):
                add_to_mean(FULL, i)
            for h in range(2):
                nc.tensor.matmul(mean_ps[:, h * 512:(h + 1) * 512], zero[:, 0:P], zero[:], start=False, stop=True)

        @block.vector
        def _(dve):
            def statistics(j, i):
                dve.wait_ge(transposed, j * NX + i + 1)
                for h in range(2):
                    last = nc.vector.bn_stats(stats[:, i, h], xt[:, i, h * 512:(h + 1) * 512])
                last.then_inc(chain, 1)
                hold(dve, chain, j * (2 * NX) + i * 2 + 1, passed)
                nc.vector.bn_aggr(mv[:, i], stats[:, i].rearrange("p a b -> p (a b)")).then_inc(chain, 1)
                dve.wait_ge(chain, j * (2 * NX) + i * 2 + 2)
                nc.vector.tensor_scalar(mv[:, i, 1:2], mv[:, i, 1:2], EPS_C, None, ALU.add).then_inc(var_ready, 1)

            def normalise(j, i):
                dve.wait_ge(std_ready, j * NX + i + 1)
                nc.vector.reciprocal(rstd[:, i:i + 1], std[:, i:i + 1]).then_inc(inverted, 1)
                dve.wait_ge(inverted, j * NX + i + 1)
                nc.vector.tensor_scalar(xn[:, ds(j * (NX * C) + i * C, C)], xt[:, i], mv[:, i, 0:1],
                                        rstd[:, i:i + 1], ALU.subtract, ALU.mult).then_inc(normalised, 1)

            dve.sem_inc(normalised, NX)
            statistics(0, 0)
            with dve.Fori(0, FULL) as j:
                for i in range(NX):
                    statistics(j + (i + 1) // NX, (i + 1) % NX)
                    normalise(j, i)
            for i in range(LEFT):
                if i + 1 < LEFT:
                    statistics(FULL, i + 1)
                normalise(FULL, i)

        @block.scalar
        def _(act):
            def root(j, i):
                act.wait_ge(var_ready, j * NX + i + 1)
                nc.scalar.activation(std[:, i:i + 1], mv[:, i, 1:2], ACT.Sqrt).then_inc(std_ready, 1)

            with act.Fori(0, FULL) as j:
                for i in range(NX):
                    root(j, i)
            for i in range(LEFT):
                root(FULL, i)


def stage_pixel_variance(nc, xn, mean_w, mean_ps, rstd2):
    with Scope(nc, "n2") as sc:
        sq = sc.sb("sq", [P, 2, C])
        zero = sc.sb("zero", [P, 512])
        var_ps = sc.ps("var_ps", [P, C])
        zero_ready, centred, squared = sc.sem("zero_ready"), sc.sem("centred"), sc.sem("squared")
        summed, var_done, chain = sc.sem("summed"), sc.sem("var_done"), sc.sem("chain")
        block = sc.block()

        @block.gpsimd
        def _(pool):
            nc.gpsimd.memset(zero[:], 0.0).then_inc(zero_ready, 1)

        @block.vector
        def _(dve):
            with dve.Fori(0, NT) as t:
                nc.vector.tensor_tensor(xn[:, ds(t * C, C)], xn[:, ds(t * C, C)], mean_ps[:],
                                        ALU.subtract).then_inc(centred, 1)
            dve.wait_ge(var_done, 1)
            nc.vector.tensor_scalar(rstd2[:], var_ps[:], EPS_HW, None, ALU.add).then_inc(chain, 1)
            dve.wait_ge(chain, 2)
            nc.vector.reciprocal(rstd2[:], rstd2[:]).then_inc(chain, 1)

        @block.scalar
        def _(act):
            with act.Fori(0, NT // 2) as j:
                for s in range(2):
                    act.wait_ge(zero_ready, 1)
                    act.wait_ge(summed, j * 2 + s + 1)
                    act.wait_ge(centred, j * 2 + s + 1)
                    nc.scalar.activation(sq[:, s], xn[:, ds(j * (2 * C) + s * C, C)], ACT.Square).then_inc(squared, 1)
            act.wait_ge(chain, 1)
            nc.scalar.activation(rstd2[:], rstd2[:], ACT.Sqrt).then_inc(chain, 1)

        @block.tensor
        def _(pe):
            pe.sem_inc(summed, 2)
            pe.wait_ge(zero_ready, 1)
            for h in range(2):
                nc.tensor.matmul(var_ps[:, h * 512:(h + 1) * 512], zero[:, 0:P], zero[:], start=True, stop=False)
            with pe.Fori(0, NT // 2) as j:
                for s in range(2):
                    pe.wait_ge(squared, j * 2 + s + 1)
                    for h in range(2):
                        last = nc.tensor.matmul(var_ps[:, h * 512:(h + 1) * 512], mean_w[:],
                                                sq[:, s, h * 512:(h + 1) * 512], start=False, stop=False)
                    last.then_inc(summed, 1)
            for h in range(2):
                last = nc.tensor.matmul(var_ps[:, h * 512:(h + 1) * 512], zero[:, 0:P], zero[:], start=False, stop=True)
            last.then_inc(var_done, 1)


def stage_channel_scan(nc, passed, xn, ident, rstd2, mv, x_d, lnw_d, lnb_d, dtw_d, dtb_d, loga_d):
    with Scope(nc, "n3") as sc:
        lnw, lnb, aneg = sc.sb("lnw", [P, NT]), sc.sb("lnb", [P, NT]), sc.sb("aneg", [P, NT])
        dtw, dtb, row_w = sc.sb("dtw", [P, 1]), sc.sb("dtb", [P, 1]), sc.sb("row_w", [P, P])
        xin = sc.sb("xin", [P, 2, KT, P])
        mag = sc.sb("mag", [P, 2, C])
        sp_ = sc.sb("softplus", [P, 2, C])
        decay = sc.sb("decay", [P, 2, C])
        scanned = sc.sb("scanned", [P, 2, C])
        stats, mv_t = sc.sb("stats", [P, 2, 2, 6]), sc.sb("mv_t", [P, 2, 2])
        dt_ps = sc.ps("dt_ps", [P, 2, C])
        xt = sc.ps("xt", [P, 2, C])
        par_loaded, x_loaded = sc.sem("par_loaded"), [sc.sem("x_loaded0"), sc.sem("x_loaded1")]
        scaled, normed, dt_done = sc.sem("scaled"), sc.sem("normed"), sc.sem("dt_done")
        ab_done, log_done, relu_done = sc.sem("ab_done"), sc.sem("log_done"), sc.sem("relu_done")
        sp_done, decay_done, scan_done = sc.sem("sp_done"), sc.sem("decay_done"), sc.sem("scan_done")
        transposed, added, chain = sc.sem("transposed"), sc.sem("added"), sc.sem("chain")
        achain, setup = sc.sem("achain"), sc.sem("setup")
        x_v = x_d.rearrange("(k p) t -> p k t", p=P)
        block = sc.block()

        @block.sync
        def _(sp):
            for dst, src in ((lnw, lnw_d), (lnb, lnb_d), (aneg, loga_d), (dtw, dtw_d), (dtb, dtb_d)):
                sp.dma_start(dst[:], src).then_inc(par_loaded, LOAD)
            for s in range(2):
                sp.dma_start(xin[:, s], x_v[:, :, s * P:(s + 1) * P]).then_inc(x_loaded[s], LOAD)
            with sp.Fori(0, NT // 2 - 1) as j:
                for s in range(2):
                    sp.wait_ge(transposed, j * 2 + s + 1)
                    sp.dma_start(xin[:, s], x_v[:, :, ds(j * (2 * P) + (2 + s) * P, P)]).then_inc(x_loaded[s], LOAD)

        @block.gpsimd
        def _(pool):
            with pool.Fori(0, NT) as t:
                nc.gpsimd.tensor_tensor(xn[:, ds(t * C, C)], xn[:, ds(t * C, C)], rstd2[:],
                                        ALU.mult).then_inc(scaled, 1)

        @block.vector
        def _(dve):
            nc.vector.memset(row_w[:], 0.0).then_inc(setup, 1)
            dve.wait_ge(setup, 1)
            for r in range(2):
                nc.vector.memset(row_w[r * ROW:(r + 1) * ROW, r * ROW:(r + 1) * ROW], 1.0).then_inc(setup, 1)
            dve.wait_ge(par_loaded, 5 * LOAD)
            dve.wait_ge(setup, 3)
            nc.vector.tensor_scalar(row_w[:], row_w[:], dtw[:], None, ALU.mult).then_inc(setup, 1)
            dve.sem_inc(added, 2)

            def affine(j):
                for s in range(2):
                    dve.wait_ge(scaled, j * 2 + s + 1)
                    nc.vector.tensor_scalar(xn[:, ds(j * (2 * C) + s * C, C)], xn[:, ds(j * (2 * C) + s * C, C)],
                                            lnw[:, ds(j * 2 + s, 1)], lnb[:, ds(j * 2 + s, 1)],
                                            ALU.mult, ALU.add).then_inc(normed, 1)

            def relu(j):
                for s in range(2):
                    dve.wait_ge(dt_done, j * 2 + s + 1)
                    dve.wait_ge(decay_done, j * 2 + s + 1)
                    nc.vector.tensor_scalar(sp_[:, s], dt_ps[:, s], dtb[:], 0.0, ALU.add,
                                            ALU.max).then_inc(relu_done, 1)

            def add_log(j):
                for s in range(2):
                    dve.wait_ge(log_done, j * 2 + s + 1)
                    dve.wait_ge(relu_done, j * 2 + s + 1)
                    nc.vector.tensor_tensor(sp_[:, s], sp_[:, s], mag[:, s], ALU.add).then_inc(sp_done, 1)

            def scan(j):
                for s in range(2):
                    dve.wait_ge(decay_done, j * 2 + s + 3)
                    dve.wait_ge(added, j * 2 + s + 1)
                    nc.vector.tensor_tensor_scan(scanned[:, s], decay[:, s], xn[:, ds(j * (2 * C) + s * C, C)], 0.0,
                                                 ALU.mult, ALU.add).then_inc(scan_done, 1)
                for s in range(2):
                    dve.wait_ge(scan_done, j * 2 + s + 3)
                    dve.wait_ge(transposed, j * 2 + s + 1)
                    nc.vector.tensor_tensor(xn[:, ds(j * (2 * C) + s * C, C)], scanned[:, s], xt[:, s],
                                            ALU.add).then_inc(added, 1)
                for s in range(2):
                    hold(dve, added, j * 2 + s + 3, passed)
                    for h in range(2):
                        last = nc.vector.bn_stats(stats[:, s, h], xn[:, ds(j * (2 * C) + s * C + h * 512, 512)])
                    last.then_inc(chain, 1)
                for s in range(2):
                    hold(dve, chain, j * 6 + s + 1, passed)
                    nc.vector.bn_aggr(mv_t[:, s], stats[:, s].rearrange("p a b -> p (a b)")).then_inc(chain, 1)
                for s in range(2):
                    dve.wait_ge(chain, j * 6 + s + 3)
                    nc.vector.tensor_copy(mv[:, ds(j * 4 + s * 2, 2)], mv_t[:, s]).then_inc(chain, 1)

            def step(j, before=True, after=True):
                if after:
                    affine(j + 1)
                relu(j)
                if before:
                    scan(j - 1)
                add_log(j)

            affine(0)
            step(0, before=False)
            with dve.Fori(0, NT // 2 - 2) as i:
                step(i + 1)
            step(NT // 2 - 1, after=False)
            scan(NT // 2 - 1)

        @block.scalar
        def _(act):
            act.wait_ge(par_loaded, 5 * LOAD)
            nc.scalar.activation(aneg[:], aneg[:], ACT.Exp).then_inc(achain, 1)
            act.wait_ge(achain, 1)
            nc.scalar.mul(aneg[:], aneg[:], -1.0).then_inc(achain, 1)
            act.wait_ge(achain, 2)
            act.sem_inc(decay_done, 2)
            act.sem_inc(scan_done, 2)
            with act.Fori(0, NT // 2) as j:
                for s in range(2):
                    act.wait_ge(relu_done, j * 2 + s + 1)
                    nc.scalar.activation(mag[:, s], dt_ps[:, s], ACT.Abs, bias=dtb[:]).then_inc(ab_done, 1)
                for s in range(2):
                    act.wait_ge(ab_done, j * 4 + s + 1)
                    nc.scalar.activation(mag[:, s], mag[:, s], ACT.Exp, scale=-1.0).then_inc(ab_done, 1)
                for s in range(2):
                    act.wait_ge(ab_done, j * 4 + s + 3)
                    nc.scalar.activation(mag[:, s], mag[:, s], ACT.Ln, bias=1.0).then_inc(log_done, 1)
                for s in range(2):
                    act.wait_ge(par_loaded, 5 * LOAD)
                    act.wait_ge(sp_done, j * 2 + s + 1)
                    act.wait_ge(scan_done, j * 2 + s + 1)
                    nc.scalar.activation(decay[:, s], sp_[:, s], ACT.Exp,
                                         scale=aneg[:, ds(j * 2 + s, 1)]).then_inc(decay_done, 1)

        @block.tensor
        def _(pe):
            def dt_rows(j, ahead):
                for s in range(2):
                    pe.wait_ge(normed, j * 2 + s + 1)
                    if ahead:
                        pe.wait_ge(ab_done, j * 4 - 4 + s + 1)
                    for h in range(2):
                        last = nc.tensor.matmul(dt_ps[:, s, h * 512:(h + 1) * 512], row_w[:],
                                                xn[:, ds(j * (2 * C) + s * C + h * 512, 512)], start=True, stop=True)
                    last.then_inc(dt_done, 1)

            def transpose(j):
                for s in range(2):
                    pe.wait_ge(x_loaded[s], (j + 1) * LOAD)
                    pe.wait_ge(added, j * 2 + s + 1)
                    for k in range(KT):
                        last = nc.tensor.matmul(xt[:, s, k * P:(k + 1) * P], xin[:, s, k], ident[:], is_transpose=True,
                                                start=(k % 4 == 0), stop=(k % 4 == 3))
                    last.then_inc(transposed, 1)

            pe.wait_ge(setup, 4)
            dt_rows(0, False)
            with pe.Fori(0, NT // 2 - 1) as j:
                dt_rows(j + 1, True)
                transpose(j)
            transpose(NT // 2 - 1)


def stage_token_norm(nc, xn, ident, mv, hnT_d, x1T_d, x_pad_d, state_ds):
    with Scope(nc, "n4") as sc:
        rstd, nmr = sc.sb("rstd", [P, NT]), sc.sb("nmr", [P, NT])
        hn, xs = sc.sb("hn", [P, 2, C]), sc.sb("xs", [P, 2, C])
        hn_out, x_out = sc.sb("hn_out", [P, 2, C]), sc.sb("x_out", [P, 2, C])
        zero = sc.sb("zero", [P, DB * NS])
        hn_ps, x_ps = sc.ps("hn_ps", [P, 2, C]), sc.ps("x_ps", [P, 2, C])
        zero_ready, zero_stored = sc.sem("zero_ready"), sc.sem("zero_stored")
        chain, stats_ready = sc.sem("chain"), sc.sem("stats_ready")
        normed, hn_t, x_t, x_moved = sc.sem("normed"), sc.sem("hn_t"), sc.sem("x_t"), sc.sem("x_moved")
        hn_copied, x_copied = sc.sem("hn_copied"), sc.sem("x_copied")
        hn_stored = [sc.sem("hn_stored0"), sc.sem("hn_stored1")]
        x_stored = [sc.sem("x_stored0"), sc.sem("x_stored1")]
        mv3 = mv[:].rearrange("p (t c) -> p t c", c=2)
        hn_v = hnT_d.rearrange("(k p) t -> p k t", p=P)
        x1_v = x1T_d.rearrange("(k p) t -> p k t", p=P)
        block = sc.block()

        @block.gpsimd
        def _(pool):
            nc.gpsimd.memset(zero[:], 0.0).then_inc(zero_ready, 1)
            with pool.Fori(0, NT // 2) as j:
                for s in range(2):
                    pool.wait_ge(x_t, j * 2 + s + 1)
                    nc.gpsimd.tensor_copy(xs[:, s], xn[:, ds(j * (2 * C) + s * C, C)]).then_inc(x_moved, 1)

        @block.vector
        def _(dve):
            dve.sem_inc(x_copied, 2)
            nc.vector.tensor_scalar(rstd[:], mv3[:, :, 1], EPS_T, None, ALU.add).then_inc(chain, 1)
            dve.wait_ge(chain, 2)
            nc.vector.reciprocal(rstd[:], rstd[:]).then_inc(chain, 1)
            dve.wait_ge(chain, 3)
            nc.vector.scalar_tensor_tensor(nmr[:], mv3[:, :, 0], -1.0, rstd[:], ALU.mult,
                                           ALU.mult).then_inc(stats_ready, 1)
            with dve.Fori(0, NT // 2) as j:
                for s in range(2):
                    dve.wait_ge(x_t, j * 2 + s + 3)
                    dve.wait_ge(x_stored[s], (j + 1) * LOAD)
                    nc.vector.tensor_copy(x_out[:, s], x_ps[:, s]).then_inc(x_copied, 1)

        @block.scalar
        def _(act):
            act.sem_inc(hn_copied, 2)
            act.wait_ge(chain, 1)
            nc.scalar.activation(rstd[:], rstd[:], ACT.Sqrt).then_inc(chain, 1)
            with act.Fori(0, NT // 2) as j:
                for s in range(2):
                    act.wait_ge(stats_ready, 1)
                    act.wait_ge(hn_t, j * 2 + s + 1)
                    nc.scalar.activation(hn[:, s], xn[:, ds(j * (2 * C) + s * C, C)], ACT.Identity,
                                         bias=nmr[:, ds(j * 2 + s, 1)],
                                         scale=rstd[:, ds(j * 2 + s, 1)]).then_inc(normed, 1)
                for s in range(2):
                    act.wait_ge(hn_t, j * 2 + s + 3)
                    act.wait_ge(hn_stored[s], (j + 1) * LOAD)
                    nc.scalar.activation(hn_out[:, s], hn_ps[:, s], ACT.Copy).then_inc(hn_copied, 1)

        @block.tensor
        def _(pe):
            pe.sem_inc(hn_t, 2)
            pe.sem_inc(x_t, 2)
            with pe.Fori(0, NT // 2) as j:
                for s in range(2):
                    pe.wait_ge(x_moved, j * 2 + s + 1)
                    pe.wait_ge(x_copied, j * 2 + s + 1)
                    for k in range(KT):
                        last = nc.tensor.matmul(x_ps[:, s, k * P:(k + 1) * P], xs[:, s, k * P:(k + 1) * P], ident[:],
                                                is_transpose=True, start=(k % 4 == 0), stop=(k % 4 == 3))
                    last.then_inc(x_t, 1)
                    pe.wait_ge(normed, j * 2 + s + 1)
                    pe.wait_ge(hn_copied, j * 2 + s + 1)
                    for k in range(KT):
                        last = nc.tensor.matmul(hn_ps[:, s, k * P:(k + 1) * P], hn[:, s, k * P:(k + 1) * P], ident[:],
                                                is_transpose=True, start=(k % 4 == 0), stop=(k % 4 == 3))
                    last.then_inc(hn_t, 1)

        @block.sync
        def _(sp):
            for s in range(2):
                sp.sem_inc(hn_stored[s], LOAD)
                sp.sem_inc(x_stored[s], LOAD)
            sp.wait_ge(zero_ready, 1)
            for side in (0, HALO + HW):
                sp.dma_start(x_pad_d[:, side:side + HALO].rearrange("(b p) t -> p b t", p=P),
                             zero[:, 0:DB * HALO].rearrange("p (b t) -> p b t", t=HALO)).then_inc(zero_stored, LOAD)
            for state_d in state_ds:
                sp.dma_start(state_d[0:DB].rearrange("u p n -> p u n"),
                             zero[:].rearrange("p (u n) -> p u n", n=NS)).then_inc(zero_stored, LOAD)
            with sp.Fori(0, NT // 2) as j:
                for s in range(2):
                    sp.wait_ge(x_copied, j * 2 + s + 3)
                    sp.dma_start(x1_v[:, :, ds(j * (2 * P) + s * P, P)],
                                 x_out[:, s].rearrange("p (k t) -> p k t", t=P)).then_inc(x_stored[s], LOAD)
                    sp.wait_ge(hn_copied, j * 2 + s + 3)
                    sp.dma_start(hn_v[:, :, ds(j * (2 * P) + s * P, P)],
                                 hn_out[:, s].rearrange("p (k t) -> p k t", t=P)).then_inc(hn_stored[s], LOAD)
            sp.wait_ge(zero_stored, 4 * LOAD)
            for s in range(2):
                sp.wait_ge(x_stored[s], (NT // 2 + 1) * LOAD)
                sp.wait_ge(hn_stored[s], (NT // 2 + 1) * LOAD)


def stage_scan(nc, rev, ident, hnT_d, win_d, wx_d, wdt_d, convp_d, par_d, skip_d,
               x_pad_d, xc_d, z_d, bc_d, state_d, yT_d):
    name = "bwd" if rev else "fwd"
    first = rev
    with Scope(nc, name) as sc:
        hn = sc.sb("hn", [P, KT, T])
        win = sc.sb("win", [P, 2, KT, P])
        diag = sc.sb("diag", [P, 2, TAPS, P])
        wx = sc.sb("wx", [P, 2, XO])
        convp = sc.sb("convp", [P, 2, TAPS + 1])
        x = sc.sb("x", [P, 2, T + HALO])
        xc_out = sc.sb("xc_out", [P, 2, T])
        z_out = sc.sb("z_out", [P, 2, T])
        zero = sc.sb("zero", [P, T])
        proj = sc.sb("proj", [XO, T])
        bcast_b, bcast_c = sc.sb("bcast_b", [P, NS, T]), sc.sb("bcast_c", [P, NS, T])
        par, skip = sc.sb("par", [P, 2, 1 + NS]), sc.sb("skip", [P, 2, 1])
        wdt = sc.sb("wdt", [R, 2, P])
        xc = sc.sb("xc", [P, 2, T])
        state_in, state_out = sc.sb("state_in", [P, 2, NS]), sc.sb("state_out", [P, 2, NS])
        aneg = sc.sb("aneg", [P, 2, NS])
        v = sc.sb("v", [P, T])
        mag = sc.sb("mag", [P, T])
        delta, u, du, ud = (sc.sb(n, [P, 2, T]) for n in ("delta", "u", "du", "ud"))
        w = sc.sb("w", [P, NW, G, T])
        hc = sc.sb("hc", [P, NOUT, T])
        y_out = sc.sb("y_out", [P, 2, TB, P])
        da = sc.ps("da", [P, 2, T])
        da_extra = sc.sb("da_extra", [P, 2, T])
        h = sc.ps("h", [P, 3, T])
        yT = sc.ps("yT", [P, TB, P])
        proj_ps = sc.ps("proj_ps", [P, T])
        misc = sc.ps("misc", [P, T])

        names = ("setup", "hn_loaded", "diag_done", "in_mm", "in_copied", "conv_mm", "xc_copied", "proj_mm",
                 "proj_closed", "proj_copied", "bc_stored", "dt_mm", "dt_read", "v_done", "abs_exp", "ln_done",
                 "aneg_step", "pre_step", "du_done", "ud_done", "exp_done", "w_done", "scan_done", "hc_done", "h_saved",
                 "h_saved_dve", "hc_used", "yT_copied", "stored", "passed")
        S = {n: sc.sem(n) for n in names}
        b_loaded, c_loaded = [sc.sem(f"b_loaded{g}") for g in range(NG)], [sc.sem(f"c_loaded{g}") for g in range(NG)]
        a_in, p_in, b_in, win_in = ([sc.sem(f"{n}{s}") for s in range(2)] for n in ("a_in", "p_in", "b_in", "win_in"))
        NA = 3
        NPL = 3
        NB = 2
        SCR = 4 * NW - 3

        def t0(k):
            return (NCH - 1) * T - k * T if rev else k * T

        def col(k):
            return t0(k) + HALO

        def flip(ap):
            return ap[:, ::-1] if rev else ap

        last_col = 0 if rev else T - 1
        EXTRA = {8: 0, 9: 1, 15: 0, 0: 1}

        def da_slot(n):
            return da_extra[:, EXTRA[n]] if n in EXTRA else da[:, (n - 1) % 2]

        def da_before(n):
            return {0: -7, 1: -3, 2: -2, 8: -1, 9: 0, 10: 6, 11: 7, 15: 8}.get(n, n - 2)

        x_at = 0 if rev else HALO
        tap_at = [HALO - k if rev else k for k in range(TAPS)]

        def chunks(eng, pair, between, prologue):
            prologue()
            with eng.Fori(0, DB // 2) as j:
                pair(eng, j, j, a=True, b=False)
            between()
            with eng.Fori(0, NCH - 1) as k:
                with eng.Fori(0, DB // 2 - 1) as j:
                    pair(eng, k * (DB // 2) + j, j, a=True, b=True, k=k)
                pair(eng, k * (DB // 2) + DB // 2 - 1, DB // 2 - 1, a=True, b=True, k=k, end=True)
            with eng.Fori(0, DB // 2 - 1) as j:
                pair(eng, (NCH - 1) * (DB // 2) + j, j, a=False, b=True, k=NCH - 1)
            pair(eng, NCH * (DB // 2) - 1, DB // 2 - 1, a=False, b=True, k=NCH - 1, end=True)

        def a_pair(m, b):
            return m + DB // 2 if b else m

        LATE = 5
        IN, IN2, CONV, PROJ = 2, 7, 9, 15

        stores = {(True, False): (2 if first else 1), (True, True): 4, (False, True): (2 if first else 3)}
        base = {(True, False): 0, (True, True): DB * stores[True, False],
                (False, True): DB * stores[True, False] + DB * (NCH - 1) * stores[True, True]}
        all_stores = base[False, True] + DB * stores[False, True]

        block = sc.block()

        @block.sync
        def _(sp):
            def load_win(s, db):
                sp.dma_start(win[:, s], win_d[ds(db, 1)].rearrange("o p k d -> (o p) k d")).then_inc(win_in[s], LOAD)

            def load_hn(k):
                sp.dma_start(hn[:], hnT_d.rearrange("(k p) t -> p k t", p=P)[:, :, ds(t0(k), T)]
                             ).then_inc(S["hn_loaded"], LOAD)

            def load_a(s, db, k, with_win=True):
                if first and with_win:
                    load_win(s, db)
                if first:
                    halo = x[:, s, T:T + HALO]
                    sp.dma_start(halo, x_pad_d[ds(db * P, P), ds(col(k) + T, HALO)]).then_inc(a_in[s], LOAD)
                else:
                    sp.dma_start(x[:, s], x_pad_d[ds(db * P, P), ds(t0(k), T + HALO)]).then_inc(a_in[s], LOAD)
                sp.dma_start(wx[:, s], wx_d[ds(db, 1)].rearrange("o p k -> (o p) k")).then_inc(a_in[s], LOAD)
                sp.dma_start(convp[:, s], convp_d[ds(db, 1)].rearrange("o p k -> (o p) k")).then_inc(a_in[s], LOAD)

            def load_p(s, u_, db):
                sp.dma_start(wdt[:, s], wdt_d[ds(db, 1)].rearrange("o p k -> (o p) k")).then_inc(p_in[s], LOAD)
                sp.dma_start(par[:, s], par_d[ds(db, 1)].rearrange("o p k -> (o p) k")).then_inc(p_in[s], LOAD)
                sp.dma_start(xc[:, s], xc_d[ds(u_, 1)].rearrange("o p k -> (o p) k")).then_inc(p_in[s], LOAD)

            def load_b(s, u_, db):
                sp.dma_start(skip[:, s], skip_d[ds(db, 1)].rearrange("o p k -> (o p) k")).then_inc(b_in[s], LOAD)
                sp.dma_start(state_in[:, s], state_d[ds(u_, 1)].rearrange("o p k -> (o p) k")).then_inc(b_in[s], LOAD)
                if not first:
                    load_win(s, db)

            def broadcast(k, ub=None, hn_chunk=None):
                hold(sp, S["proj_copied"], k + 1, S["passed"])
                sp.dma_start(bc_d[ds(k, 1)].rearrange("o n t -> (o n) t"), proj[R:XO, :]).then_inc(S["bc_stored"], LOAD)
                hold(sp, S["bc_stored"], k * LOAD + LOAD, S["passed"])
                for c, g in ((0, 0), (0, 1), (1, 0), (0, 2), (1, 1), (0, 3), (1, 2), (1, 3)):
                    if hn_chunk is not None and (c, g) == (0, 2):
                        load_hn(hn_chunk)
                    if ub is not None and c == 0:
                        hold(sp, S["w_done"], ub * NS + g * G + G, S["passed"])
                    elif ub is not None:
                        hold(sp, S["hc_done"], ub * NS + g * G + G + 3, S["passed"])
                    dst, sem = ((bcast_b, b_loaded), (bcast_c, c_loaded))[c]
                    src = bc_d[ds(k, 1)][:, c * NS + g * G:c * NS + (g + 1) * G].rearrange("o n t -> (o n) t")
                    sp.dma_start(dst[:, g * G:(g + 1) * G], src.partition_broadcast(P)).then_inc(sem[g], LOAD)

            def pair(eng, m, j, a, b, k=None, end=False, more=True):
                n = stores[a, b]
                ma = a_pair(m, b)
                ka = 0 if not b else k + 1
                start = base[a, b] + (m * (2 * n) if b and a or not b else (m - (NCH - 1) * (DB // 2)) * (2 * n))
                for s in range(2):
                    if not b and first and not end:
                        hold(sp, S["in_mm"], ma * 2 + s + 1, S["passed"])
                        load_win(s, j * 2 + s + 2)
                for s in range(2):
                    db = j * 2 + s
                    ua, ub = ma * 2 + s, m * 2 + s
                    db2 = s if end else db + 2
                    nxt2 = b and (a or not end)
                    if nxt2:
                        hold(sp, S["pre_step"], ub * 2 + 2, S["passed"])
                        load_p(s, ub + 2, db2)
                    if b:
                        hold(sp, S["yT_copied"], ub + 1, S["passed"])
                        sp.dma_start(yT_d[ds(ub, 1)].rearrange("o p t d -> (o p) t d"),
                                     y_out[:, 1 - s]).then_inc(S["stored"], LOAD)
                    if a:
                        if first:
                            hold(sp, S["in_copied"], ua + 3, S["passed"])
                            sp.dma_start(x_pad_d[ds(db * P, P), ds(col(ka), T)],
                                         x[:, s, x_at:x_at + T]).then_inc(S["stored"], LOAD)
                    if a and b and end and s == 0 and (more or not first):
                        hold(sp, S["in_mm"], (ua if first else ub) + 2, S["passed"])
                        load_hn(k + 2 if first else k + 1)
                    if a:
                        hold(sp, S["xc_copied"], ua + 3, S["passed"])
                        sp.dma_start(xc_d[ds(ua, 1)].rearrange("o p k -> (o p) k"),
                                     xc_out[:, s]).then_inc(S["stored"], LOAD)
                    if a and b and end and s == 1:
                        broadcast(k + 1, ub)
                    if b:
                        if not first:
                            hold(sp, S["in_copied"], ub + 3, S["passed"])
                            sp.dma_start(z_d[ds(db * P, P), ds(t0(k), T)],
                                         z_out[:, s]).then_inc(S["stored"], LOAD)
                        hold(sp, S["h_saved"], m * 26 + s * 13 + 14, S["passed"])
                        hold(sp, S["h_saved_dve"], m * 6 + s * 3 + 6, S["passed"])
                        sp.dma_start(state_d[ds(ub + DB, 1)].rearrange("o p k -> (o p) k"),
                                     state_out[:, s]).then_inc(S["stored"], LOAD)
                    hold(sp, S["stored"], start * LOAD + (s + 1) * n * LOAD, S["passed"])
                    if a:
                        hold(sp, S["proj_mm"], ua + 1, S["passed"])
                    if b:
                        hold(sp, S["exp_done"], ub * NS + NS, S["passed"])
                        hold(sp, S["ud_done"], ub + 2, S["passed"])
                    if nxt2 and a and (more or not end):
                        load_a(s, db2, ka + 1 if end else ka)
                    if nxt2:
                        load_b(s, ub + 2, db2)

            def between():
                for s in range(2):
                    load_p(s, s, s)
                for s in range(2):
                    load_b(s, s, s)
                broadcast(0, hn_chunk=1 if first else 0)
                for s in range(2):
                    load_a(s, s, 1)

            if first:
                load_hn(0)
            for s in range(2):
                load_a(s, s, 0)
            with sp.Fori(0, DB // 2 - 1) as j:
                pair(sp, j, j, a=True, b=False)
                for s in range(2):
                    load_a(s, j * 2 + s + 2, 0, with_win=False)
            pair(sp, DB // 2 - 1, DB // 2 - 1, a=True, b=False, end=True)
            between()
            with sp.Fori(0, NCH - 2) as k:
                with sp.Fori(0, DB // 2 - 1) as j:
                    pair(sp, k * (DB // 2) + j, j, a=True, b=True, k=k)
                pair(sp, k * (DB // 2) + DB // 2 - 1, DB // 2 - 1, a=True, b=True, k=k, end=True)
            for k, a in ((NCH - 2, True), (NCH - 1, False)):
                with sp.Fori(0, DB // 2 - 1) as j:
                    pair(sp, k * (DB // 2) + j, j, a=a, b=True, k=k)
                pair(sp, (k + 1) * (DB // 2) - 1, DB // 2 - 1, a=a, b=True, k=k, end=True, more=False)
            hold(sp, S["yT_copied"], NCH * DB + 1, S["passed"])
            sp.dma_start(yT_d[NCH * DB], y_out[:, 1]).then_inc(S["stored"], LOAD)
            hold(sp, S["stored"], all_stores * LOAD + LOAD, S["passed"])

        @block.tensor
        def _(pe):
            def dt_matmul(s, loads):
                pe.wait_ge(p_in[s], loads)
                nc.tensor.matmul(misc[:], wdt[:, s], proj[0:R, :], start=True, stop=True).then_inc(S["dt_mm"], 1)

            def in_proj(s, ma, m, chunk_loads, i0, i1, bank=misc[:]):
                if i0 == 0:
                    pe.wait_ge(win_in[s], (ma + 1 if first else m + 1) * LOAD)
                    pe.wait_ge(S["hn_loaded"], chunk_loads)
                for i in range(i0, i1):
                    last = nc.tensor.matmul(bank, win[:, s, i], hn[:, i], start=(i == 0), stop=(i == KT - 1))
                if i1 == KT:
                    last.then_inc(S["in_mm"], 1)

            def convolution(s, ma, bank=misc[:]):
                pe.wait_ge(S["diag_done"], ma * 2 + s + 1)
                if first:
                    pe.wait_ge(S["in_copied"], ma * 2 + s + 3)
                else:
                    pe.wait_ge(a_in[s], (ma + 1) * (NA * LOAD))
                for i in range(TAPS):
                    last = nc.tensor.matmul(bank, diag[:, s, i], x[:, s, tap_at[i]:tap_at[i] + T], start=(i == 0),
                                            stop=(i == TAPS - 1))
                last.then_inc(S["conv_mm"], 1)

            def projection(s, ma):
                pe.wait_ge(S["xc_copied"], ma * 2 + s + 3)
                nc.tensor.matmul(proj_ps[0:XO, :], wx[:, s], xc_out[:, s], start=False,
                                 stop=False).then_inc(S["proj_mm"], 1)

            def open_projection():
                nc.tensor.matmul(proj_ps[0:XO, :], zero[:, 0:XO], zero[:], start=True, stop=False)

            def close_projection():
                nc.tensor.matmul(proj_ps[0:XO, :], zero[:, 0:XO], zero[:], start=False,
                                 stop=True).then_inc(S["proj_closed"], 1)

            def pair(eng, m, j, a, b, k=None, end=False):
                ma = a_pair(m, b)
                if not b:
                    for s in range(2):
                        if first:
                            pe.wait_ge(S["in_copied"], ma * 2 + s + 1)
                            in_proj(s, ma, m, LOAD, 0, KT, bank=h[:, s])
                    for s in range(2):
                        pe.wait_ge(S["xc_copied"], ma * 2 + s + 1)
                        convolution(s, ma, bank=da[:, s])
                    for s in range(2):
                        projection(s, ma)
                    return
                for s in range(2):
                    ua, ub = ma * 2 + s, m * 2 + s
                    nxt = a or not (end and s == 1)
                    late = a and end and s == 1
                    hn_loads = (k + 2 if first else k + 1) * LOAD
                    with_in = a or not first
                    own_in = with_in and not (end and s == 1)
                    ahead_in = with_in and end and s == 0
                    for n in range(NS):
                        if nxt and n == (LATE if late else 0):
                            pe.wait_ge(S["dt_read"], ub + 1)
                            if late:
                                pe.wait_ge(S["proj_copied"], k + 2)
                                pe.wait_ge(S["xc_copied"], ua + 3)
                            elif a:
                                pe.wait_ge(S["xc_copied"], ua + 2)
                            elif not first:
                                pe.wait_ge(S["in_copied"], ub + 2)
                            dt_matmul(1 - s, (m + s) * (NPL * LOAD) + NPL * LOAD)
                            if late:
                                open_projection()
                        if own_in and IN <= n < IN + 4:
                            if n == IN:
                                pe.wait_ge(S["dt_read"], ub + 2)
                            in_proj(s, ma, m, hn_loads, 2 * (n - IN), 2 * (n - IN) + 2)
                        if ahead_in and IN2 <= n < IN2 + 4:
                            if n == IN2:
                                pe.wait_ge(S["in_copied"], (ua if first else ub) + 3)
                            in_proj(1, ma, m, hn_loads, 2 * (n - IN2), 2 * (n - IN2) + 2)
                        if a and n == (0 if late else 12 if end else CONV):
                            pe.wait_ge(S["in_copied"], (ua if first else ub) + (4 if end and s == 0 else 3))
                            if late:
                                pe.wait_ge(S["xc_copied"], ua + 2)
                            convolution(s, ma)
                        if a and not end and n == PROJ:
                            projection(s, ma)
                        if late and n == 4:
                            projection(0, ma)
                            projection(1, ma)
                            close_projection()
                        if n == NS - 1:
                            pe.wait_ge(S["ud_done"], ub + 2)
                            for tb in range(TB):
                                nc.tensor.matmul(yT[:, tb], ud[:, s, tb * P:(tb + 1) * P], ident[:],
                                                 is_transpose=True, start=False, stop=False)
                        pe.wait_ge(S["hc_done"], m * 32 + s * 16 + n + 4)
                        if n == 0:
                            pe.wait_ge(S["yT_copied"], ub + 1)
                        for tb in range(TB):
                            last = nc.tensor.matmul(yT[:, tb], hc[:, (s * 16 + n) % NOUT, tb * P:(tb + 1) * P], ident[:],
                                                    is_transpose=True, start=(n == 0 and tb == 0),
                                                    stop=(n == NS - 1 and tb == TB - 1))
                        last.then_inc(S["hc_used"], 1)

            def between():
                close_projection()
                pe.wait_ge(S["proj_copied"], 1)
                dt_matmul(0, NPL * LOAD)
                open_projection()

            def prologue():
                pe.sem_inc(S["hc_used"], NOUT)
                pe.sem_inc(S["conv_mm"], 2)
                pe.wait_ge(S["setup"], 2)
                open_projection()

            chunks(pe, pair, between, prologue)
            close_projection()

        @block.scalar
        def _(act):
            def dt_read(s, b_p1):
                act.wait_ge(S["dt_mm"], b_p1)
                nc.scalar.activation(v[:], misc[:], ACT.Identity, bias=par[:, s, 0:1]).then_inc(S["dt_read"], 1)

            def softplus_tail(s, b_p1, step):
                if step == 0:
                    act.wait_ge(S["v_done"], b_p1)
                    nc.scalar.activation(mag[:], v[:], ACT.Abs, bias=par[:, s, 0:1]).then_inc(S["abs_exp"], 1)
                    nc.scalar.activation(aneg[:, s], par[:, s, 1:1 + NS], ACT.Exp).then_inc(S["aneg_step"], 1)
                elif step == 1:
                    nc.scalar.activation(v[:], v[:], ACT.Relu, bias=par[:, s, 0:1]).then_inc(S["abs_exp"], 1)
                    act.wait_ge(S["abs_exp"], b_p1 * 3 - 1)
                    nc.scalar.activation(mag[:], mag[:], ACT.Exp, scale=-1.0).then_inc(S["abs_exp"], 1)
                    act.wait_ge(S["aneg_step"], b_p1 * 2 - 1)
                    nc.scalar.mul(aneg[:, s], aneg[:, s], -1.0).then_inc(S["aneg_step"], 1)
                elif step == 2:
                    act.wait_ge(S["abs_exp"], b_p1 * 3)
                    nc.scalar.activation(mag[:], mag[:], ACT.Ln, bias=1.0).then_inc(S["ln_done"], 1)

            def in_copy(s, ma, m, bank=misc[:]):
                act.wait_ge(S["in_mm"], (ma if first else m) * 2 + s + 1)
                if first:
                    act.wait_ge(a_in[s], (ma + 1) * (NA * LOAD))
                    out = x[:, s, x_at:x_at + T]
                else:
                    act.wait_ge(b_in[s], (m + 1) * (NB * LOAD))
                    out = z_out[:, s]
                nc.scalar.activation(out, bank, ACT.Copy).then_inc(S["in_copied"], 1)

            def xc_copy(s, ma, bank=misc[:]):
                act.wait_ge(a_in[s], (ma + 1) * (NA * LOAD))
                act.wait_ge(S["conv_mm"], ma * 2 + s + 3)
                nc.scalar.activation(xc_out[:, s], bank, ACT.Identity,
                                     bias=convp[:, s, TAPS:TAPS + 1]).then_inc(S["xc_copied"], 1)

            def proj_copy(chunk):
                act.wait_ge(S["proj_closed"], chunk + 1)
                nc.scalar.activation(proj[:], proj_ps[0:XO, :], ACT.Copy).then_inc(S["proj_copied"], 1)

            def yT_copy(s, b):
                act.wait_ge(S["hc_used"], b * NS + NOUT)
                nc.scalar.activation(y_out[:, s], yT[:], ACT.Copy).then_inc(S["yT_copied"], 1)

            def pair(eng, m, j, a, b, k=None, end=False):
                ma = a_pair(m, b)
                if not b:
                    for s in range(2):
                        if first:
                            in_copy(s, ma, m, h[:, s])
                    for s in range(2):
                        xc_copy(s, ma, da[:, s])
                    return
                for s in range(2):
                    nxt = a or not (end and s == 1)
                    late = a and end and s == 1
                    with_in = a or not first
                    ln_steps = (LATE + 5, LATE + 6, LATE + 7) if late else (5, 6, 9)
                    for n in range(NS):
                        act.wait_ge(S["scan_done"], m * 32 + (s * 16 + da_before(n) + 1 + SCR))
                        if n == 0:
                            act.wait_ge(S["pre_step"], m * 4 + s * 2 + 2)
                            act.wait_ge(S["aneg_step"], m * 4 + s * 2 + 2)
                            act.wait_ge(b_in[s], (m + 1) * (NB * LOAD))
                        nc.scalar.activation(da_slot(n), delta[:, s], ACT.Exp,
                                             scale=aneg[:, s, n:n + 1]).then_inc(S["exp_done"], 1)
                        if n >= 3:
                            act.wait_ge(S["hc_done"], m * 32 + s * 16 + n + 1)
                            nc.scalar.activation(state_out[:, s, n - 3:n - 2],
                                                 h[:, (s * 16 + n - 3) % 3, last_col:last_col + 1],
                                                 ACT.Copy).then_inc(S["h_saved"], 1)
                        if n == 2:
                            yT_copy(1 - s, m * 2 + s)
                        if n == 12:
                            nc.scalar.activation(ud[:, s], u[:, s], ACT.Copy,
                                                 scale=skip[:, s]).then_inc(S["ud_done"], 1)
                        if nxt and n == ln_steps[0] - 2:
                            act.wait_ge(p_in[1 - s], (m + s) * (NPL * LOAD) + NPL * LOAD)
                            dt_read(1 - s, m * 2 + s + 2)
                        if nxt and n in ln_steps:
                            softplus_tail(1 - s, m * 2 + s + 2, ln_steps.index(n))
                        if with_in and not (end and s == 1) and n == (8 if end else 10):
                            in_copy(s, ma, m)
                        if with_in and end and s == 0 and n == 13:
                            in_copy(1, ma, m)
                        if a and not end and n == 14:
                            xc_copy(s, ma)
                        if late and n == 0:
                            xc_copy(0, ma)
                        if late and n == 4:
                            xc_copy(1, ma)
                        if late and n == 6:
                            proj_copy(k + 1)

            def between():
                proj_copy(0)
                act.wait_ge(p_in[0], NPL * LOAD)
                dt_read(0, 1)
                for step in range(3):
                    softplus_tail(0, 1, step)

            def prologue():
                act.sem_inc(S["in_copied"], 2)
                act.sem_inc(S["xc_copied"], 2)
                act.sem_inc(S["h_saved"], 1)
                act.sem_inc(S["ud_done"], 1)
                act.wait_ge(S["setup"], 2)

            chunks(act, pair, between, prologue)
            act.wait_ge(S["stored"], all_stores * LOAD)
            yT_copy(1, NCH * DB)

        @block.gpsimd
        def _(pool):
            def diagonal(s, ma):
                pool.wait_ge(a_in[s], (ma + 1) * (NA * LOAD))
                pool.wait_ge(S["conv_mm"], ma * 2 + s + 1)
                nc.gpsimd.tensor_tensor(diag[:, s], ident[:].unsqueeze(1).to_broadcast([P, TAPS, P]),
                                        convp[:, s, 0:TAPS].unsqueeze(2).to_broadcast([P, TAPS, P]),
                                        ALU.mult).then_inc(S["diag_done"], 1)

            def pair(eng, m, j, a, b, k=None, end=False):
                ma = a_pair(m, b)
                for s in range(2):
                    if not b:
                        diagonal(s, ma)
                        continue
                    pool.wait_ge(S["pre_step"], m * 4 + s * 2 + 2)
                    nc.gpsimd.tensor_tensor(du[:, s], delta[:, s], u[:, s], ALU.mult).then_inc(S["du_done"], 1)
                    pool.wait_ge(S["du_done"], m * 2 + s + 1)
                    for g in range(NG):
                        slot = (s * NG + g) % NW
                        pool.wait_ge(b_loaded[g], k * LOAD + LOAD)
                        pool.wait_ge(S["scan_done"], m * 32 + (s * 16 + g * G + G) - NW * G + SCR)
                        if g == 0:
                            for i in range(G):
                                nc.gpsimd.tensor_tensor(w[:, slot, i], du[:, s], bcast_b[:, i],
                                                        ALU.mult).then_inc(S["w_done"], 1)
                        else:
                            nc.gpsimd.tensor_tensor(w[:, slot], du[:, s].unsqueeze(1).to_broadcast([P, G, T]),
                                                    bcast_b[:, g * G:(g + 1) * G], ALU.mult).then_inc(S["w_done"], G)
                        if a and g == 0:
                            diagonal(s, ma)

            nc.gpsimd.memset(zero[:], 0.0).then_inc(S["setup"], 1)
            with pool.Fori(0, DB // 2) as j:
                pair(pool, j, j, a=True, b=False)
            with pool.Fori(0, NCH - 1) as k:
                with pool.Fori(0, DB // 2) as j:
                    pair(pool, k * (DB // 2) + j, j, a=True, b=True, k=k)
            with pool.Fori(0, DB // 2) as j:
                pair(pool, (NCH - 1) * (DB // 2) + j, j, a=False, b=True, k=NCH - 1)

        @block.vector
        def _(dve):
            def clip_step(b_p1):
                dve.wait_ge(S["dt_read"], b_p1)
                nc.vector.tensor_scalar(v[:], v[:], 1e-5, 1.0, ALU.max, ALU.min).then_inc(S["v_done"], 1)

            def delta_step(s, b_p1):
                dve.wait_ge(S["ln_done"], b_p1)
                dve.wait_ge(S["abs_exp"], b_p1 * 3)
                nc.vector.tensor_tensor(delta[:, s], v[:], mag[:], ALU.add).then_inc(S["pre_step"], 1)
                nc.vector.tensor_scalar(u[:, s], xc[:, s], 10.0, -10.0, ALU.min, ALU.max).then_inc(S["pre_step"], 1)

            def saved_by(q, m):
                unit, n = divmod(q, NS)
                if n < NS - 3:
                    dve.wait_ge(S["h_saved"], m * 26 + (unit * 13 + n + 2))
                else:
                    dve.wait_ge(S["h_saved_dve"], m * 6 + (unit * 3 + n - 12 + 3))

            def pair(eng, m, j, a, b, k=None, end=False):
                ma = a_pair(m, b)
                for s in range(2):
                    if not b:
                        continue
                    nxt = a or not (end and s == 1)
                    late = a and end and s == 1
                    clip_at, delta_at = 3 + (LATE - 1 if late else 0), LATE + 8 if late else 10

                    def scan(n):
                        p = s * NS + n
                        dve.wait_ge(S["exp_done"], m * 32 + p + 1)
                        if n < G or n % G == 0:
                            dve.wait_ge(S["w_done"], m * 32 + (s * 16 + (n + 1 if n < G else n + G)))
                        if n == 0:
                            dve.wait_ge(b_in[s], (m + 1) * (NB * LOAD))
                        q = p - 3 if p >= 3 else {0: -2, 1: -1, 2: -3}[p]
                        dve.wait_ge(S["hc_done"], m * 32 + q + 4)
                        saved_by(q, m)
                        nc.vector.tensor_tensor_scan(flip(h[:, p % 3]), flip(da_slot(n)), flip(w[:, (s * NG + n // G) % NW, n % G]),
                                                     state_in[:, s, n:n + 1], ALU.mult,
                                                     ALU.add).then_inc(S["scan_done"], 1)

                    def weigh(n):
                        p = s * NS + n
                        if n % G == 0:
                            dve.wait_ge(c_loaded[n // G], k * LOAD + LOAD)
                        dve.wait_ge(S["scan_done"], m * 32 + p + 1 + SCR)
                        dve.wait_ge(S["hc_used"], m * 32 + p + 1)
                        nc.vector.tensor_tensor(hc[:, p % NOUT], h[:, p % 3], bcast_c[:, n],
                                                ALU.mult).then_inc(S["hc_done"], 1)

                    for n in range(NS):
                        if n == delta_at and nxt:
                            dve.wait_ge(p_in[1 - s], (m + s) * (NPL * LOAD) + NPL * LOAD)
                            dve.wait_ge(S["ud_done"], m * 2 + s + 1)
                            delta_step(1 - s, m * 2 + s + 2)
                        scan(n)
                        if n:
                            weigh(n - 1)
                        if n == clip_at and nxt:
                            clip_step(m * 2 + s + 2)
                    weigh(NS - 1)
                    for n in range(NS - 3, NS):
                        nc.vector.tensor_copy(state_out[:, s, n:n + 1],
                                              h[:, (s * NS + n) % 3, last_col:last_col + 1]
                                              ).then_inc(S["h_saved_dve"], 1)

            def between():
                dve.wait_ge(p_in[0], NPL * LOAD)
                clip_step(1)
                delta_step(0, 1)

            def prologue():
                dve.sem_inc(S["scan_done"], SCR)
                dve.sem_inc(S["hc_done"], 3)
                dve.sem_inc(S["h_saved_dve"], 3)
                nc.vector.memset(yT[:], 0.0).then_inc(S["setup"], 1)

            chunks(dve, pair, between, prologue)


def stage_out(nc, passed, ident, yf_d, yb_d, z_d, wout_d, x1T_d, out_d):
    with Scope(nc, "out") as sc:
        wout = sc.sb("wout", [P, KT, DB, P])
        yg = sc.sb("yg", [P, 2, DB, T])
        yf, yb = sc.sb("yf", [P, 2, T]), sc.sb("yb", [P, 2, T])
        z, sz = sc.sb("z", [P, 2, T]), sc.sb("sz", [P, 2, T])
        x1 = sc.sb("x1", [P, 2, T])
        o, test = sc.sb("o", [P, 2, T]), sc.sb("test", [P, 2, T])
        zero, one, minus = sc.sb("zero", [P, T]), sc.sb("one", [P, T]), sc.sb("minus", [P, T])
        yt_ps, o_ps = sc.ps("yt_ps", [P, 2, T]), sc.ps("o_ps", [P, 2, T])
        w_loaded, const_ready = sc.sem("w_loaded"), sc.sem("const_ready")
        y_loaded, x_loaded = [sc.sem(f"y_loaded{s}") for s in range(2)], [sc.sem(f"x_loaded{s}") for s in range(2)]
        o_stored = [sc.sem(f"o_stored{s}") for s in range(2)]
        summed, silu_done, yt_done, gated = sc.sem("summed"), sc.sem("silu_done"), sc.sem("yt_done"), sc.sem("gated")
        o_mm, o_read, o_step, o_done = sc.sem("o_mm"), sc.sem("o_read"), sc.sem("o_step"), sc.sem("o_done")
        STEPS = 6
        block = sc.block()

        def chunks(eng, prepare, project, ahead=0):
            def step(c, g, q):
                q2 = q + ahead
                if q2 < KT:
                    prepare(c + 1, 1 - g, q2)
                elif not (isinstance(c, int) and c + 2 == NCH):
                    prepare(c + 2, g, q2 - KT)
                project(c, g, q)

            for q in range(KT):
                prepare(0, 0, q)
            for q in range(ahead):
                prepare(1, 1, q)
            with eng.Fori(0, NCH // 2 - 1) as i:
                for g in range(2):
                    for q in range(KT):
                        step(i * 2 + g, g, q)
            for q in range(KT):
                step(NCH - 2, 0, q)
            for q in range(KT):
                project(NCH - 1, 1, q)

        @block.sync
        def _(sp):
            sp.sem_inc(o_stored[0], LOAD)
            sp.sem_inc(o_stored[1], LOAD)

            def prepare(c, g, q):
                for s in range(2):
                    db = 2 * q + s
                    hold(sp, gated, c * DB + db + 1, passed)
                    sp.dma_start(yf[:, s], yf_d[ds(c * DB + db + 1, 1)].rearrange("o p t d -> (o p) (t d)")
                                 ).then_inc(y_loaded[s], LOAD)
                    sp.dma_start(yb[:, s], yb_d[ds((NCH - 1) * DB + db + 1 - c * DB, 1)]
                                 .rearrange("o p t d -> (o p) (t d)")).then_inc(y_loaded[s], LOAD)
                    sp.dma_start(z[:, s], z_d[db * P:(db + 1) * P, ds(c * T, T)]).then_inc(y_loaded[s], LOAD)
                if isinstance(c, int) and c == 0:
                    sp.dma_start(wout[:, q], wout_d[q]).then_inc(w_loaded, LOAD)

            def project(c, g, q):
                s = q % 2
                hold(sp, o_done, c * KT + q + 1, passed)
                sp.dma_start(x1[:, s], x1T_d[q * P:(q + 1) * P, ds(c * T, T)]).then_inc(x_loaded[s], LOAD)
                hold(sp, o_done, c * KT + q + 3, passed)
                sp.dma_start(out_d[q * P:(q + 1) * P, ds(c * T, T)], o[:, s]).then_inc(o_stored[s], LOAD)

            chunks(sp, prepare, project, ahead=1)
            for s in range(2):
                sp.wait_ge(o_stored[s], (NCH * KT // 2 + 1) * LOAD)

        @block.gpsimd
        def _(pool):
            nc.gpsimd.memset(zero[:], 0.0).then_inc(const_ready, 1)
            nc.gpsimd.memset(one[:], 1.0).then_inc(const_ready, 1)
            nc.gpsimd.memset(minus[:], -1.0).then_inc(const_ready, 1)

            def prepare(c, g, q):
                for s in range(2):
                    pool.wait_ge(y_loaded[s], c * (KT * 3 * LOAD) + (q + 1) * 3 * LOAD)
                    nc.gpsimd.tensor_tensor(yf[:, s], yf[:, s], yb[:, s], ALU.add).then_inc(summed, 1)

            chunks(pool, prepare, lambda c, g, q: None)

        @block.scalar
        def _(act):
            def prepare(c, g, q):
                for s in range(2):
                    act.wait_ge(y_loaded[s], c * (KT * 3 * LOAD) + (q + 1) * 3 * LOAD)
                    nc.scalar.activation(sz[:, s], z[:, s], ACT.Silu).then_inc(silu_done, 1)

            chunks(act, prepare, lambda c, g, q: None)

        @block.tensor
        def _(pe):
            def prepare(c, g, q):
                for s in range(2):
                    u = 2 * q + s
                    pe.wait_ge(summed, c * DB + u + 1)
                    pe.wait_ge(gated, c * DB + u + 1)
                    for tb in range(TB):
                        last = nc.tensor.matmul(yt_ps[:, s, tb * P:(tb + 1) * P], yf[:, s, tb * P:(tb + 1) * P],
                                                ident[:], is_transpose=True, start=(tb == 0), stop=(tb == TB - 1))
                    last.then_inc(yt_done, 1)

            def project(c, g, q):
                if q == 0:
                    pe.wait_ge(w_loaded, KT * LOAD)
                    pe.wait_ge(gated, c * DB + DB + 2)
                pe.wait_ge(o_read, c * KT + q + 1)
                for b in range(DB):
                    last = nc.tensor.matmul(o_ps[:, q % 2], wout[:, q, b], yg[:, g, b], start=(b == 0),
                                            stop=(b == DB - 1))
                last.then_inc(o_mm, 1)

            chunks(pe, prepare, project)

        @block.vector
        def _(dve):
            dve.sem_inc(gated, 2)
            dve.sem_inc(o_read, 2)
            dve.sem_inc(o_done, 2)
            u32 = mybir.dt.uint32

            def prepare(c, g, q):
                for s in range(2):
                    u = 2 * q + s
                    dve.wait_ge(yt_done, c * DB + u + 1)
                    dve.wait_ge(silu_done, c * DB + u + 1)
                    nc.vector.tensor_tensor(yg[:, g, u], yt_ps[:, s], sz[:, s], ALU.mult).then_inc(gated, 1)

            def project(c, g, q):
                s = q % 2

                def after(step):
                    hold(dve, o_step, c * (KT * STEPS) + (q * STEPS + step), passed)

                dve.wait_ge(const_ready, 3)
                dve.wait_ge(o_mm, c * KT + q + 1)
                dve.wait_ge(o_stored[s], c * (KT // 2 * LOAD) + (q // 2 + 1) * LOAD)
                nc.vector.tensor_copy(o[:, s], o_ps[:, s]).then_inc(o_read, 1)
                dve.wait_ge(o_read, c * KT + q + 3)
                nc.vector.tensor_tensor(test[:, s], o[:, s], o[:, s], ALU.not_equal).then_inc(o_step, 1)
                after(1)
                nc.vector.copy_predicated(o[:, s], test[:, s].bitcast(u32), zero[:]).then_inc(o_step, 1)
                for step, (op, bound, value) in ((2, (ALU.is_gt, FMAX, one)), (4, (ALU.is_lt, -FMAX, minus))):
                    dve.wait_ge(o_step, c * (KT * STEPS) + (q * STEPS + step))
                    nc.vector.tensor_scalar(test[:, s], o[:, s], bound, None, op).then_inc(o_step, 1)
                    after(step + 1)
                    nc.vector.copy_predicated(o[:, s], test[:, s].bitcast(u32), value[:]).then_inc(o_step, 1)
                dve.wait_ge(o_step, c * (KT * STEPS) + (q * STEPS + STEPS))
                dve.wait_ge(x_loaded[s], c * (KT // 2 * LOAD) + (q // 2 + 1) * LOAD)
                nc.vector.tensor_tensor(o[:, s], o[:, s], x1[:, s], ALU.add).then_inc(o_done, 1)

            chunks(dve, prepare, project)


def metaformer(nc, x, dt_w, dt_b, log_a, ln_w, ln_b, winx, winz, wout, wx, wdt, convp, par, skip, out):
    def scratch(name, shape):
        return nc.dram_tensor(name, shape, F32).ap()

    hnT, x1T = scratch("hnT", (C, HW)), scratch("x1T", (C, HW))
    x_pad, z = scratch("x_pad", (DI, HALO + HW + HALO)), scratch("z", (DI, HW))
    xc = scratch("xc", (NCH * DB, P, T))
    bc = scratch("bc", (NCH, 2 * NS, T))
    states = [scratch(f"state{d}", ((NCH + 1) * DB, P, NS)) for d in range(2)]
    yT = [scratch(f"yT{d}", (NCH * DB + 1, P, TB, P)) for d in range(2)]
    with Scope(nc, "all") as top:
        ident = top.sb("ident", [P, P])
        passed = top.sem("passed")
        with Scope(nc, "norm") as sc:
            xn = sc.sb("xn", [P, NT * C])
            mv = sc.sb("mv", [P, NT * 2])
            mean_w = sc.sb("mean_w", [P, P])
            rstd2 = sc.sb("rstd2", [P, C])
            with Scope(nc, "mean") as ms:
                mean_ps = ms.ps("mean_ps", [P, C])
                stage_channel_norm(nc, passed, xn, ident, mean_w, mean_ps, x)
                stage_pixel_variance(nc, xn, mean_w, mean_ps, rstd2)
            stage_channel_scan(nc, passed, xn, ident, rstd2, mv, x, ln_w, ln_b, dt_w, dt_b, log_a)
            stage_token_norm(nc, xn, ident, mv, hnT, x1T, x_pad, states)
        for rev in (True, False):
            d = int(rev)
            stage_scan(nc, rev, ident, hnT, winx if rev else winz, wx[d], wdt[d], convp[d], par[d], skip[d], x_pad, xc, z, bc,
                       states[d], yT[d])
        stage_out(nc, passed, ident, yT[0], yT[1], z, wout, x1T, out)


def kernel(**inputs):
    import numpy as np
    import concourse.bacc as bacc
    from concourse.bass_utils import run_bass_kernel_spmd

    g = {n: np.asarray(a) for n, a in inputs.items()}

    def tiles(a, n):
        return a.reshape(n, P, a.shape[1] // P, P).transpose(0, 3, 2, 1)

    def per_block(*cols):
        return np.concatenate([c.reshape(DB, P, -1) for c in cols], axis=2)

    win = g["L0_ffn_in_proj_w"]
    arrays = {
        "x": g["x"].reshape(C, HW),
        "dt_w": np.concatenate([g["L0_conv_dt_w"].reshape(ROW, 1)] * 2),
        "dt_b": np.broadcast_to(g["L0_conv_dt_b"].reshape(1, 1), (P, 1)),
        "log_a": np.repeat(g["L0_conv_log_A"].reshape(NT, 2).T, ROW, axis=0),
        "ln_w": g["L0_conv_ln_w"].reshape(NT, P).T,
        "ln_b": g["L0_conv_ln_b"].reshape(NT, P).T,
        "winx": tiles(win[:DI], DB),
        "winz": tiles(win[DI:], DB),
        "wout": tiles(g["L0_ffn_out_proj_w"], KT),
    }
    for d, b in enumerate(("", "b_")):
        arrays[f"wx{d}"] = g[f"L0_ffn_x_proj_{b}w"].T.reshape(DB, P, XO)
        arrays[f"wdt{d}"] = g[f"L0_ffn_dt_proj_{b}w"].reshape(DB, P, R).transpose(0, 2, 1)
        arrays[f"convp{d}"] = per_block(g[f"L0_ffn_conv1d_{b}w"], g[f"L0_ffn_conv1d_{b}bias"])
        arrays[f"par{d}"] = per_block(g[f"L0_ffn_dt_proj_{b}bias"], g["L0_ffn_A_b_log" if d else "L0_ffn_A_log"])
        arrays[f"skip{d}"] = per_block(g["L0_ffn_D_b" if d else "L0_ffn_D"])
    arrays = {n: np.ascontiguousarray(a) for n, a in arrays.items()}

    nc = bacc.Bacc("TRN2", target_bir_lowering=False, num_devices=1)
    ap = {n: nc.dram_tensor(n, a.shape, F32, kind="ExternalInput").ap() for n, a in arrays.items()}
    out = nc.dram_tensor("out", (C, HW), F32, kind="ExternalOutput").ap()
    both = {n: [ap[f"{n}0"], ap[f"{n}1"]] for n in ("wx", "wdt", "convp", "par", "skip")}
    metaformer(nc, ap["x"], ap["dt_w"], ap["dt_b"], ap["log_a"], ap["ln_w"], ap["ln_b"], ap["winx"], ap["winz"],
               ap["wout"], both["wx"], both["wdt"], both["convp"], both["par"], both["skip"], out)
    r = run_bass_kernel_spmd(nc, [arrays], core_ids=[0])
    return r.results[0]["out"].reshape(1, C, 64, 64)
```
